# Optimizing a Trainium2 kernel written in Bass

```python
import numpy as np
import jax
import jax.numpy as jnp

def _softmax(x, axis=-1):
    return jax.nn.softmax(x, axis=axis)

def _gelu(x):
    return jax.nn.gelu(x, approximate=True)

def _silu(x):
    return jax.nn.silu(x)

def _sigmoid(x):
    return jax.nn.sigmoid(x)

def _layernorm(x, axis=-1, eps=1e-05):
    m = jnp.mean(x, axis=axis, keepdims=True)
    v = jnp.var(x, axis=axis, keepdims=True)
    return (x - m) / jnp.sqrt(v + eps)

def _scatter_add(tgt, idx, src, axis=0):
    return tgt.at[idx].add(src)

def _segment_sum(src, seg, n):
    return jax.ops.segment_sum(src, seg, n)
kernel_name = 'mk_gnn_ffn_d1_gnn_r8_82fe00'

def setup_inputs(seed: int=0):
    np.random.seed(seed)
    _w = jnp.asarray

    def _rec_inputs():
        import jax
        import jax.numpy as jnp
        _gk = jax.random.key(seed)
        x = -0.0003713 + 1 * jax.random.normal(jax.random.fold_in(_gk, 1), (6250, 256), jnp.float32)
        src = jax.random.randint(jax.random.fold_in(_gk, 2), (100000,), 0, 6250, jnp.int32)
        dst = jax.random.randint(jax.random.fold_in(_gk, 3), (100000,), 0, 6250, jnp.int32)
        _o = jnp.argsort(dst, stable=True)
        src = src[_o]
        dst = dst[_o]
        return (x, src, dst)
    x, src, dst = _rec_inputs()

    def _L0_gnn_setup():
        import jax, jax.numpy as jnp
        import numpy as np
        N_NODES = 6250
        N_EDGES = 100000
        IN_FEAT = 256
        OUT_FEAT = 64
        NHEAD = 4
        ALPHA = 0.2
        key = jax.random.key(seed)
        k_x, k_e, k_w, k_al, k_ar = jax.random.split(key, 5)
        x = jax.random.normal(k_x, (N_NODES, IN_FEAT), dtype=jnp.float32)
        edge = jax.random.randint(k_e, (2, N_EDGES), 0, N_NODES, dtype=jnp.int64)
        stdv_w = np.sqrt(6.0 / (IN_FEAT + OUT_FEAT * NHEAD))
        W = jax.random.uniform(k_w, (IN_FEAT, OUT_FEAT * NHEAD), minval=-stdv_w, maxval=stdv_w, dtype=jnp.float32)
        stdv_a = np.sqrt(6.0 / (NHEAD + OUT_FEAT))
        a_l = jax.random.uniform(k_al, (1, NHEAD, OUT_FEAT), minval=-stdv_a, maxval=stdv_a, dtype=jnp.float32)
        a_r = jax.random.uniform(k_ar, (1, NHEAD, OUT_FEAT), minval=-stdv_a, maxval=stdv_a, dtype=jnp.float32)
        return {'x': x, 'edge': edge, 'W': W, 'a_l': a_l, 'a_r': a_r}
    _L0_gnn_all = _L0_gnn_setup()
    _L0_gnn_in = {k: v for k, v in _L0_gnn_all.items() if k in ('W', 'a_l', 'a_r')}
    del _L0_gnn_all

    def _L0_ffn_setup():
        import math
        import jax, jax.numpy as jnp
        import numpy as np
        CAPACITY_FACTOR = 1.25
        TOP_K = 2
        LN_EPS = 1e-05

        def _layer_norm(x, gamma, beta):
            mu = jnp.mean(x, axis=-1, keepdims=True)
            var = jnp.var(x, axis=-1, keepdims=True)
            return (x - mu) * jax.lax.rsqrt(var + LN_EPS) * gamma + beta
        key = jax.random.key(seed)
        ks = jax.random.split(key, 4)
        B, S, D, F, E = (8, 512, 256, 512, 8)
        x = jax.random.normal(ks[0], (B, S, D), dtype=jnp.float32)
        Wr = jax.random.normal(ks[1], (D, E), dtype=jnp.float32) / np.sqrt(D)
        br = jnp.zeros((E,), jnp.float32)
        W1 = jax.random.normal(ks[2], (E, D, F), dtype=jnp.float32) / np.sqrt(D)
        b1 = jnp.zeros((E, F), jnp.float32)
        W2 = jax.random.normal(ks[3], (E, F, D), dtype=jnp.float32) / np.sqrt(F)
        b2 = jnp.zeros((E, D), jnp.float32)
        gamma = jnp.ones((D,), jnp.float32)
        beta = jnp.zeros((D,), jnp.float32)
        return {'x': x, 'Wr': Wr, 'br': br, 'W1': W1, 'b1': b1, 'W2': W2, 'b2': b2, 'gamma': gamma, 'beta': beta}
    _L0_ffn_all = _L0_ffn_setup()
    _L0_ffn_in = {k: v for k, v in _L0_ffn_all.items() if k in ('Wr', 'br', 'W1', 'b1', 'W2', 'b2', 'gamma', 'beta')}
    del _L0_ffn_all
    return {'x': x, 'src': src, 'dst': dst, 'L0_gnn_W': _L0_gnn_in['W'], 'L0_gnn_a_l': _L0_gnn_in['a_l'], 'L0_gnn_a_r': _L0_gnn_in['a_r'], 'L0_ffn_Wr': _L0_ffn_in['Wr'], 'L0_ffn_br': _L0_ffn_in['br'], 'L0_ffn_W1': _L0_ffn_in['W1'], 'L0_ffn_b1': _L0_ffn_in['b1'], 'L0_ffn_W2': _L0_ffn_in['W2'], 'L0_ffn_b2': _L0_ffn_in['b2'], 'L0_ffn_gamma': _L0_ffn_in['gamma'], 'L0_ffn_beta': _L0_ffn_in['beta']}

def reference(x, src, dst, L0_gnn_W, L0_gnn_a_l, L0_gnn_a_r, L0_ffn_Wr, L0_ffn_br, L0_ffn_W1, L0_ffn_b1, L0_ffn_W2, L0_ffn_b2, L0_ffn_gamma, L0_ffn_beta):
    import jax
    import jax.numpy as jnp

    def _L0_gnn_ref(x, edge, W, a_l, a_r):
        import jax, jax.numpy as jnp
        import numpy as np
        N_NODES = 6250
        N_EDGES = 100000
        IN_FEAT = 256
        OUT_FEAT = 64
        NHEAD = 4
        ALPHA = 0.2
        N = x.shape[0]
        H, F = (a_l.shape[1], a_l.shape[2])
        h = (x @ W).reshape(N, H, F)
        h_l = (a_l * h).sum(-1)
        h_r = (a_r * h).sum(-1)
        row, col = (edge[0], edge[1])
        e = jax.nn.leaky_relu(h_l[row] + h_r[col], ALPHA)
        m = jax.lax.stop_gradient(jax.ops.segment_max(e, row, num_segments=N))
        ex = jnp.exp(e - m[row])
        denom = jax.ops.segment_sum(ex, row, num_segments=N)[row]
        att = ex / jnp.maximum(denom, jnp.asarray(1e-16, ex.dtype))
        msg = att[:, :, None] * h[col]
        out = jax.ops.segment_sum(msg, row, num_segments=N)
        return out.reshape(N, H * F)

    def _L0_ffn_ref(x, Wr, br, W1, b1, W2, b2, gamma, beta):
        import math
        import jax, jax.numpy as jnp
        import numpy as np
        CAPACITY_FACTOR = 1.25
        TOP_K = 2
        LN_EPS = 1e-05

        def _layer_norm(x, gamma, beta):
            mu = jnp.mean(x, axis=-1, keepdims=True)
            var = jnp.var(x, axis=-1, keepdims=True)
            return (x - mu) * jax.lax.rsqrt(var + LN_EPS) * gamma + beta
        B, S, D = x.shape
        E = Wr.shape[1]
        N = B * S
        K = TOP_K
        logits = jnp.mean(x, axis=1) @ Wr + br
        routing_weights = jax.nn.softmax(logits, axis=-1)
        capacity = float(math.ceil(N * CAPACITY_FACTOR / E))
        expected_loads = routing_weights.sum(axis=0) * (N / B)
        scale = jnp.where(expected_loads > capacity, capacity / expected_loads, 1.0)
        routing_weights = jax.nn.softmax(routing_weights * scale, axis=-1)
        rw_tok = jnp.broadcast_to(routing_weights[:, None, :], (B, S, E)).reshape(N, E)
        top_w, top_i = jax.lax.top_k(rw_tok, K)
        top_w = jax.nn.softmax(top_w, axis=-1)
        xf = x.reshape(N, D)
        h = jax.nn.gelu(jnp.einsum('nd,edf->enf', xf, W1) + b1[:, None, :], approximate=False)
        y = jnp.einsum('enf,efd->end', h, W2) + b2[:, None, :]
        w_dense = jnp.zeros((N, E), x.dtype).at[jnp.arange(N)[:, None], top_i].add(top_w)
        out = jnp.einsum('ne,end->nd', w_dense, y).reshape(B, S, D)
        out = _layer_norm(out + x, gamma, beta)
        return out
    edge_index = jnp.stack([src, dst])
    x = x + _L0_gnn_ref(_layernorm(x, axis=-1), edge_index, L0_gnn_W, L0_gnn_a_l, L0_gnn_a_r)
    x = x + _L0_ffn_ref(_layernorm(x, axis=-1)[None], L0_ffn_Wr, L0_ffn_br, L0_ffn_W1, L0_ffn_b1, L0_ffn_W2, L0_ffn_b2, L0_ffn_gamma, L0_ffn_beta)[0]
    return x

_drawn_inputs = setup_inputs


def setup_inputs(seed=0):
    import zlib

    import numpy as np

    out = dict(_drawn_inputs(seed))
    spreads = {'L0_ffn_br': (0.0, 2.0),
     'L0_ffn_b1': (0.0, 0.384),
     'L0_ffn_b2': (0.0, 0.1),
     'L0_ffn_gamma': (1.0, 0.2),
     'L0_ffn_beta': (0.0, 0.1)}
    factors = {'L0_ffn_Wr': 64.0}
    for name, (base, spread) in spreads.items():
        noise = np.random.default_rng([zlib.crc32(name.encode()), seed]).standard_normal(out[name].shape)
        drawn = base * np.exp(spread * noise) if base else spread * noise
        out[name] = jnp.asarray(drawn.astype(out[name].dtype))
    for name, factor in factors.items():
        out[name] = (out[name] * factor).astype(out[name].dtype)
    return out
```

```python
from contextlib import ExitStack

import concourse.bass as bass
from concourse import mybir

P = 128
F32 = mybir.dt.float32
F16 = mybir.dt.float16
BF16 = mybir.dt.bfloat16
I32 = mybir.dt.int32
U32 = mybir.dt.uint32
U16 = mybir.dt.uint16
ALU = mybir.AluOpType
ACT = mybir.ActivationFunctionType
X = mybir.AxisListType.X
XY = mybir.AxisListType.XY
ds = bass.ds


class Count:

    def __init__(self, sem):
        self.sem, self.value = sem, 0

    def add(self, instruction):
        instruction.then_inc(self.sem, 1)
        self.value = self.value + 1


def gat_moe_block(nc, x, src, dst, gat_w, a_l, a_r, w_r, b_r, w_1, b_1, w_2, b_2, gamma, beta, out):
    N, D = x.shape
    E = src.shape[0]
    H, FH = a_l.shape[1], a_l.shape[2]
    NX, FF = w_1.shape[0], w_1.shape[2]
    HD = H * FH
    HW = HD + H
    KD = D // P
    NB = -(-N // P)
    TRASH = NB
    BINS = NB + 1 + (NB + 1) % 2
    LAST = N - (NB - 1) * P
    EC = -(-E // P)
    UT = 8
    ECP = -(-EC // UT) * UT
    E_LAST = E - (P - 1) * EC
    PAIRS = (E + NB * (2 * P - 1)) // (2 * P)
    G = 8
    R = 3
    GROUPS = -(-(-(-2 * PAIRS // G)) // R) * R
    TILES = GROUPS * G
    TPAD = TILES + 2 * G
    HALF = TILES // 2
    SHIFT = 11
    LOW = (1 << SHIFT) - 1
    NEG = float(2 ** 80)
    SLOPE = 0.2
    EPS = 1e-5
    TOKENS = N
    CAPACITY = float(-(-TOKENS * 5 // (4 * NX)))
    ROWS = BINS * P
    CB = 4
    CN = CB * P
    FULL = (NB - 1) // CB
    XB = (FULL + 1) * CB
    assert HD == D == 2 * P and FF == 4 * P and TILES <= 2 * 512 and N < 4 << SHIFT and GROUPS < P

    h_table = nc.dram_tensor("h_table", (ROWS, HW), F32, kind="Internal").ap()
    hr_table = nc.dram_tensor("hr_table", (ROWS, H), F32, kind="Internal").ap()
    bin_table = nc.dram_tensor("bin_table", (P, G // 2), I32, kind="Internal").ap()

    with ExitStack() as ctx:
        def sb(name, shape, dt=F32):
            return ctx.enter_context(nc.sbuf_tensor(name, shape, dt))

        def sem(name):
            return ctx.enter_context(nc.semaphore(name))

        def sems(name, n):
            return [sem(f"{name}{k}") for k in range(n)]

        def carve(arena, sizes):
            at, views = 0, []
            for dt, shape in sizes:
                n = 1
                for k in shape:
                    n *= k
                words = n * mybir.dt.size(dt) // 4
                v = arena[:, at:at + words]
                if dt != F32:
                    v = v.bitcast(dt)
                if len(shape) == 2:
                    v = v.rearrange("p (a b) -> p a b", b=shape[1])
                elif len(shape) == 3:
                    v = v.rearrange("p (a b c) -> p a b c", b=shape[1], c=shape[2])
                elif len(shape) == 4:
                    v = v.rearrange("p (a b c d) -> p a b c d", b=shape[1], c=shape[2], d=shape[3])
                views.append(v)
                at += words
            return views

        x_sb = sb("x_sb", [P, XB, D])
        wx = sb("wx", [P, KD, HD + 2 * H])
        al_bc = sb("al_bc", [P, HD])
        ar_bc = sb("ar_bc", [P, HD])
        hl = sb("hl", [P, BINS, H])
        hr = sb("hr", [P, BINS, H])
        top = sb("top", [P, BINS, H])
        table = sb("table", [P, BINS, 2 * H, 3], BF16)
        mv = sb("mv", [P, XB, 2])
        rstd = sb("rstd", [P, XB])
        nmr = sb("nmr", [P, XB])
        stats = sb("stats", [P, 2, 6])
        mv_one = sb("mv_one", [P, 2, 2])
        tmp_a = sb("tmp_a", [P, XB, 2 * H])
        tmp_b = sb("tmp_b", [P, XB, 2 * H])
        iota_1 = sb("iota_1", [P, P])
        iota_p16 = sb("iota_p16", [P, P], F16)
        iota_t16 = sb("iota_t16", [P, TILES], F16)
        iota_b = sb("iota_b", [P, BINS + 1])
        iota_pair = sb("iota_pair", [P, G // 2])
        part_i = sb("part_i", [P, 1], I32)
        part_k = sb("part_k", [P, 1])
        ident = sb("ident", [P, P])
        ident_b = sb("ident_b", [P, P], BF16)
        before = sb("before", [P, P])
        ones = sb("ones", [P, P])
        zeros16 = sb("zeros16", [P, HALF], F16)
        l_mask = sb("l_mask", [P, P], BF16)
        l_hr = sb("l_hr", [P, H, P], BF16)
        coef = sb("coef", [P, 12])
        slot_s = sb("slot_s", [P, TPAD])
        slot_d = sb("slot_d", [P, TPAD], I32)
        slot_r = sb("slot_r", [P, TPAD, 5], BF16)
        bins_row = sb("bins_row", [1, P * G // 2], I32)
        small = sb("small", [1, 64])
        logit = sb("logit", [1, 16 * NX])
        chosen = sb("chosen", [1, 2], I32)
        mean_row = sb("mean_row", [1, D])
        mean_col = sb("mean_col", [P, KD])
        wr_sb = sb("wr_sb", [P, KD, NX])
        br_row = sb("br_row", [1, NX])
        top_w = sb("top_w", [P, 2])

        arena_a = sb("arena_a", [P, BINS * HW])
        (src_i, dst_i, work_i, code_a, code_b, pos, tile_of, place_of, bin_16, mask, rank) = carve(arena_a, [
            (I32, [ECP]), (I32, [ECP]), (I32, [ECP]), (F32, [ECP]), (F32, [ECP]), (F32, [ECP]), (F32, [ECP]),
            (F32, [ECP]), (F16, [ECP]), (U16, [2, ECP]), (F32, [2, ECP])])
        (acc,) = carve(arena_a, [(F32, [BINS, HW])])
        (act_t, u_t, u_rows) = carve(arena_a, [(F32, [2, 8, CN]), (F32, [KD, CN]), (F32, [2, CB, D])])
        arena_b = sb("arena_b", [P, 11100])
        ONEHOTS = 4
        (oh_tile, oh_a, oh_b) = carve(arena_b, [(F16, [ONEHOTS, TILES]), (F16, [ONEHOTS, P]), (F16, [ONEHOTS, P])])
        n0 = ONEHOTS * (TILES + 2 * P) // 2
        (xh, xh_t, h_out) = carve(arena_b[:, n0:], [(F32, [2, D]), (F32, [2, KD, P]), (F32, [2, HW])])
        n0 += 4 * D + 2 * HW
        (count, base, total, ends, bin_i) = carve(arena_b[:, n0:], [
            (F32, [BINS]), (F32, [BINS]), (F32, [BINS]), (F32, [BINS]), (I32, [BINS])])
        n0 += 5 * BINS
        (bin_cmp, bin_of, bin_of_i) = carve(arena_b[:, n0:], [(F32, [G // 2, NB]), (F32, [G // 2]), (I32, [G // 2])])
        n0 += G // 2 * NB + G
        (slot_a, slot_b, slot_t) = carve(arena_b[:, n0:], [(I32, [TILES]), (I32, [TILES]), (F32, [TILES])])
        (rows, onehot, onehot_t) = carve(arena_b, [(F32, [R, G, HW]), (F32, [R, G, P]), (BF16, [R, G, P])])
        n1 = R * G * (HW + P + P // 2)
        (idx, terms) = carve(arena_b[:, n1:], [(U32, [R, G]), (F32, [R, G, 2 * H])])
        (hr_rows, pack, pack_t, res_a, res_b) = carve(arena_b, [
            (F32, [R, G, H]), (BF16, [R, G, 32]), (BF16, [R, 2, P]), (F32, [G, H]), (F32, [G, H])])
        part_top = sb("part_top", [P, 2, H])
        (w1_sb, w2_sb, y) = carve(arena_b, [(F32, [2, KD, FF]), (F32, [2, 4, D]), (F32, [2, CB, D])])
        b1_sb = sb("b1_sb", [P, 2, FF // P])
        b2_bc = sb("b2_bc", [P, 2, D])
        gamma_bc = sb("gamma_bc", [P, D])
        beta_bc = sb("beta_bc", [P, D])
        mv2 = sb("mv2", [P, 2, CB, 2])
        ve2 = sb("ve2", [P, 2, CB])
        r2 = sb("r2", [P, 2, CB])
        t2 = sb("t2", [P, 2, CB])
        half_col = sb("half_col", [P, CB])
        stats2 = sb("stats2", [P, CB, 6])

        ps = ctx.enter_context(nc.psum_tensor("ps", [P, 8, 512], F32))

        s_const = sem("s_const")
        s_fill = sem("s_fill")
        s_edges = sem("s_edges")
        s_w = sem("s_w")
        s_x = sem("s_x")
        s_small = sem("s_small")
        s_dve = sem("s_dve")
        s_go = sem("s_go")
        s_std = sem("s_std")
        s_var = sem("s_var")
        s_norm = sem("s_norm")
        s_xh = sem("s_xh")
        s_xhp = sem("s_xhp")
        s_xht = sem("s_xht")
        s_h = sem("s_h")
        s_hcopy = sem("s_hcopy")
        s_hst = sems("s_hst", 2)
        s_hrst = sem("s_hrst")
        s_cnt = sem("s_cnt")
        s_base = sem("s_base")
        s_bins = sem("s_bins")
        s_binst = sem("s_binst")
        s_binld = sem("s_binld")
        s_oh = sem("s_oh")
        s_mm = sems("s_mm", ONEHOTS)
        s_slots = sem("s_slots")
        s_table = sem("s_table")
        s_idx = sems("s_idx", R)
        s_turn = sem("s_turn")
        s_gat = sems("s_gat", R)
        s_pack = sems("s_pack", R)
        s_packp = sems("s_packp", R)
        s_packt = sems("s_packt", R)
        s_plane = sems("s_plane", 2)
        s_plfree = sems("s_plfree", 2)
        s_max = sems("s_max", R)
        s_tab = sem("s_tab")
        s_idxb = sems("s_idxb", R)
        s_gatb = sems("s_gatb", R)
        s_onehot = sems("s_onehot", R)
        s_ohp = sem("s_ohp")
        s_oht = sem("s_oht")
        s_look = sems("s_look", R)
        s_terms = sems("s_terms", R)
        s_arg = sems("s_arg", R)
        s_wgt = sems("s_wgt", R)
        s_msg = sems("s_msg", R)
        s_sum = sems("s_sum", 4)
        s_acc = sems("s_acc", 3)
        s_done = sems("s_done", R)
        s_x1 = sem("s_x1")
        s_u = sem("s_u")
        s_umm = sem("s_umm")
        s_mean = sem("s_mean")
        s_meanp = sem("s_meanp")
        s_meanc = sem("s_meanc")
        s_logit = sem("s_logit")
        s_rt = sem("s_rt")
        s_rte = sem("s_rte")
        s_choice = sem("s_choice")
        s_wb = sem("s_wb")
        s_exp = sem("s_exp")
        s_expw = sem("s_expw")
        s_ub = sem("s_ub")
        s_utp = sem("s_utp")
        s_ut = sem("s_ut")
        s_m1 = sem("s_m1")
        s_act = sem("s_act")
        s_m2 = sem("s_m2")
        s_y = sem("s_y")
        s_pow = sem("s_pow")
        s_out = sem("s_out")
        s_st = sems("s_st", 2)

        LD_EDGES, LD_W, LD_X, LD_SMALL = 4, 3, 2, 4
        N_CONST = 10
        block = ctx.enter_context(nc.Block())

        @block.sync
        def _(sp):
            sp.wait_ge(s_fill, 2)
            for a, v in ((src, src_i), (dst, dst_i)):
                body = a[0:(P - 1) * EC].rearrange("(p c) -> p c", c=EC)
                sp.dma_start(v[0:P - 1, 0:EC], body).then_inc(s_edges, 16)
                tail = a[(P - 1) * EC:E].rearrange("(p c) -> p c", p=1)
                sp.dma_start(v[P - 1:P, 0:E_LAST], tail).then_inc(s_edges, 16)
            sp.wait_ge(s_fill, 3)
            sp.dma_start(x_sb[:, 0:NB - 1, :], x[0:(NB - 1) * P, :].rearrange("(b p) d -> p b d", p=P)).then_inc(s_x, 16)
            sp.dma_start(x_sb[0:LAST, NB - 1, :], x[(NB - 1) * P:N, :]).then_inc(s_x, 16)
            sp.dma_start(wx[:, :, 0:HD], gat_w.rearrange("(k p) n -> p k n", p=P)).then_inc(s_w, 16)
            for a, v in ((a_l, al_bc), (a_r, ar_bc)):
                sp.dma_start(v[:, :], a.rearrange("o h f -> o (h f)").to_broadcast([P, HD])).then_inc(s_w, 16)
            sp.dma_start(wr_sb[:, :, :], w_r.rearrange("(k p) n -> p k n", p=P)).then_inc(s_small, 16)
            sp.dma_start(br_row[:, :], b_r.rearrange("(o n) -> o n", o=1)).then_inc(s_small, 16)
            for a, v in ((gamma, gamma_bc), (beta, beta_bc)):
                sp.dma_start(v[:, :], a.rearrange("(o n) -> o n", o=1).to_broadcast([P, D])).then_inc(s_small, 16)
            with sp.Fori(0, BINS // 2) as i:
                for u in range(2):
                    sp.wait_ge(s_hcopy, (i * 2 + u) * 3 + 3)
                    sp.dma_start(h_table[ds((i * 2 + u) * P, P), :], h_out[:, u, :]).then_inc(s_hst[u], 16)
            sp.dma_start(hr_table.rearrange("(b p) h -> p b h", p=P), hr[:, :, :]).then_inc(s_hrst, 16)
            sp.wait_ge(s_bins, 1)
            sp.dma_start(bin_table, bin_of_i).then_inc(s_binst, 16)
            sp.wait_ge(s_binst, 16)
            sp.dma_start(bins_row[:, :], bin_table.rearrange("(o g) q -> o (g q)", o=1)).then_inc(s_binld, 16)
            sp.wait_ge(s_choice, 1)
            for k in range(2):
                e = sp.value_load(chosen[0:1, k:k + 1], min_val=0, max_val=NX - 1)
                sp.dma_start(w1_sb[:, k, :, :], w_1[ds(e, 1), :, :].rearrange("e (k p) f -> p (e k) f", p=P)).then_inc(s_exp, 16)
                sp.dma_start(w2_sb[:, k, :, :], w_2[ds(e, 1), :, :].rearrange("e (k p) f -> p (e k) f", p=P)).then_inc(s_exp, 16)
                with nc.allow_non_contiguous_dma(reason="512 biases, one a partition"):
                    sp.dma_start(b1_sb[:, k, :], b_1[ds(e, 1), :].rearrange("e (k p) -> p (e k)", p=P)).then_inc(s_exp, 16)
                sp.dma_start(b2_bc[:, k, :], b_2[ds(e, 1), :].to_broadcast([P, D])).then_inc(s_exp, 16)
            with sp.Fori(0, FULL // 2) as i:
                for u in range(2):
                    c = i * 2 + u
                    sp.wait_ge(s_out, (c + 1) * CB)
                    sp.dma_start(out[ds(c * CN, CN), :].rearrange("(b p) d -> p b d", p=P), y[:, u, :, :]).then_inc(s_st[u], 16)
            sp.wait_ge(s_out, FULL * CB + 1)
            sp.dma_start(out[(NB - 1) * P:N, :], y[0:LAST, 0, 0, :]).then_inc(s_st[0], 16)
            sp.wait_ge(s_st[0], 16 * (FULL // 2 + 1))
            sp.wait_ge(s_st[1], 16 * (FULL // 2))

        @block.gpsimd
        def _(pool):
            iota = dict(allow_small_or_imprecise_dtypes=True)
            pool.iota(iota_1[:, :], pattern=[[1, P]], base=1, channel_multiplier=0, **iota).then_inc(s_const, 1)
            pool.iota(iota_p16[:, :], pattern=[[1, P]], base=0, channel_multiplier=0, **iota).then_inc(s_const, 1)
            pool.iota(iota_t16[:, :], pattern=[[1, TILES]], base=1, channel_multiplier=0, **iota).then_inc(s_const, 1)
            pool.iota(iota_b[:, :], pattern=[[1, BINS + 1]], base=0, channel_multiplier=0, **iota).then_inc(s_const, 1)
            pool.iota(iota_pair[:, :], pattern=[[1, G // 2]], base=0, channel_multiplier=G // 2, **iota).then_inc(s_const, 1)
            pool.iota(part_i[:, :], pattern=[[1, 1]], base=0, channel_multiplier=1).then_inc(s_const, 1)
            pool.memset(ones[:, :], 1.0).then_inc(s_const, 1)
            pool.memset(ident[:, :], 0.0).then_inc(s_const, 1)
            pool.wait_ge(s_const, 8)
            pool.affine_select(out=ident[:, :], in_=ident[:, :], compare_op=ALU.not_equal, fill=1.0, base=0,
                               pattern=[[-1, P]], channel_multiplier=1).then_inc(s_const, 1)
            pool.affine_select(out=before[:, :], in_=ones[:, :], compare_op=ALU.is_gt, fill=0.0, base=0,
                               pattern=[[1, P]], channel_multiplier=-1).then_inc(s_const, 1)
            pool.wait_ge(s_hrst, 16)
            with pool.Fori(0, GROUPS // R) as i:
                for r in range(R):
                    pool.wait_ge(s_idx[r], i + 1)
                    pool.wait_ge(s_pack[r], i)
                    pool.sem_inc(s_turn, 1)
                    for t in range(G):
                        pool.indirect_dma_start(out=hr_rows[:, r, t, :], out_offset=None, in_=hr_table,
                                                in_offset=bass.IndirectOffsetOnAxis(ap=idx[:, r, t:t + 1], axis=0)
                                                ).then_inc(s_gat[r], 16)
            for u in range(2):
                pool.wait_ge(s_hst[u], 16 * (BINS // 2))
            pool.wait_ge(s_tab, 1)
            with pool.Fori(0, GROUPS // R) as i:
                for r in range(R):
                    pool.wait_ge(s_idxb[r], i + 1)
                    pool.wait_ge(s_done[r], i)
                    pool.sem_inc(s_turn, 1)
                    for t in range(G):
                        pool.indirect_dma_start(out=rows[:, r, t, :], out_offset=None, in_=h_table,
                                                in_offset=bass.IndirectOffsetOnAxis(ap=idx[:, r, t:t + 1], axis=0)
                                                ).then_inc(s_gatb[r], 16)
            def power(c, u, n):
                pool.wait_ge(s_y, c + 1)
                pool.tensor_tensor(r2[:, u, 0:n], ve2[:, u, 0:n], half_col[:, 0:n], ALU.pow).then_inc(s_pow, 1)
            with pool.Fori(0, FULL // 2) as i:
                for u in range(2):
                    power(i * 2 + u, u, CB)
            power(FULL, 0, 1)

        @block.scalar
        def _(act):
            act.wait_ge(s_var, 1)
            act.activation(rstd[:, :], rstd[:, :], ACT.Sqrt).then_inc(s_std, 1)
            act.wait_ge(s_norm, 1)

            def normalise(b, u):
                act.activation(xh[:, u, :], x_sb[:, ds(b, 1), :].rearrange("p o d -> p (o d)"), ACT.Identity,
                               scale=rstd[:, ds(b, 1)], bias=nmr[:, ds(b, 1)]).then_inc(s_xh, 1)

            normalise(0, 0)
            with act.Fori(0, BINS // 2) as i:
                for u in range(2):
                    b = i * 2 + u
                    act.wait_ge(s_xhp, b + 1)
                    act.activation(xh_t[:, u, :, :].rearrange("p k n -> p (k n)"), ps[:, 4 + u, 0:D], ACT.Copy).then_inc(s_xht, 1)
                    normalise(b + 1, 1 - u)
                    act.wait_ge(s_h, b + 1)
                    act.wait_ge(s_hst[u], i * 16)
                    act.activation(h_out[:, u, :], ps[:, 6 + u, 0:HW], ACT.Copy).then_inc(s_hcopy, 1)
                    act.activation(hr[:, ds(b, 1), :].rearrange("p o h -> p (o h)"), ps[:, 6 + u, HD:HW], ACT.Copy).then_inc(s_hcopy, 1)
                    act.activation(hl[:, ds(b, 1), :].rearrange("p o h -> p (o h)"), ps[:, 6 + u, HW:HW + H], ACT.Copy).then_inc(s_hcopy, 1)
            act.wait_ge(s_table, 1)

            def place_targets(g, r, sem_out):
                act.activation(idx[:, r, :], slot_d[:, ds(g * G, G)], ACT.Copy).then_inc(sem_out[r], 1)

            with act.Fori(0, GROUPS // R) as i:
                for r in range(R):
                    g = i * R + r
                    act.wait_ge(s_gat[r], i * 16 * G)
                    place_targets(g, r, s_idx)
                    act.wait_ge(s_packp[r], i + 1)
                    act.wait_ge(s_max[r], i)
                    act.activation(pack_t[:, r, :, :].rearrange("p k n -> p (k n)"),
                                   ps[:, 4 + r, 0:P].bitcast(BF16), ACT.Copy).then_inc(s_packt[r], 1)
            act.wait_ge(s_tab, 1)

            def copy_onehots(g, i, r, k):
                act.wait_ge(s_ohp, g * 2 + k + 1)
                act.wait_ge(s_look[r], i)
                act.activation(onehot_t[:, r, 4 * k:4 * k + 4, :].rearrange("p k n -> p (k n)"), ps[:, k, :], ACT.Copy).then_inc(s_oht, 1)

            for r in range(2):
                place_targets(r, r, s_idxb)
            for k in range(2):
                copy_onehots(0, 0, 0, k)
            with act.Fori(0, GROUPS // R) as i:
                for r in range(R):
                    g = i * R + r
                    far, fi = (r + 2) % R, i + (r + 2) // R
                    near, ni = (r + 1) % R, i + (r + 1) // R
                    act.wait_ge(s_gatb[far], fi * 16 * G)
                    place_targets(g + 2, far, s_idxb)
                    for k in range(2):
                        copy_onehots(g + 1, ni, near, k)
                    act.wait_ge(s_arg[r], i + 1)
                    act.activation(rows[:, r, :, HD:HW], terms[:, r, :, 0:H], ACT.Exp).then_inc(s_wgt[r], 1)
            act.wait_ge(s_x1, 1)
            act.activation(rstd[:, :], rstd[:, :], ACT.Sqrt).then_inc(s_std, 1)
            act.wait_ge(s_rt, 1)
            act.activation(logit[0:1, NX:2 * NX], logit[0:1, NX:2 * NX], ACT.Exp).then_inc(s_rte, 1)
            act.wait_ge(s_rt, 2)
            act.activation(logit[0:1, 3 * NX:4 * NX], logit[0:1, 3 * NX:4 * NX], ACT.Exp).then_inc(s_rte, 1)
            act.wait_ge(s_rt, 3)
            act.activation(small[0:1, 10:11], small[0:1, 10:11], ACT.Exp).then_inc(s_rte, 1)
            act.wait_ge(s_exp, 8 * 16)

            def transposes_out(c, n):
                act.wait_ge(s_utp, c + 1)
                act.wait_ge(s_m1, c * 8)
                for k in range(KD):
                    act.activation(u_t[:, k, 0:n * P], ps[:, k, 0:n * P], ACT.Copy).then_inc(s_ut, 1)

            def gelus(c, u, n):
                for f in range(8):
                    act.wait_ge(s_m1, c * 8 + f + 1)
                    act.activation(act_t[:, u, f, 0:n * P], ps[:, 2 + f % 2, 0:n * P], ACT.Gelu,
                                   bias=b1_sb[:, f // 4, f % 4:f % 4 + 1]).then_inc(s_act, 1)

            with act.Fori(0, FULL // 2) as i:
                for u in range(2):
                    c = i * 2 + u
                    transposes_out(c, CB)
                    act.wait_ge(s_y, i * 2)
                    gelus(c, u, CB)
            transposes_out(FULL, 1)
            act.wait_ge(s_y, FULL)
            gelus(FULL, 0, 1)

        @block.tensor
        def _(pe):
            pe.wait_ge(s_const, N_CONST)
            pe.wait_ge(s_norm, 2)
            with pe.Fori(0, BINS // 2) as i:
                for u in range(2):
                    b = i * 2 + u
                    pe.wait_ge(s_xh, b + 1)
                    for k in range(KD):
                        last = pe.transpose(ps[:, 4 + u, k * P:(k + 1) * P], xh[:, u, k * P:(k + 1) * P], ident[:, :])
                    last.then_inc(s_xhp, 1)
                    pe.wait_ge(s_xht, b + 1)
                    pe.wait_ge(s_hcopy, i * 6)
                    for k in range(KD):
                        last = pe.matmul(ps[:, 6 + u, 0:HW + H], xh_t[:, u, k, :], wx[:, k, :], start=(k == 0), stop=(k == KD - 1))
                    last.then_inc(s_h, 1)
            pe.wait_ge(s_cnt, BINS)
            pe.wait_ge(s_hcopy, 3 * BINS)
            pe.matmul(ps[:, 4, 0:BINS], before[:, :], count, start=True, stop=True)
            pe.matmul(ps[:, 5, 0:BINS], ones[:, :], count, start=True, stop=True).then_inc(s_base, 1)
            def onto(k, lhs, rhs, **flags):
                return pe.matmul(ps[:, k, 0:HALF], lhs, rhs, skip_group_check=True, **flags)

            pe.wait_ge(s_fill, 5)
            for k in range(4):
                onto(k, zeros16[:, 0:P], zeros16[:, :], start=True, stop=False)
            with pe.Fori(0, ECP // UT) as i:
                for t in range(UT):
                    q = t % ONEHOTS
                    pe.wait_ge(s_oh, (i * UT + t) * 3 + 3)
                    for k in range(4):
                        last = onto(k, (oh_a if k < 2 else oh_b)[:, q, :], oh_tile[:, q, k % 2 * HALF:(k % 2 + 1) * HALF],
                                    start=False, stop=False)
                    last.then_inc(s_mm[q], 1)
            for k in range(4):
                last = onto(k, zeros16[:, 0:P], zeros16[:, :], start=False, stop=True)
            last.then_inc(s_slots, 1)
            pe.wait_ge(s_table, 1)
            with pe.Fori(0, GROUPS // R) as i:
                for r in range(R):
                    pe.wait_ge(s_pack[r], i + 1)
                    pe.wait_ge(s_packt[r], i)
                    for k in range(2):
                        last = pe.transpose(ps[:, 4 + r, k * P // 2:(k + 1) * P // 2].bitcast(BF16),
                                            pack[:, r, 4 * k:4 * k + 4, :].rearrange("p t n -> p (t n)"), ident_b[:, :])
                    last.then_inc(s_packp[r], 1)
                    pe.wait_ge(s_packt[r], i + 1)
                    for q in range(G // 2):
                        w = q % 2
                        pe.wait_ge(s_plfree[w], (i * R + r) * 2 + q // 2)
                        for t in (2 * q, 2 * q + 1):
                            lo = 32 * (t % 4)
                            moving = pack_t[lo:lo + 32, r, t // 4, :]
                            plane = ps[:, 2 * w + t % 2, :].rearrange("p (h n) -> p h n", h=H)
                            pe.matmul(plane, l_mask[lo:lo + 32, :], moving.rearrange("p (o n) -> p o n", o=1).to_broadcast([32, H, P]),
                                      start=True, stop=False, skip_group_check=True)
                            for h in range(H):
                                last = pe.matmul(plane[:, h, :], l_hr[lo:lo + 32, h, :], moving, start=False, stop=(h == H - 1),
                                                 skip_group_check=True)
                        last.then_inc(s_plane[w], 1)
            pe.wait_ge(s_tab, 1)
            pe.wait_ge(s_binld, 16)

            def turn_onehots(g, i, r):
                pe.wait_ge(s_onehot[r], i * G + G)
                for k in range(2):
                    pe.wait_ge(s_oht, g * 2)
                    for t in range(4):
                        last = pe.transpose(ps[:, k, t * P:(t + 1) * P], onehot[:, r, 4 * k + t, :], ident[:, :])
                    last.then_inc(s_ohp, 1)

            def look_up(g, i, r):
                pe.wait_ge(s_oht, g * 2 + 2)
                pe.wait_ge(s_terms[r], i)
                for q in range(G // 2):
                    b = pe.value_load(bins_row[0:1, ds(g * (G // 2) + q, 1)], min_val=0, max_val=TRASH)
                    for t in (2 * q, 2 * q + 1):
                        at = r % 2 * 256 + t * 6 * H
                        last = pe.matmul(ps[:, 2 + r // 2, at:at + 6 * H], onehot_t[:, r, t, :],
                                         table[:, ds(b, 1), :, :].rearrange("p o v s -> p (o v s)"),
                                         start=True, stop=True, skip_group_check=True)
                last.then_inc(s_look[r], 1)

            def add_pair(g, i, r, q):
                pe.wait_ge(s_msg[r], i * (G // 2) + q + 1)
                if q < 3:
                    pe.wait_ge(s_acc[q], g)
                else:
                    pe.wait_ge(s_done[(r - 1) % R], i + int(r > 0))
                for t in (2 * q, 2 * q + 1):
                    last = pe.matmul(ps[:, 4 + q, 0:HW], onehot[:, r, t, :], rows[:, r, t, :], start=(t % 2 == 0), stop=(t % 2 == 1))
                last.then_inc(s_sum[q], 1)

            turn_onehots(0, 0, 0)
            look_up(0, 0, 0)
            with pe.Fori(0, GROUPS // R) as i:
                for r in range(R):
                    g = i * R + r
                    near, ni = (r + 1) % R, i + (r + 1) // R
                    turn_onehots(g + 1, ni, near)
                    add_pair(g, i, r, 0)
                    add_pair(g, i, r, 1)
                    look_up(g + 1, ni, near)
                    add_pair(g, i, r, 2)
                    add_pair(g, i, r, 3)
            pe.wait_ge(s_fill, 6)
            with pe.Fori(0, BINS // 2) as i:
                for u in range(2):
                    b = i * 2 + u
                    pe.wait_ge(s_u, b + 1)
                    pe.matmul(ps[0:1, u, 0:D], ones[:, 0:1], xh[:, u, :], start=True, stop=True).then_inc(s_umm, 1)
            pe.wait_ge(s_mean, 1)
            for k in range(KD):
                last = pe.matmul(ps[:, 2, k:k + 1], mean_row[0:1, k * P:(k + 1) * P], ones[0:1, 0:1], start=True, stop=True)
            last.then_inc(s_meanp, 1)
            pe.wait_ge(s_meanc, 1)
            pe.wait_ge(s_small, 16 * LD_SMALL)
            for k in range(KD):
                last = pe.matmul(ps[0:1, 3, 0:NX], mean_col[:, k:k + 1], wr_sb[:, k, :], start=(k == 0), stop=(k == KD - 1))
            last.then_inc(s_logit, 1)
            pe.wait_ge(s_choice, 1)
            pe.matmul(ps[:, 4, 0:2], ones[0:1, :], small[0:1, 12:14], start=True, stop=True).then_inc(s_wb, 1)
            def transposes(c, u, n):
                pe.wait_ge(s_ub, c * CB + n)
                pe.wait_ge(s_ut, c * KD)
                for b in range(n):
                    for k in range(KD):
                        last = pe.transpose(ps[:, k, b * P:(b + 1) * P], u_rows[:, u, b, k * P:(k + 1) * P], ident[:, :])
                last.then_inc(s_utp, 1)

            def first_product(c, n):
                pe.wait_ge(s_ut, (c + 1) * KD)
                for f in range(8):
                    pe.wait_ge(s_act, c * 8 + (f - 1 if f else 0)) if f else None
                    for k in range(KD):
                        last = pe.matmul(ps[:, 2 + f % 2, 0:n * P], w1_sb[:, f // 4, k, f % 4 * P:(f % 4 + 1) * P],
                                         u_t[:, k, 0:n * P], start=(k == 0), stop=(k == KD - 1))
                    last.then_inc(s_m1, 1)

            def second_product(c, u, n):
                pe.wait_ge(s_act, (c + 1) * 8)
                pe.wait_ge(s_y, c)
                for b in range(n):
                    for f in range(8):
                        last = pe.matmul(ps[:, 4 + b, 0:D], act_t[:, u, f, b * P:(b + 1) * P], w2_sb[:, f // 4, f % 4, :],
                                         start=(f == 0), stop=(f == 7))
                    last.then_inc(s_m2, 1)

            pe.wait_ge(s_expw, 1)
            with pe.Fori(0, FULL // 2) as i:
                for u in range(2):
                    c = i * 2 + u
                    transposes(c, u, CB)
                    first_product(c, CB)
                    second_product(c, u, CB)
            transposes(FULL, 0, 1)
            first_product(FULL, 1)
            second_product(FULL, 0, 1)

        @block.vector
        def _(dve):
            own = Count(s_dve)

            def link(instruction):
                own.add(instruction)
                dve.wait_ge(s_dve, own.value)

            dve.memset(src_i, (1 << 13) - 1).then_inc(s_fill, 1)
            dve.memset(dst_i, 0).then_inc(s_fill, 1)
            dve.memset(x_sb[:, NB - 1:XB, :], 0.0).then_inc(s_fill, 1)
            dve.memset(count, 0.0).then_inc(s_fill, 1)
            dve.memset(zeros16[:, :], 0.0).then_inc(s_fill, 1)
            dve.wait_ge(s_fill, 5)
            own.add(dve.memset(mv[:, :, :], 0.0))
            dve.wait_ge(s_x, 16 * LD_X)

            def moments(row, b, u):
                dve.sem_inc(s_go, 1)
                link(dve.bn_stats(stats[:, u, :], row))
                dve.sem_inc(s_go, 1)
                link(dve.bn_aggr(mv_one[:, u, :], stats[:, u, :]))
                link(dve.tensor_scalar(mv[:, ds(b, 1), :].rearrange("p o v -> p (o v)"), mv_one[:, u, :], 0.0, None, ALU.add))

            def row_of(b):
                return x_sb[:, ds(b, 1), :].rearrange("p o d -> p (o d)")

            start = own.value
            with dve.Fori(0, BINS // 2) as i:
                own.value = i * 6 + start
                for u in range(2):
                    moments(row_of(i * 2 + u), i * 2 + u, u)
            own.value = start + BINS * 3
            ve = tmp_a[:, :, 0]
            sq = tmp_a[:, :, 1]

            def inverse_std(n_std, s_out):
                link(dve.tensor_scalar(ve, mv[:, :, 1], EPS, None, ALU.add))
                dve.tensor_copy(rstd[:, :], ve).then_inc(s_out, 1)
                dve.wait_ge(s_std, n_std)
                link(dve.reciprocal(nmr[:, :], rstd[:, :]))
                link(dve.tensor_tensor(sq, nmr[:, :], nmr[:, :], ALU.mult))
                link(dve.tensor_tensor(sq, sq, ve, ALU.mult))
                link(dve.tensor_scalar(sq, sq, -0.5, 1.5, ALU.mult, ALU.add))
                link(dve.tensor_tensor(rstd[:, :], nmr[:, :], sq, ALU.mult))
                link(dve.scalar_tensor_tensor(out=nmr[:, :], in0=mv[:, :, 0], scalar=-1.0, in1=rstd[:, :], op0=ALU.mult, op1=ALU.mult))

            inverse_std(1, s_var)
            dve.sem_inc(s_norm, 1)
            dve.wait_ge(s_w, 16 * LD_W)
            prod = tmp_b[:, 0:2 * P // (2 * H), :].rearrange("p a b -> p (a b)")
            for k in range(KD):
                for a, at in ((ar_bc, HD), (al_bc, HW)):
                    link(dve.tensor_tensor(prod, wx[:, k, 0:HD], a[:, :], ALU.mult))
                    link(dve.tensor_reduce(wx[:, k, at:at + H], prod.rearrange("p (h f) -> p h f", h=H), X, ALU.add))
            dve.sem_inc(s_norm, 1)
            dve.wait_ge(s_edges, 16 * LD_EDGES)
            dve.wait_ge(s_const, N_CONST)
            link(dve.tensor_scalar(work_i, src_i, 7, None, ALU.logical_shift_right))
            link(dve.tensor_copy(bin_16, work_i))
            link(dve.tensor_scalar(work_i, dst_i, SHIFT, 8, ALU.logical_shift_right, ALU.logical_shift_left))
            link(dve.tensor_scalar(src_i, src_i, P - 1, None, ALU.bitwise_and))
            link(dve.scalar_tensor_tensor(out=code_a, in0=src_i, scalar=1.0, in1=work_i, op0=ALU.add, op1=ALU.add))
            link(dve.tensor_scalar(dst_i, dst_i, LOW, None, ALU.bitwise_and))
            link(dve.tensor_copy(code_b, dst_i))
            U = BINS // 5
            with dve.Fori(0, 5) as i:
                for k in range(U):
                    b = i * U + k
                    dve.wait_ge(s_cnt, b)
                    dve.tensor_scalar(rank[:, 0, :], bin_16, iota_b[:, ds(b, 1)], 0.0, ALU.is_equal, ALU.add,
                                      accum_out=count[:, ds(b, 1)]).then_inc(s_cnt, 1)
            dve.wait_ge(s_base, 1)
            link(dve.tensor_scalar(bin_i, ps[:, 5, 0:BINS], float(2 * P - 1), None, ALU.add))
            link(dve.tensor_scalar(bin_i, bin_i, 8, None, ALU.logical_shift_right))
            link(dve.tensor_copy(total, bin_i))
            link(dve.tensor_tensor_scan(ends, total, total, 0.0, ALU.add, ALU.max))
            link(dve.tensor_tensor(total, ends, total, ALU.subtract))
            link(dve.scalar_tensor_tensor(out=base, in0=total, scalar=float(2 * P), in1=ps[:, 4, 0:BINS], op0=ALU.mult, op1=ALU.add))
            link(dve.tensor_tensor(bin_cmp, iota_pair[:, :].rearrange("p (q o) -> p q o", o=1).to_broadcast([P, G // 2, NB]),
                                   ends[:, 0:NB].rearrange("p (o b) -> p o b", o=1).to_broadcast([P, G // 2, NB]), ALU.is_ge))
            link(dve.tensor_reduce(bin_of, bin_cmp, X, ALU.add))
            dve.tensor_copy(bin_of_i, bin_of).then_inc(s_bins, 1)
            link(dve.memset(pos, 0.0))
            link(dve.tensor_scalar(mask[:, 0, :], bin_16, iota_b[:, 0:1], None, ALU.is_equal))
            start = own.value
            with dve.Fori(0, 5) as i:
                own.value = i * (3 * U) + start
                for k in range(U):
                    b = i * U + k
                    w = k % 2
                    link(dve.tensor_tensor_scan(rank[:, w, :], mask[:, w, :], mask[:, w, :], base[:, ds(b, 1)], ALU.add, ALU.max))
                    own.add(dve.tensor_scalar(mask[:, 1 - w, :], bin_16, iota_b[:, ds(b + 1, 1)], None, ALU.is_equal))
                    link(dve.copy_predicated(pos, mask[:, w, :], rank[:, w, :]))
            own.value = start + 3 * U * 5
            link(dve.tensor_scalar(dst_i, pos, float(P - 1), None, ALU.add))
            link(dve.tensor_scalar(work_i, dst_i, 7, None, ALU.logical_shift_right))
            link(dve.tensor_copy(tile_of, work_i))
            link(dve.tensor_scalar(work_i, dst_i, P - 1, None, ALU.bitwise_and))
            link(dve.tensor_copy(place_of, work_i))
            with dve.Fori(0, ECP // UT) as i:
                for t in range(UT):
                    q = t % ONEHOTS
                    j = i * UT + t
                    dve.wait_ge(s_mm[q], i * (UT // ONEHOTS) + t // ONEHOTS)
                    dve.tensor_scalar(oh_a[:, q, :], iota_p16[:, :], place_of[:, ds(j, 1)], code_a[:, ds(j, 1)],
                                      ALU.is_equal, ALU.mult).then_inc(s_oh, 1)
                    dve.tensor_scalar(oh_b[:, q, :], iota_p16[:, :], place_of[:, ds(j, 1)], code_b[:, ds(j, 1)],
                                      ALU.is_equal, ALU.mult).then_inc(s_oh, 1)
                    dve.tensor_scalar(oh_tile[:, q, :], iota_t16[:, :], tile_of[:, ds(j, 1)], None, ALU.is_equal).then_inc(s_oh, 1)
            own.add(dve.memset(slot_s[:, :], 0.0))
            own.add(dve.memset(slot_d[:, :], 0))
            link(dve.memset(slot_r[:, :, :], 0.0))
            dve.wait_ge(s_slots, 1)

            def halves(v):
                return v.rearrange("p (k n) -> p k n", k=2)

            own.add(dve.tensor_copy(halves(slot_a), ps[:, 0:2, 0:HALF]))
            link(dve.tensor_copy(halves(slot_b), ps[:, 2:4, 0:HALF]))
            link(dve.tensor_scalar(slot_d[:, 0:TILES], slot_a, 8, SHIFT, ALU.logical_shift_right, ALU.logical_shift_left))
            link(dve.tensor_tensor(slot_d[:, 0:TILES], slot_d[:, 0:TILES], slot_b, ALU.bitwise_or))
            link(dve.tensor_scalar(slot_a, slot_a, 255, None, ALU.bitwise_and))
            link(dve.tensor_copy(slot_s[:, 0:TILES], slot_a))
            link(dve.tensor_tensor(slot_t, slot_s[:, 0:TILES], slot_s[:, 0:TILES], ALU.mult))
            link(dve.tensor_copy(slot_a, slot_t))
            link(dve.tensor_scalar(slot_b, slot_a, P - 1, None, ALU.bitwise_and))
            own.add(dve.memset(slot_r[:, :, 0:2], 1.0))
            own.add(dve.tensor_copy(slot_r[:, 0:TILES, 2], slot_s[:, 0:TILES]))
            own.add(dve.tensor_copy(slot_r[:, 0:TILES, 4], slot_b))
            link(dve.tensor_tensor(slot_r[:, 0:TILES, 3], slot_t, slot_b, ALU.subtract))
            link(dve.tensor_scalar(part_i[:, :], part_i[:, :], 31, None, ALU.bitwise_and))
            link(dve.tensor_copy(part_k[:, :], part_i[:, :]))
            for k, value in enumerate((-NEG, -NEG, 2 * NEG, -NEG, -NEG)):
                link(dve.tensor_scalar(coef[:, k:k + 1], part_k[:, :], float(k), value, ALU.is_equal, ALU.mult))
            link(dve.tensor_tensor(coef[:, 3:4], coef[:, 3:4], coef[:, 4:5], ALU.add))
            sq_n, lo_n, lo_i = slot_t[:, 0:P], slot_t[:, P:2 * P], slot_a[:, 0:P]
            link(dve.tensor_tensor(sq_n, iota_1[:, :], iota_1[:, :], ALU.mult))
            link(dve.tensor_copy(lo_i, sq_n))
            link(dve.tensor_scalar(lo_i, lo_i, P - 1, None, ALU.bitwise_and))
            link(dve.tensor_copy(lo_n, lo_i))
            link(dve.tensor_tensor(sq_n, sq_n, lo_n, ALU.subtract))
            link(dve.tensor_scalar(sq_n, sq_n, coef[:, 0:1], coef[:, 3:4], ALU.mult, ALU.add))
            link(dve.scalar_tensor_tensor(out=sq_n, in0=lo_n, scalar=coef[:, 1:2], in1=sq_n, op0=ALU.mult, op1=ALU.add))
            link(dve.scalar_tensor_tensor(out=l_mask[:, :], in0=iota_1[:, :], scalar=coef[:, 2:3], in1=sq_n, op0=ALU.mult, op1=ALU.add))
            for h in range(H):
                link(dve.tensor_scalar(coef[:, 5:6], part_k[:, :], float(5 + 3 * h), None, ALU.is_ge))
                link(dve.tensor_scalar(coef[:, 6:7], part_k[:, :], float(7 + 3 * h), None, ALU.is_le))
                link(dve.tensor_tensor(coef[:, 7:8], coef[:, 5:6], coef[:, 6:7], ALU.mult))
                link(dve.tensor_scalar(l_hr[:, h, :], ones[:, :], coef[:, 7:8], None, ALU.mult))
            link(dve.tensor_copy(ident_b[:, :], ident[:, :]))
            own.add(dve.memset(top[:, :, :], -1e30))
            link(dve.memset(pack, 0.0))
            dve.sem_inc(s_table, 1)

            def split(out, value, a, b):
                link(dve.tensor_copy(out[..., 0], value))
                link(dve.tensor_tensor(a, value, out[..., 0], ALU.subtract))
                link(dve.tensor_copy(out[..., 1], a))
                link(dve.tensor_tensor(b, a, out[..., 1], ALU.subtract))
                return dve.tensor_copy(out[..., 2], b)

            dve.wait_ge(s_binld, 16)
            start = own.value
            per_group = 5 + 3
            with dve.Fori(0, GROUPS // R) as i:
                own.value = i * (per_group * R) + start
                for r in range(R):
                    g = i * R + r
                    dve.wait_ge(s_packp[r], i)
                    own.add(dve.tensor_copy(pack[:, r, :, 0:5], slot_r[:, ds(g * G, G), :]))
                    dve.wait_ge(s_gat[r], (i + 1) * 16 * G)
                    last = split(pack[:, r, :, 5:5 + 3 * H].rearrange("p t (h s) -> p t h s", s=3), hr_rows[:, r, :, :], res_a, res_b)
                    last.then_inc(s_pack[r], 1)
                    for q in range(G // 2):
                        w = q % 2
                        b = dve.value_load(bins_row[0:1, ds(g * (G // 2) + q, 1)], min_val=0, max_val=TRASH)
                        dve.wait_ge(s_plane[w], g * 2 + q // 2 + 1)
                        dve.tensor_reduce(part_top[:, w, :], ps[:, 2 * w:2 * w + 2, :].rearrange("p t (h n) -> p h t n", h=H),
                                          XY, ALU.max).then_inc(s_plfree[w], 1)
                        dve.wait_ge(s_plfree[w], g * 2 + q // 2 + 1)
                        where = top[:, ds(b, 1), :].rearrange("p o h -> p (o h)")
                        ins = dve.tensor_tensor(where, where, part_top[:, w, :], ALU.max)
                        if q < G // 2 - 1:
                            link(ins)
                        else:
                            ins.then_inc(s_max[r], 1)
                            dve.wait_ge(s_max[r], i + 1)
            own.value = start + per_group * GROUPS
            dve.wait_ge(s_hcopy, 3 * BINS)
            link(dve.tensor_tensor(tmp_a[:, 0:BINS, 0:H], hl[:, :, :], top[:, :, :], ALU.add))
            link(dve.scalar_tensor_tensor(out=tmp_b[:, 0:BINS, H:2 * H], in0=tmp_a[:, 0:BINS, 0:H], scalar=SLOPE, in1=tmp_a[:, 0:BINS, 0:H], op0=ALU.mult, op1=ALU.max))
            link(dve.tensor_copy(tmp_b[:, 0:BINS, 0:H], hl[:, :, :]))
            link(split(table, tmp_b[:, 0:BINS, :], tmp_a[:, 0:BINS, :], tmp_a[:, 0:BINS, :]))
            link(dve.memset(acc, 0.0))
            dve.sem_inc(s_tab, 1)

            def one_hot(g, r, t):
                dve.tensor_scalar(onehot[:, r, t, :], iota_1[:, :], slot_s[:, ds(g * G + t, 1)], None, ALU.is_equal).then_inc(s_onehot[r], 1)

            for r in range(2):
                for t in range(G):
                    one_hot(r, r, t)
            start = own.value
            per_group = 3
            with dve.Fori(0, GROUPS // R) as i:
                own.value = i * (per_group * R) + start
                for r in range(R):
                    g = i * R + r
                    far = (r + 2) % R
                    dve.wait_ge(s_look[r], i + 1)
                    at = r % 2 * 256
                    dve.tensor_reduce(terms[:, r, :, :], ps[:, 2 + r // 2, at:at + 6 * H * G].rearrange("p (t v s) -> p t v s", t=G, s=3),
                                      X, ALU.add).then_inc(s_terms[r], 1)
                    dve.wait_ge(s_terms[r], i + 1)
                    dve.wait_ge(s_gatb[r], (i + 1) * 16 * G)
                    z, m = terms[:, r, :, 0:H], terms[:, r, :, H:2 * H]
                    link(dve.tensor_tensor(z, z, rows[:, r, :, HD:HW], ALU.add))
                    link(dve.scalar_tensor_tensor(out=z, in0=z, scalar=SLOPE, in1=z, op0=ALU.mult, op1=ALU.max))
                    link(dve.tensor_tensor(z, z, m, ALU.subtract))
                    dve.tensor_scalar(z, z, 0.0, None, ALU.min).then_inc(s_arg[r], 1)
                    dve.wait_ge(s_done[far], i + int(r > 0))
                    one_hot(g + 2, far, 0)
                    one_hot(g + 2, far, 1)

                    def weigh(q):
                        v = rows[:, r, 2 * q:2 * q + 2, 0:HD].rearrange("p t (h f) -> p t h f", h=H)
                        w = rows[:, r, 2 * q:2 * q + 2, HD:HW].rearrange("p t (h o) -> p t h o", o=1)
                        dve.tensor_tensor(v, v, w.to_broadcast([P, 2, H, FH]), ALU.mult).then_inc(s_msg[r], 1)

                    def add_up(q):
                        b = dve.value_load(bins_row[0:1, ds(g * (G // 2) + q, 1)], min_val=0, max_val=TRASH)
                        dve.wait_ge(s_sum[q], g + 1)
                        where = acc[:, ds(b, 1), :].rearrange("p o n -> p (o n)")
                        ins = dve.tensor_tensor(where, where, ps[:, 4 + q, 0:HW], ALU.add)
                        if q < 3:
                            ins.then_inc(s_acc[q], 1)
                            dve.wait_ge(s_acc[q], g + 1)
                        else:
                            ins.then_inc(s_done[r], 1)
                            dve.wait_ge(s_done[r], i + 1)

                    dve.wait_ge(s_wgt[r], i + 1)
                    weigh(0)
                    weigh(1)
                    for t in (2, 3):
                        one_hot(g + 2, far, t)
                    add_up(0)
                    weigh(2)
                    for t in (4, 5):
                        one_hot(g + 2, far, t)
                    add_up(1)
                    weigh(3)
                    for t in (6, 7):
                        one_hot(g + 2, far, t)
                    add_up(2)
                    add_up(3)
            own.value = start + per_group * GROUPS
            den = tmp_b[:, 0:BINS, 0:H]
            link(dve.tensor_scalar(den, acc[:, :, HD:HW], 1e-16, None, ALU.max))
            link(dve.reciprocal(den, den))
            start = own.value
            with dve.Fori(0, BINS // 2) as i:
                own.value = i * 10 + start
                for u in range(2):
                    b = i * 2 + u
                    v = acc[:, ds(b, 1), 0:HD].rearrange("p o (h f) -> p (o h) f", h=H)
                    link(dve.tensor_tensor(v, v, tmp_b[:, ds(b, 1), 0:H].rearrange("p o h -> p h o").to_broadcast([P, H, FH]), ALU.mult))
                    link(dve.tensor_tensor(row_of(b), row_of(b), acc[:, ds(b, 1), 0:HD].rearrange("p o d -> p (o d)"), ALU.add))
                    moments(row_of(b), b, u)
            own.value = start + 5 * BINS
            inverse_std(2, s_x1)
            dve.sem_inc(s_fill, 1)
            link(dve.memset(mean_row[:, :], 0.0))
            start = own.value
            own.add(dve.memset(xh, 0.0))
            link(dve.memset(half_col[:, :], -0.5))
            start = own.value
            with dve.Fori(0, BINS // 2) as i:
                own.value = i * 2 + start
                for u in range(2):
                    b = i * 2 + u
                    dve.tensor_scalar(xh[:, u, :], row_of(b), rstd[:, ds(b, 1)], nmr[:, ds(b, 1)], ALU.mult, ALU.add).then_inc(s_u, 1)
                    dve.wait_ge(s_umm, b + 1)
                    link(dve.tensor_tensor(mean_row[:, :], mean_row[:, :], ps[0:1, u, 0:D], ALU.add))
            own.value = start + BINS
            dve.tensor_scalar(mean_row[:, :], mean_row[:, :], 1.0 / TOKENS, None, ALU.mult).then_inc(s_mean, 1)
            dve.wait_ge(s_meanp, 1)
            dve.tensor_copy(mean_col[:, :], ps[:, 2, 0:KD]).then_inc(s_meanc, 1)
            dve.wait_ge(s_logit, 1)
            dve.wait_ge(s_small, 16 * LD_SMALL)

            def row(k):
                return logit[0:1, k * NX:(k + 1) * NX]

            def one(k):
                return small[0:1, k:k + 1]

            link(dve.tensor_tensor(row(0), ps[0:1, 3, 0:NX], br_row[:, :], ALU.add))
            link(dve.tensor_reduce(one(0), row(0), X, ALU.max))
            dve.tensor_scalar(row(1), row(0), one(0), None, ALU.subtract).then_inc(s_rt, 1)
            dve.wait_ge(s_rte, 1)
            link(dve.tensor_reduce(one(1), row(1), X, ALU.add))
            link(dve.reciprocal(one(2), one(1)))
            link(dve.tensor_scalar(row(2), row(1), one(2), None, ALU.mult))
            link(dve.tensor_scalar(row(4), row(2), float(TOKENS), None, ALU.mult))
            link(dve.reciprocal(row(5), row(4)))
            link(dve.tensor_scalar(row(5), row(5), CAPACITY, 1.0, ALU.mult, ALU.min))
            link(dve.tensor_tensor(row(6), row(2), row(5), ALU.mult))
            link(dve.tensor_reduce(one(3), row(6), X, ALU.max))
            dve.tensor_scalar(row(3), row(6), one(3), None, ALU.subtract).then_inc(s_rt, 1)
            dve.wait_ge(s_rte, 2)
            link(dve.tensor_reduce(one(4), row(3), X, ALU.add))
            link(dve.reciprocal(one(5), one(4)))
            link(dve.tensor_scalar(row(7), row(3), one(5), None, ALU.mult))
            for k in range(2):
                link(dve.tensor_reduce(one(6 + k), row(7), X, ALU.max))
                link(dve.tensor_scalar(row(8), row(7), one(6 + k), float(-NX), ALU.is_equal, ALU.mult))
                link(dve.tensor_tensor(row(8), row(8), iota_b[0:1, 0:NX], ALU.add))
                link(dve.tensor_reduce(one(8 + k), row(8), X, ALU.min))
                link(dve.tensor_scalar(one(8 + k), one(8 + k), float(NX), None, ALU.add))
                link(dve.tensor_scalar(row(9), iota_b[0:1, 0:NX], one(8 + k), -4.0, ALU.is_equal, ALU.mult))
                link(dve.tensor_tensor(row(7), row(7), row(9), ALU.add))
            link(dve.tensor_copy(chosen[:, :], small[0:1, 8:10]))
            dve.tensor_tensor(one(10), one(7), one(6), ALU.subtract).then_inc(s_rt, 1)
            dve.wait_ge(s_rte, 3)
            link(dve.tensor_scalar(one(11), one(10), 1.0, None, ALU.add))
            link(dve.reciprocal(one(12), one(11)))
            link(dve.tensor_tensor(one(13), one(10), one(12), ALU.mult))
            dve.sem_inc(s_choice, 1)
            dve.wait_ge(s_wb, 1)
            link(dve.tensor_copy(top_w[:, :], ps[:, 4, 0:2]))
            dve.wait_ge(s_exp, 8 * 16)
            for k in range(2):
                v = w2_sb[:, k, :, :].rearrange("p k n -> p (k n)")
                link(dve.tensor_scalar(v, v, top_w[:, k:k + 1], None, ALU.mult))
                link(dve.tensor_scalar(b2_bc[:, k, :], b2_bc[:, k, :], top_w[:, k:k + 1], None, ALU.mult))
            link(dve.tensor_tensor(b2_bc[:, 0, :], b2_bc[:, 0, :], b2_bc[:, 1, :], ALU.add))
            dve.sem_inc(s_expw, 1)

            def rows_in(c, u, n):
                for b in range(n):
                    w = c * CB + b
                    dve.tensor_scalar(u_rows[:, u, b, :], row_of(w), rstd[:, ds(w, 1)], nmr[:, ds(w, 1)], ALU.mult, ALU.add).then_inc(s_ub, 1)

            def sums(c, u, n):
                for b in range(n):
                    v = y[:, u, b, :]
                    dve.wait_ge(s_m2, c * CB + b + 1)
                    link(dve.tensor_tensor(v, ps[:, 4 + b, 0:D], u_rows[:, u, b, :], ALU.add))
                    link(dve.tensor_tensor(v, v, b2_bc[:, 0, :], ALU.add))
                    link(dve.bn_stats(stats2[:, b, :], v))
                    dve.sem_inc(s_go, 1)
                    link(dve.bn_aggr(mv2[:, u, b, :], stats2[:, b, :]))
                dve.tensor_scalar(ve2[:, u, 0:n], mv2[:, u, 0:n, 1], EPS, None, ALU.add).then_inc(s_y, 1)

            def finish(c, u, n):
                dve.wait_ge(s_pow, c + 1)
                link(dve.tensor_tensor(t2[:, u, 0:n], r2[:, u, 0:n], r2[:, u, 0:n], ALU.mult))
                link(dve.tensor_tensor(t2[:, u, 0:n], t2[:, u, 0:n], ve2[:, u, 0:n], ALU.mult))
                link(dve.tensor_scalar(t2[:, u, 0:n], t2[:, u, 0:n], -0.5, 1.5, ALU.mult, ALU.add))
                link(dve.tensor_tensor(r2[:, u, 0:n], r2[:, u, 0:n], t2[:, u, 0:n], ALU.mult))
                for b in range(n):
                    v = y[:, u, b, :]
                    link(dve.tensor_scalar(v, v, mv2[:, u, b, 0:1], r2[:, u, b:b + 1], ALU.subtract, ALU.mult))
                    link(dve.tensor_tensor(v, v, gamma_bc[:, :], ALU.mult))
                    link(dve.tensor_tensor(v, v, beta_bc[:, :], ALU.add))
                    dve.tensor_tensor(v, v, row_of(c * CB + b), ALU.add).then_inc(s_out, 1)

            rows_in(0, 0, CB)
            start = own.value
            per_chunk = 4 * CB + 4 + 3 * CB
            with dve.Fori(0, FULL // 2) as i:
                own.value = i * (2 * per_chunk) + start
                for u in range(2):
                    c = i * 2 + u
                    rows_in(c + 1, 1 - u, CB)
                    dve.wait_ge(s_st[u], i * 16)
                    sums(c, u, CB)
                    finish(c, u, CB)
            own.value = start + FULL * per_chunk
            dve.wait_ge(s_st[0], FULL // 2 * 16)
            sums(FULL, 0, 1)
            finish(FULL, 0, 1)


_INS = ['x', 'src', 'dst', 'L0_gnn_W', 'L0_gnn_a_l', 'L0_gnn_a_r', 'L0_ffn_Wr', 'L0_ffn_br', 'L0_ffn_W1', 'L0_ffn_b1',
        'L0_ffn_W2', 'L0_ffn_b2', 'L0_ffn_gamma', 'L0_ffn_beta']


def kernel(**inputs):
    import numpy as _np
    import concourse.bacc as _bacc
    from concourse import mybir as _mybir
    from concourse.bass_utils import run_bass_kernel_spmd as _run

    nc = _bacc.Bacc("TRN2", target_bir_lowering=False, num_devices=1)
    arrays, args = {}, []
    for name in _INS:
        a = _np.ascontiguousarray(inputs[name])
        arrays[f"in_{name}_dram"] = a
        args.append(nc.dram_tensor(f"in_{name}_dram", a.shape, _mybir.dt.from_np(a.dtype), kind="ExternalInput").ap())
    shape = inputs["x"].shape
    args.append(nc.dram_tensor("out_0_dram", shape, _mybir.dt.float32, kind="ExternalOutput").ap())
    gat_moe_block(nc, *args)
    r = _run(nc, [arrays], core_ids=[0])
    return r.results[0]["out_0_dram"]
```

```python
from contextlib import ExitStack

import concourse.bass as bass
from concourse import mybir

P = 128
F32 = mybir.dt.float32
F16 = mybir.dt.float16
BF16 = mybir.dt.bfloat16
I32 = mybir.dt.int32
U32 = mybir.dt.uint32
U16 = mybir.dt.uint16
ALU = mybir.AluOpType
ACT = mybir.ActivationFunctionType
PE = mybir.EngineType.PE
DVE = mybir.EngineType.DVE
X = mybir.AxisListType.X
XY = mybir.AxisListType.XY
ds = bass.ds


class Count:

    def __init__(self, sem):
        self.sem, self.value = sem, 0

    def add(self, instruction):
        instruction.then_inc(self.sem, 1)
        self.value = self.value + 1


def gat_moe_block(nc, x, src, dst, gat_w, a_l, a_r, w_r, b_r, w_1, b_1, w_2, b_2, gamma, beta, out):
    N, D = x.shape
    E = src.shape[0]
    H, FH = a_l.shape[1], a_l.shape[2]
    NX, FF = w_1.shape[0], w_1.shape[2]
    HD = H * FH
    HW = HD + H
    KD = D // P
    NB = -(-N // P)
    TRASH = NB
    BINS = NB + 1 + (NB + 1) % 2
    LAST = N - (NB - 1) * P
    EC = -(-E // P)
    UT = 8
    ECP = -(-EC // UT) * UT
    E_LAST = E - (P - 1) * EC
    PAIRS = (E + NB * (2 * P - 1)) // (2 * P)
    G = 8
    R = 3
    GROUPS = -(-(-(-2 * PAIRS // G)) // R) * R
    TILES = GROUPS * G
    TPAD = TILES + 2 * G
    SC = 3
    EC_POOL = min(E_LAST, ECP * 3 // 7) // (SC * UT) * (SC * UT)
    NPAIRS = TILES // 2
    HALF = TILES // 2
    SHIFT = 11
    LOW = (1 << SHIFT) - 1
    NEG = float(2 ** 80)
    SLOPE = 0.2
    EPS = 1e-5
    TOKENS = N
    CAPACITY = float(-(-TOKENS * 5 // (4 * NX)))
    ROWS = BINS * P
    BB = 5
    CB = 4
    CN = CB * P
    FULL = (NB - 1) // CB
    XB = (FULL + 1) * CB
    assert HD == D == 2 * P and FF == 4 * P and TILES <= 2 * 512 and N < 4 << SHIFT and GROUPS < P

    h_table = nc.dram_tensor("h_table", (ROWS, HW), F32, kind="Internal").ap()
    hr_table = nc.dram_tensor("hr_table", (ROWS, H), F32, kind="Internal").ap()
    slot_table = nc.dram_tensor("slot_table", (P * TILES + 1, 1), I32, kind="Internal").ap()
    bin_table = nc.dram_tensor("bin_table", (P, G // 2), I32, kind="Internal").ap()

    with ExitStack() as ctx:
        def sb(name, shape, dt=F32):
            return ctx.enter_context(nc.sbuf_tensor(name, shape, dt))

        def sem(name):
            return ctx.enter_context(nc.semaphore(name))

        def sems(name, n):
            return [sem(f"{name}{k}") for k in range(n)]

        def carve(arena, sizes):
            at, views = 0, []
            for dt, shape in sizes:
                n = 1
                for k in shape:
                    n *= k
                words = n * mybir.dt.size(dt) // 4
                v = arena[:, at:at + words]
                if dt != F32:
                    v = v.bitcast(dt)
                if len(shape) == 2:
                    v = v.rearrange("p (a b) -> p a b", b=shape[1])
                elif len(shape) == 3:
                    v = v.rearrange("p (a b c) -> p a b c", b=shape[1], c=shape[2])
                elif len(shape) == 4:
                    v = v.rearrange("p (a b c d) -> p a b c d", b=shape[1], c=shape[2], d=shape[3])
                views.append(v)
                at += words
            return views

        x_sb = sb("x_sb", [P, XB, D])
        wx = sb("wx", [P, KD, HD + 2 * H])
        al_bc = sb("al_bc", [P, HD])
        ar_bc = sb("ar_bc", [P, HD])
        hl = sb("hl", [P, BINS, H])
        hr = sb("hr", [P, BINS, H])
        top = sb("top", [P, BINS, H])
        table = sb("table", [P, BINS, 2 * H, 3], BF16)
        mv = sb("mv", [P, XB, 2])
        rstd = sb("rstd", [P, XB])
        nmr = sb("nmr", [P, XB])
        stats = sb("stats", [P, BB, 6])
        mv_one = sb("mv_one", [P, BB, 2])
        rstd_now = sb("rstd_now", [P, 2, BB])
        tmp_a = sb("tmp_a", [P, XB, 2 * H])
        tmp_b = sb("tmp_b", [P, XB, 2 * H])
        iota_1 = sb("iota_1", [P, P])
        iota_p16 = sb("iota_p16", [P, P], F16)
        iota_t16 = sb("iota_t16", [P, TILES], F16)
        iota_b = sb("iota_b", [P, BINS + 1])
        iota_pair = sb("iota_pair", [P, G // 2])
        part_i = sb("part_i", [P, 1], I32)
        part_k = sb("part_k", [P, 1])
        ident = sb("ident", [P, P])
        ident_b = sb("ident_b", [P, P], BF16)
        before = sb("before", [P, P])
        ones = sb("ones", [P, P])
        zeros16 = sb("zeros16", [P, HALF], F16)
        l_mask = sb("l_mask", [P, P], BF16)
        l_hr = sb("l_hr", [P, H, P], BF16)
        coef = sb("coef", [P, 12])
        slot_s = sb("slot_s", [P, TPAD])
        slot_d = sb("slot_d", [P, TPAD], I32)
        slot_r = sb("slot_r", [P, TPAD, 5], BF16)
        bins_row = sb("bins_row", [1, P * G // 2], I32)
        small = sb("small", [1, 64])
        logit = sb("logit", [1, 16 * NX])
        chosen = sb("chosen", [1, 2], I32)
        mean_row = sb("mean_row", [1, D])
        mean_col = sb("mean_col", [P, KD])
        wr_sb = sb("wr_sb", [P, KD, NX])
        br_row = sb("br_row", [1, NX])
        top_w = sb("top_w", [P, 2])
        nmr_sum = sb("nmr_sum", [P, 1])

        ACC_PART = -(-BINS * HW // (GROUPS // R))
        arena_a = sb("arena_a", [P, ACC_PART * (GROUPS // R)])
        (src_i, dst_i, work_i, code_a, code_b, pos, tile_of, place_of, bin_16, mask, rank, code_c, linear) = carve(arena_a, [
            (I32, [ECP]), (I32, [ECP]), (I32, [ECP]), (F32, [ECP]), (F32, [ECP]), (F32, [ECP]), (F32, [ECP]),
            (F32, [ECP]), (F16, [ECP]), (U16, [2, ECP]), (F32, [2, ECP]), (F32, [ECP]), (F32, [ECP])])
        stage_at = sb("stage_at", [P, SC, UT], U32)
        stage_code = sb("stage_code", [P, SC, UT], I32)
        (acc,) = carve(arena_a, [(F32, [BINS, HW])])
        (act_t, u_t, u_rows) = carve(arena_a, [(F32, [2, 8, CN]), (F32, [KD, CN]), (F32, [2, CB, D])])
        arena_b = sb("arena_b", [P, 11700])
        ONEHOTS = 4
        (oh_tile, oh_a, oh_b) = carve(arena_b, [(F16, [ONEHOTS, TILES]), (F16, [ONEHOTS, P]), (F16, [ONEHOTS, P])])
        n0 = ONEHOTS * (TILES + 2 * P) // 2
        (xh, xh_t, h_out) = carve(arena_b[:, n0:], [(F32, [2, D]), (F32, [2, KD, P]), (F32, [2, HW])])
        n0 += 4 * D + 2 * HW
        (count, base, total, ends, bin_i) = carve(arena_b[:, n0:], [
            (F32, [BINS]), (F32, [BINS]), (F32, [BINS]), (F32, [BINS]), (I32, [BINS])])
        n0 += 5 * BINS
        (bin_cmp, bin_of, bin_of_i) = carve(arena_b[:, n0:], [(F32, [G // 2, NB]), (F32, [G // 2]), (I32, [G // 2])])
        n0 += G // 2 * NB + G
        (slot_a, slot_b, slot_t) = carve(arena_b[:, n0:], [(I32, [TILES]), (I32, [TILES]), (F32, [TILES])])
        (rows, onehot, onehot_t) = carve(arena_b, [(F32, [R, G, HW]), (F32, [R, G, P]), (BF16, [R, G, P])])
        n1 = R * G * (HW + P + P // 2)
        (terms,) = carve(arena_b[:, n1:], [(F32, [R, G, 2 * H])])
        idx = sb("idx", [P, R, G], U32)
        (hr_rows, pack, pack_t, res_a, res_b) = carve(arena_b, [
            (F32, [R, G, H]), (BF16, [R, G, 32]), (BF16, [R, 2, P]), (F32, [G, H]), (F32, [G, H])])
        n0 += 3 * TILES
        (pair_top, run_before, bins_all, new_bin) = carve(arena_b[:, n0:], [
            (F32, [H, NPAIRS]), (F32, [H, NPAIRS + 1]), (I32, [NPAIRS]), (F32, [NPAIRS])])
        (slot_c,) = carve(arena_b[:, n0:], [(I32, [TILES])])
        run_top = run_before[:, :, 1:NPAIRS + 1]
        pairs_to = sb("pairs_to", [1, BINS], I32)
        (w1_sb, w2_sb, y) = carve(arena_b, [(F32, [2, KD, FF]), (F32, [2, 4, D]), (F32, [2, CB, D])])
        b1_sb = sb("b1_sb", [P, 2, FF // P])
        b2_bc = sb("b2_bc", [P, 2, D])
        gamma_bc = sb("gamma_bc", [P, D])
        beta_bc = sb("beta_bc", [P, D])
        mv2 = sb("mv2", [P, 2, CB, 2])
        ve2 = sb("ve2", [P, 2, CB])
        r2 = sb("r2", [P, 2, CB])
        t2 = sb("t2", [P, 2, CB])
        half_col = sb("half_col", [P, CB])

        ps = ctx.enter_context(nc.psum_tensor("ps", [P, 8, 512], F32))

        s_const = sem("s_const")
        s_fill = sem("s_fill")
        s_edges = sem("s_edges")
        s_w = sem("s_w")
        s_x = sem("s_x")
        s_small = sem("s_small")
        s_dve = sem("s_dve")
        s_go = sem("s_go")
        s_std = sem("s_std")
        s_var = sem("s_var")
        s_norm = sem("s_norm")
        s_xh = sem("s_xh")
        s_xhp = sem("s_xhp")
        s_xht = sem("s_xht")
        s_h = sem("s_h")
        s_hcopy = sem("s_hcopy")
        s_hst = sems("s_hst", 2)
        s_hrst = sem("s_hrst")
        s_cnt = sem("s_cnt")
        s_base = sem("s_base")
        s_bins = sem("s_bins")
        s_binst = sem("s_binst")
        s_binld = sem("s_binld")
        s_binall = sem("s_binall")
        s_oh = sem("s_oh")
        s_mm = sems("s_mm", ONEHOTS)
        s_zero = sem("s_zero")
        s_zeroed = sem("s_zeroed")
        s_linear = sem("s_linear")
        s_stage = sems("s_stage", SC)
        s_scat = sems("s_scat", SC)
        s_slotld = sem("s_slotld")
        s_slots = sem("s_slots")
        s_table = sem("s_table")
        s_idx = sems("s_idx", R)
        s_turn = sem("s_turn")
        s_gat = sems("s_gat", R)
        s_pack = sems("s_pack", R)
        s_packp = sems("s_packp", R)
        s_packt = sems("s_packt", R)
        s_plane = sems("s_plane", 2)
        s_plfree = sems("s_plfree", 2)
        s_tab = sem("s_tab")
        s_idxb = sems("s_idxb", R)
        s_gatb = sems("s_gatb", R)
        s_onehot = sems("s_onehot", R)
        s_ohp = sem("s_ohp")
        s_oht = sem("s_oht")
        s_look = sems("s_look", R)
        s_terms = sems("s_terms", R)
        s_arg = sems("s_arg", R)
        s_wgt = sems("s_wgt", R)
        s_msg = sems("s_msg", R)
        s_sum = sems("s_sum", 4)
        s_acc = sems("s_acc", 3)
        s_done = sems("s_done", R)
        s_x1 = sem("s_x1")
        s_u = sem("s_u")
        s_umm = sems("s_umm", 2)
        s_mean = sem("s_mean")
        s_meanp = sem("s_meanp")
        s_meanc = sem("s_meanc")
        s_logit = sem("s_logit")
        s_rt = sem("s_rt")
        s_rte = sem("s_rte")
        s_choice = sem("s_choice")
        s_wb = sem("s_wb")
        s_exp = sem("s_exp")
        s_expw = sem("s_expw")
        s_ub = sem("s_ub")
        s_utp = sem("s_utp")
        s_ut = sem("s_ut")
        s_m1 = sem("s_m1")
        s_act = sem("s_act")
        s_m2 = sem("s_m2")
        s_y = sem("s_y")
        s_pow = sem("s_pow")
        s_out = sem("s_out")
        s_st = sems("s_st", 2)

        LD_EDGES, LD_W, LD_X, LD_SMALL = 4, 3, 2, 4
        N_CONST = 10
        block = ctx.enter_context(nc.Block())

        def bins_of(engine, g):
            _, bins = nc.values_load_multi_w_load_instructions(
                bins_row[0:1, ds(g * (G // 2), G // 2)], engines=[engine], min_val=0, max_val=TRASH,
                skip_runtime_bounds_check_because="a pair's bin is a count of at most TRASH comparisons that hold")
            return bins

        @block.sync
        def _(sp):
            sp.wait_ge(s_fill, 2)
            for a, v in ((src, src_i), (dst, dst_i)):
                body = a[0:(P - 1) * EC].rearrange("(p c) -> p c", c=EC)
                sp.dma_start(v[0:P - 1, 0:EC], body).then_inc(s_edges, 16)
                tail = a[(P - 1) * EC:E].rearrange("(p c) -> p c", p=1)
                sp.dma_start(v[P - 1:P, 0:E_LAST], tail).then_inc(s_edges, 16)
            sp.wait_ge(s_fill, 3)
            sp.dma_start(x_sb[:, 0:NB - 1, :], x[0:(NB - 1) * P, :].rearrange("(b p) d -> p b d", p=P)).then_inc(s_x, 16)
            sp.dma_start(x_sb[0:LAST, NB - 1, :], x[(NB - 1) * P:N, :]).then_inc(s_x, 16)
            sp.dma_start(wx[:, :, 0:HD], gat_w.rearrange("(k p) n -> p k n", p=P)).then_inc(s_w, 16)
            for a, v in ((a_l, al_bc), (a_r, ar_bc)):
                sp.dma_start(v[:, :], a.rearrange("o h f -> o (h f)").to_broadcast([P, HD])).then_inc(s_w, 16)
            sp.dma_start(wr_sb[:, :, :], w_r.rearrange("(k p) n -> p k n", p=P)).then_inc(s_small, 16)
            sp.dma_start(br_row[:, :], b_r.rearrange("(o n) -> o n", o=1)).then_inc(s_small, 16)
            for a, v in ((gamma, gamma_bc), (beta, beta_bc)):
                sp.dma_start(v[:, :], a.rearrange("(o n) -> o n", o=1).to_broadcast([P, D])).then_inc(s_small, 16)
            sp.wait_ge(s_zero, 1)
            table_rows = slot_table[1:P * TILES + 1, :].rearrange("(p t) o -> p (t o)", p=P)
            sp.dma_start(table_rows, slot_d[:, 0:TILES]).then_inc(s_zeroed, 16)
            with sp.Fori(0, BINS // 2) as i:
                for u in range(2):
                    sp.wait_ge(s_hcopy, (i * 2 + u) * 3 + 3)
                    sp.dma_start(h_table[ds((i * 2 + u) * P, P), :], h_out[:, u, :]).then_inc(s_hst[u], 16)
            sp.dma_start(hr_table.rearrange("(b p) h -> p b h", p=P), hr[:, :, :]).then_inc(s_hrst, 16)
            sp.wait_ge(s_bins, 1)
            sp.dma_start(bin_table, bin_of_i).then_inc(s_binst, 16)
            sp.wait_ge(s_binst, 16)
            sp.dma_start(bins_row[:, :], bin_table.rearrange("(o g) q -> o (g q)", o=1)).then_inc(s_binld, 16)
            for r in range(SC):
                sp.wait_ge(s_scat[r], EC_POOL // SC * 16)
            sp.dma_start(slot_c, table_rows).then_inc(s_slotld, 16)
            sp.dma_start(bins_all, bin_table[0:GROUPS, :].rearrange("(o g) q -> o (g q)", o=1).to_broadcast([P, NPAIRS])).then_inc(s_binall, 16)
            sp.wait_ge(s_choice, 1)
            for k in range(2):
                e = sp.value_load(chosen[0:1, k:k + 1], min_val=0, max_val=NX - 1)
                sp.dma_start(w1_sb[:, k, :, :], w_1[ds(e, 1), :, :].rearrange("e (k p) f -> p (e k) f", p=P)).then_inc(s_exp, 16)
                sp.dma_start(w2_sb[:, k, :, :], w_2[ds(e, 1), :, :].rearrange("e (k p) f -> p (e k) f", p=P)).then_inc(s_exp, 16)
                with nc.allow_non_contiguous_dma(reason="512 biases, one a partition"):
                    sp.dma_start(b1_sb[:, k, :], b_1[ds(e, 1), :].rearrange("e (k p) -> p (e k)", p=P)).then_inc(s_exp, 16)
                sp.dma_start(b2_bc[:, k, :], b_2[ds(e, 1), :].to_broadcast([P, D])).then_inc(s_exp, 16)
            with sp.Fori(0, FULL // 2) as i:
                for u in range(2):
                    c = i * 2 + u
                    sp.wait_ge(s_out, (c + 1) * CB)
                    sp.dma_start(out[ds(c * CN, CN), :].rearrange("(b p) d -> p b d", p=P), y[:, u, :, :]).then_inc(s_st[u], 16)
            sp.wait_ge(s_out, FULL * CB + 1)
            sp.dma_start(out[(NB - 1) * P:N, :], y[0:LAST, 0, 0, :]).then_inc(s_st[0], 16)
            sp.wait_ge(s_st[0], 16 * (FULL // 2 + 1))
            sp.wait_ge(s_st[1], 16 * (FULL // 2))

        @block.gpsimd
        def _(pool):
            iota = dict(allow_small_or_imprecise_dtypes=True)
            pool.iota(iota_1[:, :], pattern=[[1, P]], base=1, channel_multiplier=0, **iota).then_inc(s_const, 1)
            pool.iota(iota_p16[:, :], pattern=[[1, P]], base=0, channel_multiplier=0, **iota).then_inc(s_const, 1)
            pool.iota(iota_t16[:, :], pattern=[[1, TILES]], base=1, channel_multiplier=0, **iota).then_inc(s_const, 1)
            pool.iota(iota_b[:, :], pattern=[[1, BINS + 1]], base=0, channel_multiplier=0, **iota).then_inc(s_const, 1)
            pool.iota(iota_pair[:, :], pattern=[[1, G // 2]], base=0, channel_multiplier=G // 2, **iota).then_inc(s_const, 1)
            pool.iota(part_i[:, :], pattern=[[1, 1]], base=0, channel_multiplier=1).then_inc(s_const, 1)
            pool.memset(ones[:, :], 1.0).then_inc(s_const, 1)
            pool.memset(ident[:, :], 0.0).then_inc(s_const, 1)
            pool.wait_ge(s_const, 8)
            pool.affine_select(out=ident[:, :], in_=ident[:, :], compare_op=ALU.not_equal, fill=1.0, base=0,
                               pattern=[[-1, P]], channel_multiplier=1).then_inc(s_const, 1)
            pool.affine_select(out=before[:, :], in_=ones[:, :], compare_op=ALU.is_gt, fill=0.0, base=0,
                               pattern=[[1, P]], channel_multiplier=-1).then_inc(s_const, 1)
            pool.wait_ge(s_zeroed, 16)
            with pool.Fori(0, EC_POOL // (SC * UT)) as i:
                for r in range(SC):
                    pool.wait_ge(s_stage[r], i + 1)
                    pool.sem_inc(s_turn, 1)
                    for t in range(UT):
                        pool.indirect_dma_start(out=slot_table, out_offset=bass.IndirectOffsetOnAxis(ap=stage_at[:, r, t:t + 1], axis=0),
                                                in_=stage_code[:, r, t:t + 1], in_offset=None).then_inc(s_scat[r], 16)
            pool.wait_ge(s_hrst, 16)
            def gather_hr(i, r):
                pool.wait_ge(s_idx[r], i + 1)
                pool.wait_ge(s_pack[r], i)
                pool.sem_inc(s_turn, 1)
                for t in range(G):
                    pool.indirect_dma_start(out=hr_rows[:, r, t, :], out_offset=None, in_=hr_table,
                                            in_offset=bass.IndirectOffsetOnAxis(ap=idx[:, r, t:t + 1], axis=0)
                                            ).then_inc(s_gat[r], 16)

            with pool.Fori(0, GROUPS // R) as i:
                for r in range(R):
                    gather_hr(i, r)
            gather_hr(GROUPS // R, 0)
            for u in range(2):
                pool.wait_ge(s_hst[u], 16 * (BINS // 2))
            pool.wait_ge(s_tab, 1)

            def gather_rows(i, r):
                pool.wait_ge(s_idxb[r], i + 1)
                pool.wait_ge(s_done[r], i)
                pool.sem_inc(s_turn, 1)
                for t in range(G):
                    pool.indirect_dma_start(out=rows[:, r, t, :], out_offset=None, in_=h_table,
                                            in_offset=bass.IndirectOffsetOnAxis(ap=idx[:, r, t:t + 1], axis=0)
                                            ).then_inc(s_gatb[r], 16)

            with pool.Fori(0, GROUPS // R) as i:
                for r in range(R):
                    gather_rows(i, r)
            gather_rows(GROUPS // R, 0)
            def power(c, u, n):
                pool.wait_ge(s_y, c + 1)
                pool.tensor_tensor(r2[:, u, 0:n], ve2[:, u, 0:n], half_col[:, 0:n], ALU.pow).then_inc(s_pow, 1)
            with pool.Fori(0, FULL // 2) as i:
                for u in range(2):
                    power(i * 2 + u, u, CB)
            power(FULL, 0, 1)

        @block.scalar
        def _(act):
            act.wait_ge(s_var, 1)
            act.activation(rstd[:, :], rstd[:, :], ACT.Sqrt).then_inc(s_std, 1)
            act.wait_ge(s_norm, 1)

            def normalise(b, u):
                act.activation(xh[:, u, :], x_sb[:, ds(b, 1), :].rearrange("p o d -> p (o d)"), ACT.Identity,
                               scale=rstd[:, ds(b, 1)], bias=nmr[:, ds(b, 1)]).then_inc(s_xh, 1)

            normalise(0, 0)
            with act.Fori(0, BINS // 2) as i:
                for u in range(2):
                    b = i * 2 + u
                    act.wait_ge(s_xhp, b + 1)
                    act.activation(xh_t[:, u, :, :].rearrange("p k n -> p (k n)"), ps[:, 4 + u, 0:D], ACT.Copy).then_inc(s_xht, 1)
                    normalise(b + 1, 1 - u)
                    act.wait_ge(s_h, b + 1)
                    act.wait_ge(s_hst[u], i * 16)
                    act.activation(h_out[:, u, :], ps[:, 6 + u, 0:HW], ACT.Copy).then_inc(s_hcopy, 1)
                    act.activation(hr[:, ds(b, 1), :].rearrange("p o h -> p (o h)"), ps[:, 6 + u, HD:HW], ACT.Copy).then_inc(s_hcopy, 1)
                    act.activation(hl[:, ds(b, 1), :].rearrange("p o h -> p (o h)"), ps[:, 6 + u, HW:HW + H], ACT.Copy).then_inc(s_hcopy, 1)
            act.wait_ge(s_linear, 1)
            with act.Fori(0, EC_POOL // (SC * UT)) as i:
                for r in range(SC):
                    at = (i * SC + r) * UT
                    act.wait_ge(s_scat[r], i * 16 * UT)
                    act.activation(stage_at[:, r, :], linear[:, ds(at, UT)], ACT.Copy)
                    act.activation(stage_code[:, r, :], code_c[:, ds(at, UT)], ACT.Copy).then_inc(s_stage[r], 1)
            act.wait_ge(s_table, 1)

            def place_targets(g, r, sem_out):
                act.activation(idx[:, r, :], slot_d[:, ds(g * G, G)], ACT.Copy).then_inc(sem_out[r], 1)

            for r in range(2):
                place_targets(r, r, s_idx)
            with act.Fori(0, GROUPS // R) as i:
                for r in range(R):
                    g = i * R + r
                    far, fi = (r + 2) % R, i + (r + 2) // R
                    act.wait_ge(s_gat[far], fi * 16 * G)
                    place_targets(g + 2, far, s_idx)
                    act.wait_ge(s_packp[r], i + 1)
                    act.wait_ge(s_plane[1], (i * R + r) * 2)
                    act.activation(pack_t[:, r, :, :].rearrange("p k n -> p (k n)"),
                                   ps[:, 4 + r, 0:P].bitcast(BF16), ACT.Copy).then_inc(s_packt[r], 1)
            act.wait_ge(s_tab, 1)

            def copy_onehots(g, i, r, k):
                act.wait_ge(s_ohp, g * 2 + k + 1)
                act.wait_ge(s_look[r], i)
                act.activation(onehot_t[:, r, 4 * k:4 * k + 4, :].rearrange("p k n -> p (k n)"), ps[:, k, :], ACT.Copy).then_inc(s_oht, 1)

            def weights(i, r):
                act.wait_ge(s_arg[r], i + 1)
                act.activation(rows[:, r, :, HD:HW], terms[:, r, :, 0:H], ACT.Exp).then_inc(s_wgt[r], 1)

            for r in range(2):
                place_targets(r, r, s_idxb)
            for r in range(2):
                for k in range(2):
                    copy_onehots(r, 0, r, k)
            weights(0, 0)
            with act.Fori(0, GROUPS // R) as i:
                for r in range(R):
                    g = i * R + r
                    far, fi = (r + 2) % R, i + (r + 2) // R
                    act.wait_ge(s_gatb[far], fi * 16 * G)
                    place_targets(g + 2, far, s_idxb)
                    weights(i + (r + 1) // R, (r + 1) % R)
                    for k in range(2):
                        copy_onehots(g + 2, fi, far, k)
            act.wait_ge(s_x1, 1)
            act.activation(rstd[:, :], rstd[:, :], ACT.Sqrt).then_inc(s_std, 1)
            act.wait_ge(s_rt, 1)
            act.activation(logit[0:1, NX:2 * NX], logit[0:1, NX:2 * NX], ACT.Exp).then_inc(s_rte, 1)
            act.wait_ge(s_rt, 2)
            act.activation(logit[0:1, 3 * NX:4 * NX], logit[0:1, 3 * NX:4 * NX], ACT.Exp).then_inc(s_rte, 1)
            act.wait_ge(s_rt, 3)
            act.activation(small[0:1, 10:11], small[0:1, 10:11], ACT.Exp).then_inc(s_rte, 1)
            act.wait_ge(s_exp, 8 * 16)

            def transposes_out(c, n):
                act.wait_ge(s_utp, c + 1)
                act.wait_ge(s_m1, c * 8)
                for k in range(KD):
                    act.activation(u_t[:, k, 0:n * P], ps[:, k, 0:n * P], ACT.Copy).then_inc(s_ut, 1)

            def gelus(c, u, n):
                for f in range(8):
                    act.wait_ge(s_m1, c * 8 + f + 1)
                    act.activation(act_t[:, u, f, 0:n * P], ps[:, 2 + f % 2, 0:n * P], ACT.Gelu,
                                   bias=b1_sb[:, f // 4, f % 4:f % 4 + 1]).then_inc(s_act, 1)

            transposes_out(0, CB)
            with act.Fori(0, FULL // 2) as i:
                for u in range(2):
                    c = i * 2 + u
                    gelus(c, u, CB)
                    transposes_out(c + 1, CB)
            gelus(FULL, 0, 1)

        @block.tensor
        def _(pe):
            pe.wait_ge(s_const, N_CONST)
            pe.wait_ge(s_cnt, BINS)
            pe.matmul(ps[:, 4, 0:BINS], before[:, :], count, start=True, stop=True)
            pe.matmul(ps[:, 5, 0:BINS], ones[:, :], count, start=True, stop=True).then_inc(s_base, 1)
            pe.wait_ge(s_norm, 2)
            with pe.Fori(0, BINS // 2) as i:
                for u in range(2):
                    b = i * 2 + u
                    pe.wait_ge(s_xh, b + 1)
                    for k in range(KD):
                        last = pe.transpose(ps[:, 4 + u, k * P:(k + 1) * P], xh[:, u, k * P:(k + 1) * P], ident[:, :])
                    last.then_inc(s_xhp, 1)
                    pe.wait_ge(s_xht, b + 1)
                    pe.wait_ge(s_hcopy, i * 6)
                    for k in range(KD):
                        last = pe.matmul(ps[:, 6 + u, 0:HW + H], xh_t[:, u, k, :], wx[:, k, :], start=(k == 0), stop=(k == KD - 1))
                    last.then_inc(s_h, 1)
            def onto(k, lhs, rhs, **flags):
                return pe.matmul(ps[:, k, 0:HALF], lhs, rhs, skip_group_check=True, **flags)

            pe.wait_ge(s_fill, 5)
            for k in range(4):
                onto(k, zeros16[:, 0:P], zeros16[:, :], start=True, stop=False)
            with pe.Fori(0, (ECP - EC_POOL) // UT) as i:
                for t in range(UT):
                    q = t % ONEHOTS
                    pe.wait_ge(s_oh, (i * UT + t) * 3 + 3)
                    for k in range(4):
                        last = onto(k, (oh_a if k < 2 else oh_b)[:, q, :], oh_tile[:, q, k % 2 * HALF:(k % 2 + 1) * HALF],
                                    start=False, stop=False)
                    last.then_inc(s_mm[q], 1)
            for k in range(4):
                last = onto(k, zeros16[:, 0:P], zeros16[:, :], start=False, stop=True)
            last.then_inc(s_slots, 1)
            pe.wait_ge(s_table, 1)
            def turn_pack(i, r):
                pe.wait_ge(s_pack[r], i + 1)
                pe.wait_ge(s_packt[r], i)
                for k in range(2):
                    last = pe.transpose(ps[:, 4 + r, k * P // 2:(k + 1) * P // 2].bitcast(BF16),
                                        pack[:, r, 4 * k:4 * k + 4, :].rearrange("p t n -> p (t n)"), ident_b[:, :])
                last.then_inc(s_packp[r], 1)

            turn_pack(0, 0)
            with pe.Fori(0, GROUPS // R) as i:
                for r in range(R):
                    pe.wait_ge(s_packt[r], i + 1)
                    for q in range(G // 2):
                        w = q % 2
                        if q == G // 2 - 1:
                            turn_pack(i + (r + 1) // R, (r + 1) % R)
                        pe.wait_ge(s_plfree[w], (i * R + r) * 2 + q // 2)
                        for t in (2 * q, 2 * q + 1):
                            lo = 32 * (t % 4)
                            moving = pack_t[lo:lo + 32, r, t // 4, :]
                            plane = ps[:, 2 * w + t % 2, :].rearrange("p (h n) -> p h n", h=H)
                            pe.matmul(plane, l_mask[lo:lo + 32, :], moving.rearrange("p (o n) -> p o n", o=1).to_broadcast([32, H, P]),
                                      start=True, stop=False, skip_group_check=True)
                            for h in range(H):
                                last = pe.matmul(plane[:, h, :], l_hr[lo:lo + 32, h, :], moving, start=False, stop=(h == H - 1),
                                                 skip_group_check=True)
                        last.then_inc(s_plane[w], 1)
            pe.wait_ge(s_tab, 1)
            pe.wait_ge(s_binld, 16)

            def turn_onehots(g, i, r):
                pe.wait_ge(s_onehot[r], i * 2 + 2)
                for k in range(2):
                    pe.wait_ge(s_oht, g * 2)
                    for t in range(4):
                        last = pe.transpose(ps[:, k, t * P:(t + 1) * P], onehot[:, r, 4 * k + t, :], ident[:, :])
                    last.then_inc(s_ohp, 1)

            def look_up(g, i, r, bins):
                pe.wait_ge(s_oht, g * 2 + 2)
                pe.wait_ge(s_terms[r], i)
                for q, b in enumerate(bins):
                    for t in (2 * q, 2 * q + 1):
                        at = r % 2 * 256 + t * 6 * H
                        last = pe.matmul(ps[:, 2 + r // 2, at:at + 6 * H], onehot_t[:, r, t, :],
                                         table[:, ds(b, 1), :, :].rearrange("p o v s -> p (o v s)"),
                                         start=True, stop=True, skip_group_check=True)
                last.then_inc(s_look[r], 1)

            def add_pair(g, i, r, q):
                pe.wait_ge(s_msg[r], i * (G // 2) + q + 1)
                if q < 3:
                    pe.wait_ge(s_acc[q], g)
                else:
                    pe.wait_ge(s_done[(r - 1) % R], i + int(r > 0))
                for t in (2 * q, 2 * q + 1):
                    last = pe.matmul(ps[:, 4 + q, 0:HW], onehot[:, r, t, :], rows[:, r, t, :], start=(t % 2 == 0), stop=(t % 2 == 1))
                last.then_inc(s_sum[q], 1)

            turn_onehots(0, 0, 0)
            look_up(0, 0, 0, bins_of(PE, 0))
            turn_onehots(1, 0, 1)
            with pe.Fori(0, GROUPS // R) as i:
                for r in range(R):
                    g = i * R + r
                    near, ni = (r + 1) % R, i + (r + 1) // R
                    bins = bins_of(PE, g + 1)
                    add_pair(g, i, r, 0)
                    add_pair(g, i, r, 1)
                    look_up(g + 1, ni, near, bins)
                    add_pair(g, i, r, 2)
                    add_pair(g, i, r, 3)
                    turn_onehots(g + 2, i + (r + 2) // R, (r + 2) % R)
            pe.wait_ge(s_fill, 6)
            def onto_mean(lhs, b, **flags):
                return pe.matmul(ps[0:1, 0, 0:D], lhs, x_sb[:, ds(b, 1), :].rearrange("p o d -> p (o d)"), skip_group_check=True, **flags)

            onto_mean(ones[:, 0:1], XB - 1, start=True, stop=False)
            with pe.Fori(0, BINS // (2 * BB)) as i:
                for u in range(2):
                    pe.wait_ge(s_u, i * 2 + u + 1)
                    for k in range(BB):
                        last = onto_mean(rstd_now[:, u, k:k + 1], (i * 2 + u) * BB + k, start=False, stop=False)
                    last.then_inc(s_umm[u], 1)
            pe.wait_ge(s_u, BINS // BB + 1)
            onto_mean(ones[:, 0:1], XB - 1, start=False, stop=True)
            pe.matmul(ps[0:1, 1, 0:1], nmr_sum[:, :], ones[:, 0:1], start=True, stop=True).then_inc(s_umm[0], 1)
            pe.wait_ge(s_mean, 1)
            for k in range(KD):
                last = pe.matmul(ps[:, 2, k:k + 1], mean_row[0:1, k * P:(k + 1) * P], ones[0:1, 0:1], start=True, stop=True)
            last.then_inc(s_meanp, 1)
            pe.wait_ge(s_meanc, 1)
            pe.wait_ge(s_small, 16 * LD_SMALL)
            for k in range(KD):
                last = pe.matmul(ps[0:1, 3, 0:NX], mean_col[:, k:k + 1], wr_sb[:, k, :], start=(k == 0), stop=(k == KD - 1))
            last.then_inc(s_logit, 1)
            pe.wait_ge(s_choice, 1)
            pe.matmul(ps[:, 4, 0:2], ones[0:1, :], small[0:1, 12:14], start=True, stop=True).then_inc(s_wb, 1)
            def transposes(c, u, n):
                pe.wait_ge(s_ub, c * CB + n)
                pe.wait_ge(s_ut, c * KD)
                for b in range(n):
                    for k in range(KD):
                        last = pe.transpose(ps[:, k, b * P:(b + 1) * P], u_rows[:, u, b, k * P:(k + 1) * P], ident[:, :])
                last.then_inc(s_utp, 1)

            def first_product(c, n):
                pe.wait_ge(s_ut, (c + 1) * KD)
                for f in range(8):
                    pe.wait_ge(s_act, c * 8 + (f - 1 if f else 0)) if f else None
                    for k in range(KD):
                        last = pe.matmul(ps[:, 2 + f % 2, 0:n * P], w1_sb[:, f // 4, k, f % 4 * P:(f % 4 + 1) * P],
                                         u_t[:, k, 0:n * P], start=(k == 0), stop=(k == KD - 1))
                    last.then_inc(s_m1, 1)

            def second_product(c, u, n):
                pe.wait_ge(s_act, (c + 1) * 8)
                pe.wait_ge(s_y, c)
                for b in range(n):
                    for f in range(8):
                        last = pe.matmul(ps[:, 4 + b, 0:D], act_t[:, u, f, b * P:(b + 1) * P], w2_sb[:, f // 4, f % 4, :],
                                         start=(f == 0), stop=(f == 7))
                    last.then_inc(s_m2, 1)

            transposes(0, 0, CB)
            pe.wait_ge(s_expw, 1)
            with pe.Fori(0, FULL // 2) as i:
                for u in range(2):
                    c = i * 2 + u
                    first_product(c, CB)
                    transposes(c + 1, 1 - u, CB)
                    second_product(c, u, CB)
            first_product(FULL, 1)
            second_product(FULL, 0, 1)

        @block.vector
        def _(dve):
            own = Count(s_dve)

            def link(instruction):
                own.add(instruction)
                dve.wait_ge(s_dve, own.value)

            dve.memset(src_i, (1 << 13) - 1).then_inc(s_fill, 1)
            dve.memset(dst_i, 0).then_inc(s_fill, 1)
            dve.memset(x_sb[:, NB - 1:XB, :], 0.0).then_inc(s_fill, 1)
            dve.memset(count, 0.0).then_inc(s_fill, 1)
            dve.memset(zeros16[:, :], 0.0).then_inc(s_fill, 1)
            dve.memset(slot_d[:, :], 0).then_inc(s_zero, 1)
            dve.wait_ge(s_fill, 5)
            dve.wait_ge(s_edges, 16 * LD_EDGES)
            dve.wait_ge(s_const, N_CONST)
            link(dve.tensor_scalar(work_i, src_i, 7, None, ALU.logical_shift_right))
            link(dve.tensor_copy(bin_16, work_i))
            link(dve.tensor_scalar(work_i, dst_i, SHIFT, 8, ALU.logical_shift_right, ALU.logical_shift_left))
            link(dve.tensor_scalar(src_i, src_i, P - 1, None, ALU.bitwise_and))
            link(dve.scalar_tensor_tensor(out=code_a, in0=src_i, scalar=1.0, in1=work_i, op0=ALU.add, op1=ALU.add))
            link(dve.scalar_tensor_tensor(out=code_c, in0=dst_i, scalar=256.0, in1=src_i, op0=ALU.mult, op1=ALU.add))
            link(dve.tensor_scalar(code_c, code_c, 1.0, None, ALU.add))
            link(dve.tensor_scalar(dst_i, dst_i, LOW, None, ALU.bitwise_and))
            link(dve.tensor_copy(code_b, dst_i))
            U = BINS // 5
            with dve.Fori(0, 5) as i:
                for k in range(U):
                    b = i * U + k
                    dve.wait_ge(s_cnt, b)
                    dve.tensor_scalar(rank[:, 0, :], bin_16, iota_b[:, ds(b, 1)], 0.0, ALU.is_equal, ALU.add,
                                      accum_out=count[:, ds(b, 1)]).then_inc(s_cnt, 1)
            dve.wait_ge(s_base, 1)
            link(dve.tensor_scalar(bin_i, ps[:, 5, 0:BINS], float(2 * P - 1), None, ALU.add))
            link(dve.tensor_scalar(bin_i, bin_i, 8, None, ALU.logical_shift_right))
            link(dve.tensor_copy(total, bin_i))
            link(dve.tensor_tensor_scan(ends, total, total, 0.0, ALU.add, ALU.max))
            link(dve.tensor_tensor(total, ends, total, ALU.subtract))
            link(dve.tensor_copy(pairs_to[:, :], ends[0:1, :]))
            link(dve.scalar_tensor_tensor(out=base, in0=total, scalar=float(2 * P), in1=ps[:, 4, 0:BINS], op0=ALU.mult, op1=ALU.add))
            link(dve.tensor_tensor(bin_cmp, iota_pair[:, :].rearrange("p (q o) -> p q o", o=1).to_broadcast([P, G // 2, NB]),
                                   ends[:, 0:NB].rearrange("p (o b) -> p o b", o=1).to_broadcast([P, G // 2, NB]), ALU.is_ge))
            link(dve.tensor_reduce(bin_of, bin_cmp, X, ALU.add))
            dve.tensor_copy(bin_of_i, bin_of).then_inc(s_bins, 1)
            own.add(dve.memset(mv[:, :, :], 0.0))
            dve.wait_ge(s_x, 16 * LD_X)

            def moments(i):
                dve.sem_inc(s_go, 1)
                for u in range(BB):
                    own.add(dve.bn_stats(stats[:, u, :], row_of(i * BB + u)))
                dve.wait_ge(s_dve, own.value)
                dve.sem_inc(s_go, 1)
                for u in range(BB):
                    own.add(dve.bn_aggr(mv_one[:, u, :], stats[:, u, :]))
                dve.wait_ge(s_dve, own.value)
                link(dve.tensor_scalar(mv[:, ds(i * BB, BB), :], mv_one[:, :, :], 0.0, None, ALU.add))

            def row_of(b):
                return x_sb[:, ds(b, 1), :].rearrange("p o d -> p (o d)")

            start = own.value
            with dve.Fori(0, BINS // BB) as i:
                own.value = i * (2 * BB + 1) + start
                moments(i)
            own.value = start + BINS // BB * (2 * BB + 1)
            ve = tmp_a[:, :, 0]
            sq = tmp_a[:, :, 1]

            def inverse_std(n_std, s_out):
                link(dve.tensor_scalar(ve, mv[:, :, 1], EPS, None, ALU.add))
                dve.tensor_copy(rstd[:, :], ve).then_inc(s_out, 1)
                dve.wait_ge(s_std, n_std)
                link(dve.reciprocal(nmr[:, :], rstd[:, :]))
                link(dve.tensor_tensor(sq, nmr[:, :], nmr[:, :], ALU.mult))
                link(dve.tensor_tensor(sq, sq, ve, ALU.mult))
                link(dve.tensor_scalar(sq, sq, -0.5, 1.5, ALU.mult, ALU.add))
                link(dve.tensor_tensor(rstd[:, :], nmr[:, :], sq, ALU.mult))
                link(dve.scalar_tensor_tensor(out=nmr[:, :], in0=mv[:, :, 0], scalar=-1.0, in1=rstd[:, :], op0=ALU.mult, op1=ALU.mult))

            inverse_std(1, s_var)
            dve.sem_inc(s_norm, 1)
            dve.wait_ge(s_w, 16 * LD_W)
            prod = tmp_b[:, 0:2 * P // (2 * H), :].rearrange("p a b -> p (a b)")
            for k in range(KD):
                for a, at in ((ar_bc, HD), (al_bc, HW)):
                    link(dve.tensor_tensor(prod, wx[:, k, 0:HD], a[:, :], ALU.mult))
                    link(dve.tensor_reduce(wx[:, k, at:at + H], prod.rearrange("p (h f) -> p h f", h=H), X, ALU.add))
            dve.sem_inc(s_norm, 1)
            link(dve.memset(pos, 0.0))
            link(dve.tensor_scalar(mask[:, 0, :], bin_16, iota_b[:, 0:1], None, ALU.is_equal))
            start = own.value
            with dve.Fori(0, 5) as i:
                own.value = i * (3 * U) + start
                for k in range(U):
                    b = i * U + k
                    w = k % 2
                    link(dve.tensor_tensor_scan(rank[:, w, :], mask[:, w, :], mask[:, w, :], base[:, ds(b, 1)], ALU.add, ALU.max))
                    own.add(dve.tensor_scalar(mask[:, 1 - w, :], bin_16, iota_b[:, ds(b + 1, 1)], None, ALU.is_equal))
                    link(dve.copy_predicated(pos, mask[:, w, :], rank[:, w, :]))
            own.value = start + 3 * U * 5
            link(dve.tensor_scalar(dst_i, pos, float(P - 1), None, ALU.add))
            link(dve.tensor_scalar(work_i, dst_i, 7, None, ALU.logical_shift_right))
            link(dve.tensor_copy(tile_of, work_i))
            link(dve.tensor_scalar(work_i, dst_i, P - 1, None, ALU.bitwise_and))
            link(dve.tensor_copy(place_of, work_i))
            link(dve.scalar_tensor_tensor(out=linear, in0=place_of, scalar=float(TILES), in1=tile_of, op0=ALU.mult, op1=ALU.add))
            dve.sem_inc(s_linear, 1)
            with dve.Fori(0, (ECP - EC_POOL) // UT) as i:
                for t in range(UT):
                    q = t % ONEHOTS
                    j = i * UT + t + EC_POOL
                    dve.wait_ge(s_mm[q], i * (UT // ONEHOTS) + t // ONEHOTS)
                    dve.tensor_scalar(oh_a[:, q, :], iota_p16[:, :], place_of[:, ds(j, 1)], code_a[:, ds(j, 1)],
                                      ALU.is_equal, ALU.mult).then_inc(s_oh, 1)
                    dve.tensor_scalar(oh_b[:, q, :], iota_p16[:, :], place_of[:, ds(j, 1)], code_b[:, ds(j, 1)],
                                      ALU.is_equal, ALU.mult).then_inc(s_oh, 1)
                    dve.tensor_scalar(oh_tile[:, q, :], iota_t16[:, :], tile_of[:, ds(j, 1)], None, ALU.is_equal).then_inc(s_oh, 1)
            own.add(dve.memset(slot_s[:, :], 0.0))
            link(dve.memset(slot_r[:, :, :], 0.0))
            dve.wait_ge(s_slots, 1)

            def halves(v):
                return v.rearrange("p (k n) -> p k n", k=2)

            own.add(dve.tensor_copy(halves(slot_a), ps[:, 0:2, 0:HALF]))
            link(dve.tensor_copy(halves(slot_b), ps[:, 2:4, 0:HALF]))
            link(dve.tensor_scalar(slot_d[:, 0:TILES], slot_a, 8, SHIFT, ALU.logical_shift_right, ALU.logical_shift_left))
            link(dve.tensor_tensor(slot_d[:, 0:TILES], slot_d[:, 0:TILES], slot_b, ALU.bitwise_or))
            dve.wait_ge(s_slotld, 16)
            link(dve.tensor_scalar(slot_b, slot_c, 8, None, ALU.logical_shift_right))
            link(dve.tensor_tensor(slot_d[:, 0:TILES], slot_d[:, 0:TILES], slot_b, ALU.bitwise_or))
            link(dve.tensor_tensor(slot_a, slot_a, slot_c, ALU.bitwise_or))
            link(dve.tensor_scalar(slot_a, slot_a, 255, None, ALU.bitwise_and))
            link(dve.tensor_copy(slot_s[:, 0:TILES], slot_a))
            link(dve.tensor_tensor(slot_t, slot_s[:, 0:TILES], slot_s[:, 0:TILES], ALU.mult))
            link(dve.tensor_copy(slot_a, slot_t))
            link(dve.tensor_scalar(slot_b, slot_a, P - 1, None, ALU.bitwise_and))
            own.add(dve.memset(slot_r[:, :, 0:2], 1.0))
            own.add(dve.tensor_copy(slot_r[:, 0:TILES, 2], slot_s[:, 0:TILES]))
            own.add(dve.tensor_copy(slot_r[:, 0:TILES, 4], slot_b))
            link(dve.tensor_tensor(slot_r[:, 0:TILES, 3], slot_t, slot_b, ALU.subtract))
            link(dve.tensor_scalar(part_i[:, :], part_i[:, :], 31, None, ALU.bitwise_and))
            link(dve.tensor_copy(part_k[:, :], part_i[:, :]))
            for k, value in enumerate((-NEG, -NEG, 2 * NEG, -NEG, -NEG)):
                link(dve.tensor_scalar(coef[:, k:k + 1], part_k[:, :], float(k), value, ALU.is_equal, ALU.mult))
            link(dve.tensor_tensor(coef[:, 3:4], coef[:, 3:4], coef[:, 4:5], ALU.add))
            sq_n, lo_n, lo_i = slot_t[:, 0:P], slot_t[:, P:2 * P], slot_a[:, 0:P]
            link(dve.tensor_tensor(sq_n, iota_1[:, :], iota_1[:, :], ALU.mult))
            link(dve.tensor_copy(lo_i, sq_n))
            link(dve.tensor_scalar(lo_i, lo_i, P - 1, None, ALU.bitwise_and))
            link(dve.tensor_copy(lo_n, lo_i))
            link(dve.tensor_tensor(sq_n, sq_n, lo_n, ALU.subtract))
            link(dve.tensor_scalar(sq_n, sq_n, coef[:, 0:1], coef[:, 3:4], ALU.mult, ALU.add))
            link(dve.scalar_tensor_tensor(out=sq_n, in0=lo_n, scalar=coef[:, 1:2], in1=sq_n, op0=ALU.mult, op1=ALU.add))
            link(dve.scalar_tensor_tensor(out=l_mask[:, :], in0=iota_1[:, :], scalar=coef[:, 2:3], in1=sq_n, op0=ALU.mult, op1=ALU.add))
            for h in range(H):
                link(dve.tensor_scalar(coef[:, 5:6], part_k[:, :], float(5 + 3 * h), None, ALU.is_ge))
                link(dve.tensor_scalar(coef[:, 6:7], part_k[:, :], float(7 + 3 * h), None, ALU.is_le))
                link(dve.tensor_tensor(coef[:, 7:8], coef[:, 5:6], coef[:, 6:7], ALU.mult))
                link(dve.tensor_scalar(l_hr[:, h, :], ones[:, :], coef[:, 7:8], None, ALU.mult))
            link(dve.tensor_copy(ident_b[:, :], ident[:, :]))
            own.add(dve.memset(top[:, :, :], -1e30))
            own.add(dve.memset(run_before[:, :, :], -1e30))
            own.add(dve.memset(new_bin, 0.0))
            link(dve.memset(pack, 0.0))
            dve.sem_inc(s_table, 1)

            def split(out, value, a, b):
                link(dve.tensor_copy(out[..., 0], value))
                link(dve.tensor_tensor(a, value, out[..., 0], ALU.subtract))
                link(dve.tensor_copy(out[..., 1], a))
                link(dve.tensor_tensor(b, a, out[..., 1], ALU.subtract))
                return dve.tensor_copy(out[..., 2], b)

            dve.wait_ge(s_binld, 16)

            def pack_rows(g, i, r):
                dve.wait_ge(s_packp[r], i)
                own.add(dve.tensor_copy(pack[:, r, :, 0:5], slot_r[:, ds(g * G, G), :]))
                dve.wait_ge(s_gat[r], (i + 1) * 16 * G)
                last = split(pack[:, r, :, 5:5 + 3 * H].rearrange("p t (h s) -> p t h s", s=3), hr_rows[:, r, :, :], res_a, res_b)
                last.then_inc(s_pack[r], 1)

            pack_rows(0, 0, 0)
            start = own.value
            per_group = 5
            with dve.Fori(0, GROUPS // R) as i:
                own.value = i * (per_group * R + 1) + start
                own.add(dve.tensor_scalar(arena_a[:, ds(i * ACC_PART, ACC_PART)], iota_t16[:, 0:ACC_PART], 0.0, None, ALU.mult))
                for r in range(R):
                    g = i * R + r
                    for q in range(G // 2):
                        w = q % 2
                        if q == 1:
                            pack_rows(g + 1, i + (r + 1) // R, (r + 1) % R)
                        dve.wait_ge(s_plane[w], g * 2 + q // 2 + 1)
                        dve.tensor_reduce(pair_top[:, :, ds(g * (G // 2) + q, 1)].rearrange("p h o -> p (h o)"),
                                          ps[:, 2 * w:2 * w + 2, :].rearrange("p t (h n) -> p h t n", h=H),
                                          XY, ALU.max).then_inc(s_plfree[w], 1)
            own.value = start + per_group * GROUPS + GROUPS // R
            for w in range(2):
                dve.wait_ge(s_plfree[w], NPAIRS // 2)
            dve.wait_ge(s_binall, 16)
            link(dve.tensor_tensor(new_bin[:, 1:NPAIRS], bins_all[:, 1:NPAIRS], bins_all[:, 0:NPAIRS - 1], ALU.not_equal))
            link(dve.tensor_scalar(new_bin, new_bin, -1e30, None, ALU.mult))
            for h in range(H):
                own.add(dve.tensor_tensor_scan(run_top[:, h, :], new_bin, pair_top[:, h, :], -1e30, ALU.add, ALU.max))
            dve.wait_ge(s_dve, own.value)
            start = own.value
            with dve.Fori(0, BINS // BB) as i:
                _, last_pairs = nc.values_load_multi_w_load_instructions(
                    pairs_to[0:1, ds(i * BB, BB)], engines=[DVE], min_val=0, max_val=NPAIRS,
                    skip_runtime_bounds_check_because="all bins' pairs together are at most NPAIRS")
                for k, last_pair in enumerate(last_pairs):
                    dve.tensor_scalar(top[:, ds(i * BB + k, 1), :].rearrange("p o h -> p (o h)"),
                                      run_before[:, :, ds(last_pair, 1)].rearrange("p h o -> p (h o)"), 0.0, None, ALU.add).then_inc(s_dve, 1)
            own.value = start + BINS
            dve.wait_ge(s_dve, own.value)
            dve.wait_ge(s_hcopy, 3 * BINS)
            link(dve.tensor_tensor(tmp_a[:, 0:BINS, 0:H], hl[:, :, :], top[:, :, :], ALU.add))
            link(dve.scalar_tensor_tensor(out=tmp_b[:, 0:BINS, H:2 * H], in0=tmp_a[:, 0:BINS, 0:H], scalar=SLOPE, in1=tmp_a[:, 0:BINS, 0:H], op0=ALU.mult, op1=ALU.max))
            link(dve.tensor_copy(tmp_b[:, 0:BINS, 0:H], hl[:, :, :]))
            link(split(table, tmp_b[:, 0:BINS, :], tmp_a[:, 0:BINS, :], tmp_a[:, 0:BINS, :]))
            dve.sem_inc(s_tab, 1)

            def one_hots(g, r, k):
                tiles = slot_s[:, ds(g * G + 4 * k, 4)].rearrange("p (t o) -> p t o", o=1).to_broadcast([P, 4, P])
                nodes = iota_1[:, :].rearrange("p (o n) -> p o n", o=1).to_broadcast([P, 4, P])
                dve.tensor_tensor(onehot[:, r, 4 * k:4 * k + 4, :], nodes, tiles, ALU.is_equal).then_inc(s_onehot[r], 1)

            def scores(i, r):
                dve.wait_ge(s_look[r], i + 1)
                at = r % 2 * 256
                dve.tensor_reduce(terms[:, r, :, :], ps[:, 2 + r // 2, at:at + 6 * H * G].rearrange("p (t v s) -> p t v s", t=G, s=3),
                                  X, ALU.add).then_inc(s_terms[r], 1)
                dve.wait_ge(s_terms[r], i + 1)
                dve.wait_ge(s_gatb[r], (i + 1) * 16 * G)
                z, m = terms[:, r, :, 0:H], terms[:, r, :, H:2 * H]
                link(dve.tensor_tensor(z, z, rows[:, r, :, HD:HW], ALU.add))
                link(dve.scalar_tensor_tensor(out=z, in0=z, scalar=SLOPE, in1=z, op0=ALU.mult, op1=ALU.max))
                link(dve.tensor_tensor(z, z, m, ALU.subtract))
                dve.tensor_scalar(z, z, 0.0, None, ALU.min).then_inc(s_arg[r], 1)

            for r in range(2):
                for k in range(2):
                    one_hots(r, r, k)
            scores(0, 0)
            start = own.value
            per_group = 3
            with dve.Fori(0, GROUPS // R) as i:
                own.value = i * (per_group * R) + start
                for r in range(R):
                    g = i * R + r
                    far = (r + 2) % R
                    bins = bins_of(DVE, g)

                    def weigh(q):
                        v = rows[:, r, 2 * q:2 * q + 2, 0:HD].rearrange("p t (h f) -> p t h f", h=H)
                        w = rows[:, r, 2 * q:2 * q + 2, HD:HW].rearrange("p t (h o) -> p t h o", o=1)
                        dve.tensor_tensor(v, v, w.to_broadcast([P, 2, H, FH]), ALU.mult).then_inc(s_msg[r], 1)

                    def add_up(q):
                        dve.wait_ge(s_sum[q], g + 1)
                        where = acc[:, ds(bins[q], 1), :].rearrange("p o n -> p (o n)")
                        ins = dve.tensor_tensor(where, where, ps[:, 4 + q, 0:HW], ALU.add)
                        if q < 3:
                            ins.then_inc(s_acc[q], 1)
                            dve.wait_ge(s_acc[q], g + 1)
                        else:
                            ins.then_inc(s_done[r], 1)
                            dve.wait_ge(s_done[r], i + 1)

                    dve.wait_ge(s_wgt[r], i + 1)
                    weigh(0)
                    weigh(1)
                    dve.wait_ge(s_done[far], i + int(r > 0))
                    one_hots(g + 2, far, 0)
                    weigh(2)
                    weigh(3)
                    add_up(0)
                    one_hots(g + 2, far, 1)
                    add_up(1)
                    scores(i + (r + 1) // R, (r + 1) % R)
                    add_up(2)
                    add_up(3)
            own.value = start + per_group * GROUPS
            den = tmp_b[:, 0:BINS, 0:H]
            link(dve.tensor_scalar(den, acc[:, :, HD:HW], 1e-16, None, ALU.max))
            link(dve.reciprocal(den, den))
            start = own.value
            with dve.Fori(0, BINS // BB) as i:
                own.value = i * (2 * BB + 3) + start
                v = acc[:, ds(i * BB, BB), 0:HD].rearrange("p b (h f) -> p b h f", h=H)
                w = tmp_b[:, ds(i * BB, BB), 0:H].rearrange("p b (h o) -> p b h o", o=1)
                link(dve.tensor_tensor(v, v, w.to_broadcast([P, BB, H, FH]), ALU.mult))
                batch = x_sb[:, ds(i * BB, BB), :]
                link(dve.tensor_tensor(batch, batch, acc[:, ds(i * BB, BB), 0:HD], ALU.add))
                moments(i)
            own.value = start + BINS // BB * (2 * BB + 3)
            inverse_std(2, s_x1)
            link(dve.memset(half_col[:, :], -0.5))
            dve.sem_inc(s_fill, 1)
            with dve.Fori(0, BINS // (2 * BB)) as i:
                for u in range(2):
                    dve.wait_ge(s_umm[u], i)
                    dve.tensor_scalar(rstd_now[:, u, :], rstd[:, ds((i * 2 + u) * BB, BB)], 0.0, None, ALU.add).then_inc(s_u, 1)
            dve.tensor_reduce(nmr_sum[:, :], nmr[:, 0:BINS], X, ALU.add).then_inc(s_u, 1)
            dve.wait_ge(s_umm[0], BINS // (2 * BB) + 1)
            link(dve.tensor_copy(small[0:1, 20:21], ps[0:1, 1, 0:1]))
            dve.tensor_scalar(mean_row[:, :], ps[0:1, 0, 0:D], small[0:1, 20:21], 1.0 / TOKENS, ALU.add, ALU.mult).then_inc(s_mean, 1)
            dve.wait_ge(s_meanp, 1)
            dve.tensor_copy(mean_col[:, :], ps[:, 2, 0:KD]).then_inc(s_meanc, 1)
            dve.wait_ge(s_logit, 1)
            dve.wait_ge(s_small, 16 * LD_SMALL)

            def row(k):
                return logit[0:1, k * NX:(k + 1) * NX]

            def one(k):
                return small[0:1, k:k + 1]

            link(dve.tensor_tensor(row(0), ps[0:1, 3, 0:NX], br_row[:, :], ALU.add))
            link(dve.tensor_reduce(one(0), row(0), X, ALU.max))
            dve.tensor_scalar(row(1), row(0), one(0), None, ALU.subtract).then_inc(s_rt, 1)
            dve.wait_ge(s_rte, 1)
            link(dve.tensor_reduce(one(1), row(1), X, ALU.add))
            link(dve.reciprocal(one(2), one(1)))
            link(dve.tensor_scalar(row(2), row(1), one(2), None, ALU.mult))
            link(dve.tensor_scalar(row(4), row(2), float(TOKENS), None, ALU.mult))
            link(dve.reciprocal(row(5), row(4)))
            link(dve.tensor_scalar(row(5), row(5), CAPACITY, 1.0, ALU.mult, ALU.min))
            link(dve.tensor_tensor(row(6), row(2), row(5), ALU.mult))
            link(dve.tensor_reduce(one(3), row(6), X, ALU.max))
            dve.tensor_scalar(row(3), row(6), one(3), None, ALU.subtract).then_inc(s_rt, 1)
            dve.wait_ge(s_rte, 2)
            link(dve.tensor_reduce(one(4), row(3), X, ALU.add))
            link(dve.reciprocal(one(5), one(4)))
            link(dve.tensor_scalar(row(7), row(3), one(5), None, ALU.mult))
            for k in range(2):
                link(dve.tensor_reduce(one(6 + k), row(7), X, ALU.max))
                link(dve.tensor_scalar(row(8), row(7), one(6 + k), float(-NX), ALU.is_equal, ALU.mult))
                link(dve.tensor_tensor(row(8), row(8), iota_b[0:1, 0:NX], ALU.add))
                link(dve.tensor_reduce(one(8 + k), row(8), X, ALU.min))
                link(dve.tensor_scalar(one(8 + k), one(8 + k), float(NX), None, ALU.add))
                link(dve.tensor_scalar(row(9), iota_b[0:1, 0:NX], one(8 + k), -4.0, ALU.is_equal, ALU.mult))
                link(dve.tensor_tensor(row(7), row(7), row(9), ALU.add))
            link(dve.tensor_copy(chosen[:, :], small[0:1, 8:10]))
            dve.tensor_tensor(one(10), one(7), one(6), ALU.subtract).then_inc(s_rt, 1)
            dve.wait_ge(s_rte, 3)
            link(dve.tensor_scalar(one(11), one(10), 1.0, None, ALU.add))
            link(dve.reciprocal(one(12), one(11)))
            link(dve.tensor_tensor(one(13), one(10), one(12), ALU.mult))
            dve.sem_inc(s_choice, 1)
            dve.wait_ge(s_wb, 1)
            link(dve.tensor_copy(top_w[:, :], ps[:, 4, 0:2]))
            dve.wait_ge(s_exp, 8 * 16)
            for k in range(2):
                v = w2_sb[:, k, :, :].rearrange("p k n -> p (k n)")
                link(dve.tensor_scalar(v, v, top_w[:, k:k + 1], None, ALU.mult))
                link(dve.tensor_scalar(b2_bc[:, k, :], b2_bc[:, k, :], top_w[:, k:k + 1], None, ALU.mult))
            link(dve.tensor_tensor(b2_bc[:, 0, :], b2_bc[:, 0, :], b2_bc[:, 1, :], ALU.add))
            dve.sem_inc(s_expw, 1)

            def rows_in(c, u, n):
                for b in range(n):
                    w = c * CB + b
                    dve.tensor_scalar(u_rows[:, u, b, :], row_of(w), rstd[:, ds(w, 1)], nmr[:, ds(w, 1)], ALU.mult, ALU.add).then_inc(s_ub, 1)

            def sums(c, u, n):
                for b in range(n):
                    v = y[:, u, b, :]
                    dve.wait_ge(s_m2, c * CB + b + 1)
                    link(dve.tensor_tensor(v, ps[:, 4 + b, 0:D], u_rows[:, u, b, :], ALU.add))
                    link(dve.tensor_tensor(v, v, b2_bc[:, 0, :], ALU.add))
                    link(dve.bn_stats(stats[:, b, :], v))
                    dve.sem_inc(s_go, 1)
                    link(dve.bn_aggr(mv2[:, u, b, :], stats[:, b, :]))
                dve.tensor_scalar(ve2[:, u, 0:n], mv2[:, u, 0:n, 1], EPS, None, ALU.add).then_inc(s_y, 1)

            def finish(c, u, n):
                dve.wait_ge(s_pow, c + 1)
                link(dve.tensor_tensor(t2[:, u, 0:n], r2[:, u, 0:n], r2[:, u, 0:n], ALU.mult))
                link(dve.tensor_tensor(t2[:, u, 0:n], t2[:, u, 0:n], ve2[:, u, 0:n], ALU.mult))
                link(dve.tensor_scalar(t2[:, u, 0:n], t2[:, u, 0:n], -0.5, 1.5, ALU.mult, ALU.add))
                link(dve.tensor_tensor(r2[:, u, 0:n], r2[:, u, 0:n], t2[:, u, 0:n], ALU.mult))
                for b in range(n):
                    v = y[:, u, b, :]
                    link(dve.tensor_scalar(v, v, mv2[:, u, b, 0:1], r2[:, u, b:b + 1], ALU.subtract, ALU.mult))
                    link(dve.tensor_tensor(v, v, gamma_bc[:, :], ALU.mult))
                    link(dve.tensor_tensor(v, v, beta_bc[:, :], ALU.add))
                    dve.tensor_tensor(v, v, row_of(c * CB + b), ALU.add).then_inc(s_out, 1)

            rows_in(0, 0, CB)
            start = own.value
            per_chunk = 4 * CB + 4 + 3 * CB
            with dve.Fori(0, FULL // 2) as i:
                own.value = i * (2 * per_chunk) + start
                for u in range(2):
                    c = i * 2 + u
                    rows_in(c + 1, 1 - u, CB)
                    dve.wait_ge(s_st[u], i * 16)
                    sums(c, u, CB)
                    finish(c, u, CB)
            own.value = start + FULL * per_chunk
            dve.wait_ge(s_st[0], FULL // 2 * 16)
            sums(FULL, 0, 1)
            finish(FULL, 0, 1)


_INS = ['x', 'src', 'dst', 'L0_gnn_W', 'L0_gnn_a_l', 'L0_gnn_a_r', 'L0_ffn_Wr', 'L0_ffn_br', 'L0_ffn_W1', 'L0_ffn_b1',
        'L0_ffn_W2', 'L0_ffn_b2', 'L0_ffn_gamma', 'L0_ffn_beta']


def kernel(**inputs):
    import numpy as _np
    import concourse.bacc as _bacc
    from concourse import mybir as _mybir
    from concourse.bass_utils import run_bass_kernel_spmd as _run

    nc = _bacc.Bacc("TRN2", target_bir_lowering=False, num_devices=1)
    arrays, args = {}, []
    for name in _INS:
        a = _np.ascontiguousarray(inputs[name])
        arrays[f"in_{name}_dram"] = a
        args.append(nc.dram_tensor(f"in_{name}_dram", a.shape, _mybir.dt.from_np(a.dtype), kind="ExternalInput").ap())
    shape = inputs["x"].shape
    args.append(nc.dram_tensor("out_0_dram", shape, _mybir.dt.float32, kind="ExternalOutput").ap())
    gat_moe_block(nc, *args)
    r = _run(nc, [arrays], core_ids=[0])
    return r.results[0]["out_0_dram"]
```

```python
from contextlib import ExitStack

import concourse.bass as bass
from concourse import mybir

P = 128
F32 = mybir.dt.float32
F16 = mybir.dt.float16
BF16 = mybir.dt.bfloat16
I32 = mybir.dt.int32
U32 = mybir.dt.uint32
U16 = mybir.dt.uint16
ALU = mybir.AluOpType
ACT = mybir.ActivationFunctionType
ACTIVATION = mybir.EngineType.Activation
DVE = mybir.EngineType.DVE
X = mybir.AxisListType.X
XY = mybir.AxisListType.XY
ds = bass.ds


class Count:

    def __init__(self, sem):
        self.sem, self.value = sem, 0

    def add(self, instruction):
        instruction.then_inc(self.sem, 1)
        self.value = self.value + 1


def gat_moe_block(nc, x, src, dst, gat_w, a_l, a_r, w_r, b_r, w_1, b_1, w_2, b_2, gamma, beta, out):
    N, D = x.shape
    E = src.shape[0]
    H, FH = a_l.shape[1], a_l.shape[2]
    NX, FF = w_1.shape[0], w_1.shape[2]
    HD = H * FH
    FW = FH + 1
    HW = H * FW
    SW = HW + 3 * H // 2
    KD = D // P
    NB = -(-N // P)
    TRASH = NB
    BINS = NB + 1 + (NB + 1) % 2
    LAST = N - (NB - 1) * P
    EC = -(-E // P)
    UT = 8
    ECP = -(-EC // UT) * UT
    E_LAST = E - (P - 1) * EC
    PAIRS = (E + NB * (2 * P - 1)) // (2 * P)
    G = 8
    R = 5
    AHEAD = 2
    GROUPS = -(-(-(-2 * PAIRS // G)) // R) * R
    TILES = GROUPS * G
    TPAD = TILES + R * G
    GF = GROUPS + AHEAD
    SC = 3
    EC_POOL = min(E_LAST, ECP * 3 // 7) // (SC * UT) * (SC * UT)
    NPAIRS = TILES // 2
    HALF = TILES // 2
    SHIFT = 11
    LOW = (1 << SHIFT) - 1
    NEG = float(2 ** 80)
    SLOPE = 0.2
    EPS = 1e-5
    TOKENS = N
    CAPACITY = float(-(-TOKENS * 5 // (4 * NX)))
    ROWS = BINS * P
    BB = 5
    CB = 4
    CN = CB * P
    FULL = (NB - 1) // CB
    XB = (FULL + 1) * CB
    assert HD == D == 2 * P and FF == 4 * P and TILES <= 2 * 512 and N < 4 << SHIFT and GF < P and R * G * SW + GF * 5 * H <= XB * D

    h_table = nc.dram_tensor("h_table", (ROWS, SW), F32, kind="Internal").ap()
    slot_table = nc.dram_tensor("slot_table", (P * TILES + 1, 1), I32, kind="Internal").ap()
    bin_table = nc.dram_tensor("bin_table", (P, G // 2), I32, kind="Internal").ap()

    with ExitStack() as ctx:
        def sb(name, shape, dt=F32):
            return ctx.enter_context(nc.sbuf_tensor(name, shape, dt))

        def sem(name):
            return ctx.enter_context(nc.semaphore(name))

        def sems(name, n):
            return [sem(f"{name}{k}") for k in range(n)]

        def carve(arena, sizes):
            at, views = 0, []
            for dt, shape in sizes:
                n = 1
                for k in shape:
                    n *= k
                words = n * mybir.dt.size(dt) // 4
                v = arena[:, at:at + words]
                if dt != F32:
                    v = v.bitcast(dt)
                if len(shape) == 2:
                    v = v.rearrange("p (a b) -> p a b", b=shape[1])
                elif len(shape) == 3:
                    v = v.rearrange("p (a b c) -> p a b c", b=shape[1], c=shape[2])
                elif len(shape) == 4:
                    v = v.rearrange("p (a b c d) -> p a b c d", b=shape[1], c=shape[2], d=shape[3])
                views.append(v)
                at += words
            return views

        x_sb = sb("x_sb", [P, XB, D])
        wx = sb("wx", [P, KD, HD + 2 * H])
        al_bc = sb("al_bc", [P, HD])
        ar_bc = sb("ar_bc", [P, HD])
        hl = sb("hl", [P, BINS, H])
        hr = sb("hr", [P, BINS, H])
        hr_words = sb("hr_words", [P, BINS, 3 * H // 2])
        hr_split = hr_words[:, :, :].rearrange("p b w -> p (b w)").bitcast(BF16).rearrange("p (b h s) -> p b h s", h=H, s=3)
        mv = sb("mv", [P, XB, 2])
        rstd = sb("rstd", [P, XB])
        nmr = sb("nmr", [P, XB])
        stats = sb("stats", [P, BB, 6])
        mv_one = sb("mv_one", [P, BB, 2])
        rstd_now = sb("rstd_now", [P, 2, BB])
        tmp_a = sb("tmp_a", [P, XB, 2 * H])
        tmp_b = sb("tmp_b", [P, XB, 2 * H])
        iota_1 = sb("iota_1", [P, P])
        iota_p16 = sb("iota_p16", [P, P], F16)
        iota_t16 = sb("iota_t16", [P, TILES], F16)
        iota_b = sb("iota_b", [P, BINS + 1])
        iota_pair = sb("iota_pair", [P, G // 2])
        part_i = sb("part_i", [P, 1], I32)
        part_k = sb("part_k", [P, 1])
        ident = sb("ident", [P, P])
        ident_b = sb("ident_b", [P, P], BF16)
        before = sb("before", [P, P])
        ones = sb("ones", [P, P])
        zeros16 = sb("zeros16", [P, HALF], F16)
        l_mask = sb("l_mask", [P, 4, P], BF16)
        l_hr = sb("l_hr", [P, 4, H, P], BF16)
        quarter = sb("quarter", [P, 4])
        coef = sb("coef", [P, 12])
        slot_s = sb("slot_s", [P, TPAD])
        slot_d = sb("slot_d", [P, TPAD], I32)
        slot_r = sb("slot_r", [P, TPAD, 5], BF16)
        bins_row = sb("bins_row", [1, P * G // 2], I32)
        small = sb("small", [1, 64])
        logit = sb("logit", [1, 16 * NX])
        chosen = sb("chosen", [1, 2], I32)
        mean_row = sb("mean_row", [1, D])
        mean_col = sb("mean_col", [P, KD])
        wr_sb = sb("wr_sb", [P, KD, NX])
        br_row = sb("br_row", [1, NX])
        top_w = sb("top_w", [P, 2])
        nmr_sum = sb("nmr_sum", [P, 1])

        arena_a = sb("arena_a", [P, BINS * HW])
        (src_i, dst_i, work_i, code_a, code_b, pos, tile_of, place_of, bin_16, mask, rank, code_c, linear) = carve(arena_a, [
            (I32, [ECP]), (I32, [ECP]), (I32, [ECP]), (F32, [ECP]), (F32, [ECP]), (F32, [ECP]), (F32, [ECP]),
            (F32, [ECP]), (F16, [ECP]), (U16, [2, ECP]), (F32, [2, ECP]), (F32, [ECP]), (F32, [ECP])])
        stage_at = sb("stage_at", [P, SC, UT], U32)
        stage_code = sb("stage_code", [P, SC, UT], I32)
        (acc,) = carve(arena_a, [(F32, [BINS, HW])])
        acc_h = acc.rearrange("p b (h f) -> p b h f", h=H)
        (act_t, u_t, u_rows) = carve(arena_a, [(F32, [2, 8, CN]), (F32, [KD, CN]), (F32, [2, CB, D])])
        arena_b = sb("arena_b", [P, 11700])
        ONEHOTS = 4
        (oh_tile, oh_a, oh_b) = carve(arena_b, [(F16, [ONEHOTS, TILES]), (F16, [ONEHOTS, P]), (F16, [ONEHOTS, P])])
        n0 = ONEHOTS * (TILES + 2 * P) // 2
        (xh, xh_t, h_out) = carve(arena_b[:, n0:], [(F32, [2, D]), (F32, [2, KD, P]), (F32, [2, HW])])
        n0 += 4 * D + 2 * HW
        (count, base, total, ends, bin_i) = carve(arena_b[:, n0:], [
            (F32, [BINS]), (F32, [BINS]), (F32, [BINS]), (F32, [BINS]), (I32, [BINS])])
        n0 += 5 * BINS
        (bin_cmp, bin_of, bin_of_i) = carve(arena_b[:, n0:], [(F32, [G // 2, NB]), (F32, [G // 2]), (I32, [G // 2])])
        n0 += G // 2 * NB + G
        (slot_a, slot_b, slot_t) = carve(arena_b[:, n0:], [(I32, [TILES]), (I32, [TILES]), (F32, [TILES])])
        n0 += 3 * TILES
        (slot_c, bins_all, new_bin) = carve(arena_b[:, n0:], [(I32, [TILES]), (I32, [GF * G // 2]), (F32, [GF * G // 2])])
        (onehot, onehot_t, pack, pack_t) = carve(arena_b, [
            (F32, [R, G, P]), (BF16, [R, G, P]), (BF16, [R, G, 32]), (BF16, [R, 2, P])])
        (rows, begins) = carve(x_sb[:, :, :].rearrange("p b d -> p (b d)"), [(F32, [R, G, SW]), (F32, [GF, H, 5])])
        idx = sb("idx", [P, R, G], U32)
        largest = sb("largest", [P, R, H, 5])
        running = sb("running", [P, R, H, 5])
        so_far = sb("so_far", [P, H, 4])
        so_far_m = sb("so_far_m", [P, 4, H])
        now_m = sb("now_m", [P, 4, H])
        look = sb("look", [P, R, 4, 2 * H])
        scale = sb("scale", [P, R, 4, H])
        look_split = sb("look_split", [P, R, 4, 2 * H, 3], BF16)
        look_rest = sb("look_rest", [P, 2, 4, 2 * H])
        zero_col = sb("zero_col", [P, 4, 2 * H])
        z = sb("z", [P, R, G, 2 * H])
        (w1_sb, w2_sb, y) = carve(arena_b, [(F32, [2, KD, FF]), (F32, [2, 4, D]), (F32, [2, CB, D])])
        b1_sb = sb("b1_sb", [P, 2, FF // P])
        b2_bc = sb("b2_bc", [P, 2, D])
        gamma_bc = sb("gamma_bc", [P, D])
        beta_bc = sb("beta_bc", [P, D])
        mv2 = sb("mv2", [P, 2, CB, 2])
        ve2 = sb("ve2", [P, 2, CB])
        r2 = sb("r2", [P, 2, CB])
        t2 = sb("t2", [P, 2, CB])
        half_col = sb("half_col", [P, CB])

        ps = ctx.enter_context(nc.psum_tensor("ps", [P, 8, 512], F32))

        s_const = sem("s_const")
        s_fill = sem("s_fill")
        s_edges = sem("s_edges")
        s_w = sem("s_w")
        s_x = sem("s_x")
        s_small = sem("s_small")
        s_dve = sem("s_dve")
        s_go = sem("s_go")
        s_std = sem("s_std")
        s_var = sem("s_var")
        s_norm = sem("s_norm")
        s_xh = sem("s_xh")
        s_xhp = sem("s_xhp")
        s_xht = sem("s_xht")
        s_h = sem("s_h")
        s_hcopy = sem("s_hcopy")
        s_hst = sems("s_hst", 2)
        s_hr3 = sem("s_hr3")
        s_hrst = sem("s_hrst")
        s_cnt = sem("s_cnt")
        s_base = sem("s_base")
        s_bins = sem("s_bins")
        s_binst = sem("s_binst")
        s_binld = sem("s_binld")
        s_binall = sem("s_binall")
        s_oh = sem("s_oh")
        s_mm = sems("s_mm", ONEHOTS)
        s_zero = sem("s_zero")
        s_zeroed = sem("s_zeroed")
        s_linear = sem("s_linear")
        s_stage = sems("s_stage", SC)
        s_scat = sems("s_scat", SC)
        s_slotld = sem("s_slotld")
        s_slots = sem("s_slots")
        s_table = sem("s_table")
        s_clear = sem("s_clear")
        s_target = sem("s_target")
        s_idx = sems("s_idx", R)
        s_turn = sem("s_turn")
        s_gat = sems("s_gat", R)
        s_pack = sem("s_pack")
        s_packp = sem("s_packp")
        s_packt = sem("s_packt")
        s_plane = sems("s_plane", 2)
        s_plfree = sems("s_plfree", 2)
        s_node = sem("s_node")
        s_scale = sem("s_scale")
        s_rescale = sem("s_rescale")
        s_hl = sem("s_hl")
        s_rest = sem("s_rest")
        s_split = sem("s_split")
        s_abs = sem("s_abs")
        s_onehot = sem("s_onehot")
        s_ohp = sem("s_ohp")
        s_oht = sem("s_oht")
        s_look = sem("s_look")
        s_found = sem("s_found")
        s_arg = sem("s_arg")
        s_wgt = sem("s_wgt")
        s_msg = sem("s_msg")
        s_sum = sems("s_sum", 2)
        s_add = sems("s_add", 2)
        s_passed = sem("s_passed")
        s_x2 = sems("s_x2", 2)
        s_den = sem("s_den")
        s_divided = sem("s_divided")
        s_x1 = sem("s_x1")
        s_u = sem("s_u")
        s_umm = sems("s_umm", 2)
        s_mean = sem("s_mean")
        s_meanp = sem("s_meanp")
        s_meanc = sem("s_meanc")
        s_logit = sem("s_logit")
        s_rt = sem("s_rt")
        s_rte = sem("s_rte")
        s_choice = sem("s_choice")
        s_wb = sem("s_wb")
        s_exp = sem("s_exp")
        s_expw = sem("s_expw")
        s_ub = sem("s_ub")
        s_utp = sem("s_utp")
        s_ut = sem("s_ut")
        s_m1 = sem("s_m1")
        s_act = sem("s_act")
        s_m2 = sem("s_m2")
        s_y = sem("s_y")
        s_pow = sem("s_pow")
        s_out = sem("s_out")
        s_st = sems("s_st", 2)

        PACK_AT = G * 6 * H
        assert PACK_AT + P <= 512
        LD_EDGES, LD_W, LD_X, LD_SMALL = 4, 4, 2, 4
        N_CONST = 10
        block = ctx.enter_context(nc.Block())

        def bins_of(engine, g):
            _, bins = nc.values_load_multi_w_load_instructions(
                bins_row[0:1, ds(g * (G // 2), G // 2)], engines=[engine], min_val=0, max_val=TRASH,
                skip_runtime_bounds_check_because="a pair's bin is a count of at most TRASH comparisons that hold")
            return bins

        def after(i, r, n):
            return i + (r + n) // R, (r + n) % R, i * R + r + n

        @block.sync
        def _(sp):
            sp.wait_ge(s_fill, 2)
            for a, v in ((src, src_i), (dst, dst_i)):
                body = a[0:(P - 1) * EC].rearrange("(p c) -> p c", c=EC)
                sp.dma_start(v[0:P - 1, 0:EC], body).then_inc(s_edges, 16)
                tail = a[(P - 1) * EC:E].rearrange("(p c) -> p c", p=1)
                sp.dma_start(v[P - 1:P, 0:E_LAST], tail).then_inc(s_edges, 16)
            sp.wait_ge(s_fill, 3)
            sp.dma_start(x_sb[:, 0:NB - 1, :], x[0:(NB - 1) * P, :].rearrange("(b p) d -> p b d", p=P)).then_inc(s_x, 16)
            sp.dma_start(x_sb[0:LAST, NB - 1, :], x[(NB - 1) * P:N, :]).then_inc(s_x, 16)
            for k in range(KD):
                sp.dma_start(wx[:, k, 0:HW].rearrange("p (h f) -> p h f", h=H)[:, :, 0:FH],
                             gat_w[k * P:(k + 1) * P, :].rearrange("p (h f) -> p h f", h=H)).then_inc(s_w, 16)
            for a, v in ((a_l, al_bc), (a_r, ar_bc)):
                sp.dma_start(v[:, :], a.rearrange("o h f -> o (h f)").to_broadcast([P, HD])).then_inc(s_w, 16)
            sp.dma_start(wr_sb[:, :, :], w_r.rearrange("(k p) n -> p k n", p=P)).then_inc(s_small, 16)
            sp.dma_start(br_row[:, :], b_r.rearrange("(o n) -> o n", o=1)).then_inc(s_small, 16)
            for a, v in ((gamma, gamma_bc), (beta, beta_bc)):
                sp.dma_start(v[:, :], a.rearrange("(o n) -> o n", o=1).to_broadcast([P, D])).then_inc(s_small, 16)
            sp.wait_ge(s_zero, 1)
            table_rows = slot_table[1:P * TILES + 1, :].rearrange("(p t) o -> p (t o)", p=P)
            sp.dma_start(table_rows, slot_d[:, 0:TILES]).then_inc(s_zeroed, 16)
            with sp.Fori(0, BINS // 2) as i:
                for u in range(2):
                    sp.wait_ge(s_hcopy, (i * 2 + u) * 3 + 3)
                    sp.dma_start(h_table[ds((i * 2 + u) * P, P), 0:HW], h_out[:, u, :]).then_inc(s_hst[u], 16)
            sp.wait_ge(s_bins, 1)
            sp.dma_start(bin_table, bin_of_i).then_inc(s_binst, 16)
            sp.wait_ge(s_binst, 16)
            sp.dma_start(bins_row[:, :], bin_table.rearrange("(o g) q -> o (g q)", o=1)).then_inc(s_binld, 16)
            sp.dma_start(bins_all, bin_table[0:GF, :].rearrange("(o g) q -> o (g q)", o=1).to_broadcast([P, GF * G // 2])).then_inc(s_binall, 16)
            for r in range(SC):
                sp.wait_ge(s_scat[r], EC_POOL // SC * 16)
            sp.dma_start(slot_c, table_rows).then_inc(s_slotld, 16)
            sp.wait_ge(s_hr3, 1)
            with nc.allow_non_contiguous_dma(reason="24 bytes a row, behind h"):
                sp.dma_start(h_table.rearrange("(b p) w -> p b w", p=P)[:, :, HW:SW],
                             hr_words[:, :, :]).then_inc(s_hrst, 16)
            sp.wait_ge(s_passed, 1)
            sp.dma_start(x_sb[:, 0:2 * BB, :], x[0:2 * BB * P, :].rearrange("(b p) d -> p b d", p=P)).then_inc(s_x2[0], 16)
            sp.dma_start(x_sb[:, 2 * BB:NB - 1, :], x[2 * BB * P:(NB - 1) * P, :].rearrange("(b p) d -> p b d", p=P)).then_inc(s_x2[1], 16)
            sp.dma_start(x_sb[0:LAST, NB - 1, :], x[(NB - 1) * P:N, :]).then_inc(s_x2[1], 16)
            sp.wait_ge(s_choice, 1)
            for k in range(2):
                e = sp.value_load(chosen[0:1, k:k + 1], min_val=0, max_val=NX - 1)
                sp.dma_start(w1_sb[:, k, :, :], w_1[ds(e, 1), :, :].rearrange("e (k p) f -> p (e k) f", p=P)).then_inc(s_exp, 16)
                sp.dma_start(w2_sb[:, k, :, :], w_2[ds(e, 1), :, :].rearrange("e (k p) f -> p (e k) f", p=P)).then_inc(s_exp, 16)
                with nc.allow_non_contiguous_dma(reason="512 biases, one a partition"):
                    sp.dma_start(b1_sb[:, k, :], b_1[ds(e, 1), :].rearrange("e (k p) -> p (e k)", p=P)).then_inc(s_exp, 16)
                sp.dma_start(b2_bc[:, k, :], b_2[ds(e, 1), :].to_broadcast([P, D])).then_inc(s_exp, 16)
            with sp.Fori(0, FULL // 2) as i:
                for u in range(2):
                    c = i * 2 + u
                    sp.wait_ge(s_out, (c + 1) * CB)
                    sp.dma_start(out[ds(c * CN, CN), :].rearrange("(b p) d -> p b d", p=P), y[:, u, :, :]).then_inc(s_st[u], 16)
            sp.wait_ge(s_out, FULL * CB + 1)
            sp.dma_start(out[(NB - 1) * P:N, :], y[0:LAST, 0, 0, :]).then_inc(s_st[0], 16)
            sp.wait_ge(s_st[0], 16 * (FULL // 2 + 1))
            sp.wait_ge(s_st[1], 16 * (FULL // 2))

        @block.gpsimd
        def _(pool):
            iota = dict(allow_small_or_imprecise_dtypes=True)
            pool.iota(iota_1[:, :], pattern=[[1, P]], base=1, channel_multiplier=0, **iota).then_inc(s_const, 1)
            pool.iota(iota_p16[:, :], pattern=[[1, P]], base=0, channel_multiplier=0, **iota).then_inc(s_const, 1)
            pool.iota(iota_t16[:, :], pattern=[[1, TILES]], base=1, channel_multiplier=0, **iota).then_inc(s_const, 1)
            pool.iota(iota_b[:, :], pattern=[[1, BINS + 1]], base=0, channel_multiplier=0, **iota).then_inc(s_const, 1)
            pool.iota(iota_pair[:, :], pattern=[[1, G // 2]], base=0, channel_multiplier=G // 2, **iota).then_inc(s_const, 1)
            pool.iota(part_i[:, :], pattern=[[1, 1]], base=0, channel_multiplier=1).then_inc(s_const, 1)
            pool.memset(ones[:, :], 1.0).then_inc(s_const, 1)
            pool.memset(ident[:, :], 0.0).then_inc(s_const, 1)
            pool.wait_ge(s_const, 8)
            pool.affine_select(out=ident[:, :], in_=ident[:, :], compare_op=ALU.not_equal, fill=1.0, base=0,
                               pattern=[[-1, P]], channel_multiplier=1).then_inc(s_const, 1)
            pool.affine_select(out=before[:, :], in_=ones[:, :], compare_op=ALU.is_gt, fill=0.0, base=0,
                               pattern=[[1, P]], channel_multiplier=-1).then_inc(s_const, 1)
            pool.wait_ge(s_zeroed, 16)
            with pool.Fori(0, EC_POOL // (SC * UT)) as i:
                for r in range(SC):
                    pool.wait_ge(s_stage[r], i + 1)
                    pool.sem_inc(s_turn, 1)
                    for t in range(UT):
                        pool.indirect_dma_start(out=slot_table, out_offset=bass.IndirectOffsetOnAxis(ap=stage_at[:, r, t:t + 1], axis=0),
                                                in_=stage_code[:, r, t:t + 1], in_offset=None).then_inc(s_scat[r], 16)
            pool.wait_ge(s_slots, 1)
            pool.memset(zero_col[:, :, :], 0.0)
            pool.memset(acc, 0.0).then_inc(s_clear, 1)
            pool.wait_ge(s_clear, 1)
            for u in range(2):
                pool.wait_ge(s_hst[u], 16 * (BINS // 2))
            pool.wait_ge(s_hrst, 16)

            def split_look(i, r, g):
                v, part = look[:, r, :, :], look_split[:, r, :, :, :]
                pool.wait_ge(s_node, g + 1)
                pool.tensor_tensor(part[:, :, :, 0], v, zero_col[:, :, :], ALU.add).then_inc(s_rest, 1)
                pool.wait_ge(s_rest, g * 4 + 1)
                pool.tensor_tensor(look_rest[:, 0, :, :], v, part[:, :, :, 0], ALU.subtract).then_inc(s_rest, 1)
                pool.wait_ge(s_rest, g * 4 + 2)
                pool.tensor_tensor(part[:, :, :, 1], look_rest[:, 0, :, :], zero_col[:, :, :], ALU.add).then_inc(s_rest, 1)
                pool.wait_ge(s_rest, g * 4 + 3)
                pool.tensor_tensor(look_rest[:, 1, :, :], look_rest[:, 0, :, :], part[:, :, :, 1], ALU.subtract).then_inc(s_rest, 1)
                pool.wait_ge(s_rest, g * 4 + 4)
                pool.tensor_tensor(part[:, :, :, 2], look_rest[:, 1, :, :], zero_col[:, :, :], ALU.add).then_inc(s_split, 1)

            def gather(i, r, g, first=False):
                pool.wait_ge(s_idx[r], i + 1)
                if not first:
                    pool.wait_ge(s_add[1], (g - R) * 2 + 2)
                pool.sem_inc(s_turn, 1)
                for t in range(G):
                    pool.indirect_dma_start(out=rows[:, r, t, :], out_offset=None, in_=h_table,
                                            in_offset=bass.IndirectOffsetOnAxis(ap=idx[:, r, t:t + 1], axis=0)
                                            ).then_inc(s_gat[r], 16)

            for r in range(R):
                gather(0, r, r, first=True)
            for r in range(AHEAD):
                split_look(0, r, r)
            with pool.Fori(0, GROUPS // R - 1) as i:
                for r in range(R):
                    split_look(*after(i, r, AHEAD))
                    gather(*after(i, r, R))
            for r in range(R):
                split_look(*after(GROUPS // R - 1, r, AHEAD))
                if r <= AHEAD:
                    gather(*after(GROUPS // R - 1, r, R))
            pool.wait_ge(s_den, 1)
            with pool.Fori(0, BINS // BB) as i:
                v = acc_h[:, ds(i * BB, BB), :, 0:FH]
                w = tmp_b[:, ds(i * BB, BB), 0:H].rearrange("p b (h o) -> p b h o", o=1)
                pool.tensor_tensor(v, v, w.to_broadcast([P, BB, H, FH]), ALU.mult).then_inc(s_divided, 1)
            def power(c, u, n):
                pool.wait_ge(s_y, c + 1)
                pool.tensor_tensor(r2[:, u, 0:n], ve2[:, u, 0:n], half_col[:, 0:n], ALU.pow).then_inc(s_pow, 1)
            with pool.Fori(0, FULL // 2) as i:
                for u in range(2):
                    power(i * 2 + u, u, CB)
            power(FULL, 0, 1)

        @block.scalar
        def _(act):
            act.wait_ge(s_var, 1)
            act.activation(rstd[:, :], rstd[:, :], ACT.Sqrt).then_inc(s_std, 1)
            act.wait_ge(s_norm, 1)

            def normalise(b, u):
                act.activation(xh[:, u, :], x_sb[:, ds(b, 1), :].rearrange("p o d -> p (o d)"), ACT.Identity,
                               scale=rstd[:, ds(b, 1)], bias=nmr[:, ds(b, 1)]).then_inc(s_xh, 1)

            normalise(0, 0)
            with act.Fori(0, BINS // 2) as i:
                for u in range(2):
                    b = i * 2 + u
                    act.wait_ge(s_xhp, b + 1)
                    act.activation(xh_t[:, u, :, :].rearrange("p k n -> p (k n)"), ps[:, 4 + u, 0:D], ACT.Copy).then_inc(s_xht, 1)
                    normalise(b + 1, 1 - u)
                    act.wait_ge(s_h, b + 1)
                    act.wait_ge(s_hst[u], i * 16)
                    act.activation(h_out[:, u, :], ps[:, 6 + u, 0:HW], ACT.Copy).then_inc(s_hcopy, 1)
                    act.activation(hr[:, ds(b, 1), :].rearrange("p o h -> p (o h)"),
                                   ps[:, 6 + u, 0:HW].rearrange("p (h f) -> p h f", h=H)[:, :, FH], ACT.Copy).then_inc(s_hcopy, 1)
                    act.activation(hl[:, ds(b, 1), :].rearrange("p o h -> p (o h)"), ps[:, 6 + u, HW:HW + H], ACT.Copy).then_inc(s_hcopy, 1)
            act.wait_ge(s_linear, 1)
            with act.Fori(0, EC_POOL // (SC * UT)) as i:
                for r in range(SC):
                    at = (i * SC + r) * UT
                    act.wait_ge(s_scat[r], i * 16 * UT)
                    act.activation(stage_at[:, r, :], linear[:, ds(at, UT)], ACT.Copy)
                    act.activation(stage_code[:, r, :], code_c[:, ds(at, UT)], ACT.Copy).then_inc(s_stage[r], 1)
            act.wait_ge(s_target, 1)

            def place_targets(i, r, g):
                act.activation(idx[:, r, :], slot_d[:, ds(g * G, G)], ACT.Copy).then_inc(s_idx[r], 1)

            def one_hots(i, r, g, k):
                for t in range(4 * k, 4 * k + 4):
                    act.activation(onehot[:, r, t, :], iota_1[:, :], ACT.Abs, scale=-1.0, bias=slot_s[:, ds(g * G + t, 1)]).then_inc(s_abs, 1)
                act.wait_ge(s_abs, g * G + 4 * k + 4)
                half = onehot[:, r, 4 * k:4 * k + 4, :].rearrange("p t n -> p (t n)")
                act.activation(half, half, ACT.Relu, scale=-1.0, bias=ones[:, 0:1]).then_inc(s_onehot, 1)

            def pairs_hl(i, r, g):
                for q, b in enumerate(bins_of(ACTIVATION, g)):
                    act.activation(look[:, r, q, 0:H], hl[:, ds(b, 1), :].rearrange("p o h -> p (o h)"), ACT.Copy).then_inc(s_hl, 1)

            def pack_rows(i, r, g):
                act.wait_ge(s_gat[r], (i + 1) * 16 * G)
                act.activation(pack[:, r, :, 0:5], slot_r[:, ds(g * G, G), :], ACT.Copy)
                act.activation(pack[:, r, :, 5:5 + 3 * H], rows[:, r, :, HW:SW].bitcast(BF16), ACT.Copy).then_inc(s_pack, 1)

            def copy_pack(i, r, g):
                act.wait_ge(s_packp, g + 1)
                act.activation(pack_t[:, r, :, :].rearrange("p k n -> p (k n)"), ps[:, 7, PACK_AT:PACK_AT + P].bitcast(BF16),
                               ACT.Copy).then_inc(s_packt, 1)

            def copy_onehots(i, r, g, k):
                act.wait_ge(s_ohp, g * 2 + k + 1)
                act.activation(onehot_t[:, r, 4 * k:4 * k + 4, :].rearrange("p k n -> p (k n)"), ps[:, 6, :], ACT.Copy).then_inc(s_oht, 1)

            def scales(i, r, g):
                act.wait_ge(s_node, g + 1)
                act.activation(scale[:, r, :, :], scale[:, r, :, :], ACT.Exp).then_inc(s_scale, 1)

            def rescale(i, r, g, q, b):
                act.wait_ge(s_scale, g + 1)
                if q == 0:
                    act.wait_ge(s_add[1], g * 2)
                else:
                    act.wait_ge(s_add[(q - 1) % 2], g * 2 + (q - 1) // 2 + 1)
                for h in range(H):
                    part = acc[:, ds(b, 1), h * FW:(h + 1) * FW].rearrange("p o n -> p (o n)")
                    last = act.activation(part, part, ACT.Identity, scale=scale[:, r, q, h:h + 1])
                last.then_inc(s_rescale, 1)

            def weights(i, r, g):
                act.wait_ge(s_arg, g + 1)
                act.activation(rows[:, r, :, 0:HW].rearrange("p t (h f) -> p t h f", h=H)[:, :, :, FH], z[:, r, :, 0:H],
                               ACT.Exp).then_inc(s_wgt, 1)

            for r in range(R):
                place_targets(0, r, r)
            act.wait_ge(s_table, 1)
            act.wait_ge(s_binld, 16)
            for r in range(AHEAD):
                pairs_hl(0, r, r)
            for r in range(AHEAD + 1):
                for k in range(2):
                    one_hots(0, r, r, k)
            for r in range(AHEAD + 1):
                pack_rows(0, r, r)
                copy_pack(0, r, r)
            for r in range(AHEAD):
                for k in range(2):
                    copy_onehots(0, r, r, k)
            scales(0, 0, 0)
            weights(0, 0, 0)
            act.wait_ge(s_clear, 1)
            with act.Fori(0, GROUPS // R) as i:
                for r in range(R):
                    now = after(i, r, 0)
                    bins = bins_of(ACTIVATION, now[2])
                    rescale(*now, 0, bins[0])
                    scales(*after(i, r, 1))
                    pairs_hl(*after(i, r, AHEAD))
                    place_targets(*after(i, r, R))
                    copy_onehots(*after(i, r, AHEAD), 0)
                    one_hots(*after(i, r, AHEAD + 1), 0)
                    pack_rows(*after(i, r, AHEAD + 1))
                    weights(*after(i, r, 1))
                    rescale(*now, 1, bins[1])
                    copy_onehots(*after(i, r, AHEAD), 1)
                    rescale(*now, 2, bins[2])
                    copy_pack(*after(i, r, AHEAD + 1))
                    rescale(*now, 3, bins[3])
                    one_hots(*after(i, r, AHEAD + 1), 1)
            act.wait_ge(s_x1, 1)
            act.activation(rstd[:, :], rstd[:, :], ACT.Sqrt).then_inc(s_std, 1)
            act.wait_ge(s_rt, 1)
            act.activation(logit[0:1, NX:2 * NX], logit[0:1, NX:2 * NX], ACT.Exp).then_inc(s_rte, 1)
            act.wait_ge(s_rt, 2)
            act.activation(logit[0:1, 3 * NX:4 * NX], logit[0:1, 3 * NX:4 * NX], ACT.Exp).then_inc(s_rte, 1)
            act.wait_ge(s_rt, 3)
            act.activation(small[0:1, 10:11], small[0:1, 10:11], ACT.Exp).then_inc(s_rte, 1)
            act.wait_ge(s_exp, 8 * 16)

            def transposes_out(c, n):
                act.wait_ge(s_utp, c + 1)
                act.wait_ge(s_m1, c * 8)
                for k in range(KD):
                    act.activation(u_t[:, k, 0:n * P], ps[:, k, 0:n * P], ACT.Copy).then_inc(s_ut, 1)

            def gelus(c, u, n):
                for f in range(8):
                    act.wait_ge(s_m1, c * 8 + f + 1)
                    act.activation(act_t[:, u, f, 0:n * P], ps[:, 2 + f % 2, 0:n * P], ACT.Gelu,
                                   bias=b1_sb[:, f // 4, f % 4:f % 4 + 1]).then_inc(s_act, 1)

            transposes_out(0, CB)
            with act.Fori(0, FULL // 2) as i:
                for u in range(2):
                    c = i * 2 + u
                    gelus(c, u, CB)
                    transposes_out(c + 1, CB)
            gelus(FULL, 0, 1)

        @block.tensor
        def _(pe):
            pe.wait_ge(s_const, N_CONST)
            pe.wait_ge(s_cnt, BINS)
            pe.matmul(ps[:, 4, 0:BINS], before[:, :], count, start=True, stop=True)
            pe.matmul(ps[:, 5, 0:BINS], ones[:, :], count, start=True, stop=True).then_inc(s_base, 1)
            pe.wait_ge(s_norm, 2)
            with pe.Fori(0, BINS // 2) as i:
                for u in range(2):
                    b = i * 2 + u
                    pe.wait_ge(s_xh, b + 1)
                    for k in range(KD):
                        last = pe.transpose(ps[:, 4 + u, k * P:(k + 1) * P], xh[:, u, k * P:(k + 1) * P], ident[:, :])
                    last.then_inc(s_xhp, 1)
                    pe.wait_ge(s_xht, b + 1)
                    pe.wait_ge(s_hcopy, i * 6)
                    for k in range(KD):
                        last = pe.matmul(ps[:, 6 + u, 0:HW + H], xh_t[:, u, k, :], wx[:, k, :], start=(k == 0), stop=(k == KD - 1))
                    last.then_inc(s_h, 1)
            def onto(k, lhs, rhs, **flags):
                return pe.matmul(ps[:, k, 0:HALF], lhs, rhs, skip_group_check=True, **flags)

            pe.wait_ge(s_fill, 5)
            for k in range(4):
                onto(k, zeros16[:, 0:P], zeros16[:, :], start=True, stop=False)
            with pe.Fori(0, (ECP - EC_POOL) // UT) as i:
                for t in range(UT):
                    q = t % ONEHOTS
                    pe.wait_ge(s_oh, (i * UT + t) * 3 + 3)
                    for k in range(4):
                        last = onto(k, (oh_a if k < 2 else oh_b)[:, q, :], oh_tile[:, q, k % 2 * HALF:(k % 2 + 1) * HALF],
                                    start=False, stop=False)
                    last.then_inc(s_mm[q], 1)
            for k in range(4):
                last = onto(k, zeros16[:, 0:P], zeros16[:, :], start=False, stop=True)
            last.then_inc(s_slots, 1)
            pe.wait_ge(s_table, 1)

            def turn_pack(i, r, g):
                pe.wait_ge(s_pack, g + 1)
                pe.wait_ge(s_packt, g)
                for k in range(2):
                    at = PACK_AT + k * P // 2
                    last = pe.transpose(ps[:, 7, at:at + P // 2].bitcast(BF16),
                                        pack[:, r, 4 * k:4 * k + 4, :].rearrange("p t n -> p (t n)"), ident_b[:, :])
                last.then_inc(s_packp, 1)

            def plane(i, r, g, q):
                w = q % 2
                if q == 0:
                    pe.wait_ge(s_packt, g + 1)
                pe.wait_ge(s_plfree[w], g * 2 + q // 2)
                for t in (2 * q, 2 * q + 1):
                    moving = pack_t[:, r, t // 4, :]
                    to = ps[:, 2 * w + t % 2, :].rearrange("p (h n) -> p h n", h=H)
                    pe.matmul(to, l_mask[:, t % 4, :], moving.rearrange("p (o n) -> p o n", o=1).to_broadcast([P, H, P]),
                              start=True, stop=False, skip_group_check=True)
                    for h in range(H):
                        last = pe.matmul(to[:, h, :], l_hr[:, t % 4, h, :], moving, start=False, stop=(h == H - 1),
                                         skip_group_check=True)
                last.then_inc(s_plane[w], 1)

            def turn_onehots(i, r, g, k):
                pe.wait_ge(s_onehot, g * 2 + k + 1)
                pe.wait_ge(s_oht, g * 2 + k)
                for t in range(4):
                    last = pe.transpose(ps[:, 6, t * P:(t + 1) * P], onehot[:, r, 4 * k + t, :], ident[:, :])
                last.then_inc(s_ohp, 1)

            def look_up(i, r, g):
                pe.wait_ge(s_oht, g * 2 + 2)
                pe.wait_ge(s_split, g + 1)
                pe.wait_ge(s_arg, g)
                for t in range(G):
                    last = pe.matmul(ps[:, 7, t * 6 * H:(t + 1) * 6 * H], onehot_t[:, r, t, :],
                                     look_split[:, r, t // 2, :, :].rearrange("p v s -> p (v s)"), start=True, stop=True,
                                     skip_group_check=True)
                last.then_inc(s_look, 1)

            def sum_pair(i, r, g, q):
                w = q % 2
                pe.wait_ge(s_msg, g * (G // 2) + q + 1)
                pe.wait_ge(s_add[w], g * 2 + q // 2)
                for t in (2 * q, 2 * q + 1):
                    last = pe.matmul(ps[:, 4 + w, 0:HW], onehot[:, r, t, :], rows[:, r, t, 0:HW], start=(t % 2 == 0), stop=(t % 2 == 1))
                last.then_inc(s_sum[w], 1)

            for r in range(AHEAD + 1):
                turn_pack(0, r, r)
            for r in range(AHEAD):
                for k in range(2):
                    turn_onehots(0, r, r, k)
            for r in range(AHEAD):
                for q in range(4):
                    plane(0, r, r, q)
            look_up(0, 0, 0)
            with pe.Fori(0, GROUPS // R) as i:
                for r in range(R):
                    now, near, far = after(i, r, 0), after(i, r, 1), after(i, r, AHEAD)
                    plane(*far, 0)
                    plane(*far, 1)
                    look_up(*near)
                    turn_onehots(*far, 0)
                    sum_pair(*now, 0)
                    plane(*far, 2)
                    sum_pair(*now, 1)
                    turn_onehots(*far, 1)
                    plane(*far, 3)
                    sum_pair(*now, 2)
                    turn_pack(*after(i, r, AHEAD + 1))
                    sum_pair(*now, 3)
            pe.wait_ge(s_fill, 6)
            def onto_mean(lhs, b, **flags):
                return pe.matmul(ps[0:1, 0, 0:D], lhs, x_sb[:, ds(b, 1), :].rearrange("p o d -> p (o d)"), skip_group_check=True, **flags)

            onto_mean(ones[:, 0:1], XB - 1, start=True, stop=False)
            with pe.Fori(0, BINS // (2 * BB)) as i:
                for u in range(2):
                    pe.wait_ge(s_u, i * 2 + u + 1)
                    for k in range(BB):
                        last = onto_mean(rstd_now[:, u, k:k + 1], (i * 2 + u) * BB + k, start=False, stop=False)
                    last.then_inc(s_umm[u], 1)
            pe.wait_ge(s_u, BINS // BB + 1)
            onto_mean(ones[:, 0:1], XB - 1, start=False, stop=True)
            pe.matmul(ps[0:1, 1, 0:1], nmr_sum[:, :], ones[:, 0:1], start=True, stop=True).then_inc(s_umm[0], 1)
            pe.wait_ge(s_mean, 1)
            for k in range(KD):
                last = pe.matmul(ps[:, 2, k:k + 1], mean_row[0:1, k * P:(k + 1) * P], ones[0:1, 0:1], start=True, stop=True)
            last.then_inc(s_meanp, 1)
            pe.wait_ge(s_meanc, 1)
            pe.wait_ge(s_small, 16 * LD_SMALL)
            for k in range(KD):
                last = pe.matmul(ps[0:1, 3, 0:NX], mean_col[:, k:k + 1], wr_sb[:, k, :], start=(k == 0), stop=(k == KD - 1))
            last.then_inc(s_logit, 1)
            pe.wait_ge(s_choice, 1)
            pe.matmul(ps[:, 4, 0:2], ones[0:1, :], small[0:1, 12:14], start=True, stop=True).then_inc(s_wb, 1)
            def transposes(c, u, n):
                pe.wait_ge(s_ub, c * CB + n)
                pe.wait_ge(s_ut, c * KD)
                for b in range(n):
                    for k in range(KD):
                        last = pe.transpose(ps[:, k, b * P:(b + 1) * P], u_rows[:, u, b, k * P:(k + 1) * P], ident[:, :])
                last.then_inc(s_utp, 1)

            def first_product(c, n):
                pe.wait_ge(s_ut, (c + 1) * KD)
                for f in range(8):
                    pe.wait_ge(s_act, c * 8 + (f - 1 if f else 0)) if f else None
                    for k in range(KD):
                        last = pe.matmul(ps[:, 2 + f % 2, 0:n * P], w1_sb[:, f // 4, k, f % 4 * P:(f % 4 + 1) * P],
                                         u_t[:, k, 0:n * P], start=(k == 0), stop=(k == KD - 1))
                    last.then_inc(s_m1, 1)

            def second_product(c, u, n):
                pe.wait_ge(s_act, (c + 1) * 8)
                pe.wait_ge(s_y, c)
                for b in range(n):
                    for f in range(8):
                        last = pe.matmul(ps[:, 4 + b, 0:D], act_t[:, u, f, b * P:(b + 1) * P], w2_sb[:, f // 4, f % 4, :],
                                         start=(f == 0), stop=(f == 7))
                    last.then_inc(s_m2, 1)

            transposes(0, 0, CB)
            pe.wait_ge(s_expw, 1)
            with pe.Fori(0, FULL // 2) as i:
                for u in range(2):
                    c = i * 2 + u
                    first_product(c, CB)
                    transposes(c + 1, 1 - u, CB)
                    second_product(c, u, CB)
            first_product(FULL, 1)
            second_product(FULL, 0, 1)

        @block.vector
        def _(dve):
            own = Count(s_dve)

            def link(instruction):
                own.add(instruction)
                dve.wait_ge(s_dve, own.value)

            dve.memset(src_i, (1 << 13) - 1).then_inc(s_fill, 1)
            dve.memset(dst_i, 0).then_inc(s_fill, 1)
            dve.memset(x_sb[:, NB - 1:XB, :], 0.0).then_inc(s_fill, 1)
            dve.memset(count, 0.0).then_inc(s_fill, 1)
            dve.memset(zeros16[:, :], 0.0).then_inc(s_fill, 1)
            dve.memset(slot_d[:, :], 0).then_inc(s_zero, 1)
            dve.wait_ge(s_fill, 5)
            dve.wait_ge(s_edges, 16 * LD_EDGES)
            dve.wait_ge(s_const, N_CONST)
            link(dve.tensor_scalar(work_i, src_i, 7, None, ALU.logical_shift_right))
            link(dve.tensor_copy(bin_16, work_i))
            link(dve.tensor_scalar(work_i, dst_i, SHIFT, 8, ALU.logical_shift_right, ALU.logical_shift_left))
            link(dve.tensor_scalar(src_i, src_i, P - 1, None, ALU.bitwise_and))
            link(dve.scalar_tensor_tensor(out=code_a, in0=src_i, scalar=1.0, in1=work_i, op0=ALU.add, op1=ALU.add))
            link(dve.scalar_tensor_tensor(out=code_c, in0=dst_i, scalar=256.0, in1=src_i, op0=ALU.mult, op1=ALU.add))
            link(dve.tensor_scalar(code_c, code_c, 1.0, None, ALU.add))
            link(dve.tensor_scalar(dst_i, dst_i, LOW, None, ALU.bitwise_and))
            link(dve.tensor_copy(code_b, dst_i))
            U = BINS // 5
            with dve.Fori(0, 5) as i:
                for k in range(U):
                    b = i * U + k
                    dve.wait_ge(s_cnt, b)
                    dve.tensor_scalar(rank[:, 0, :], bin_16, iota_b[:, ds(b, 1)], 0.0, ALU.is_equal, ALU.add,
                                      accum_out=count[:, ds(b, 1)]).then_inc(s_cnt, 1)
            dve.wait_ge(s_base, 1)
            link(dve.tensor_scalar(bin_i, ps[:, 5, 0:BINS], float(2 * P - 1), None, ALU.add))
            link(dve.tensor_scalar(bin_i, bin_i, 8, None, ALU.logical_shift_right))
            link(dve.tensor_copy(total, bin_i))
            link(dve.tensor_tensor_scan(ends, total, total, 0.0, ALU.add, ALU.max))
            link(dve.tensor_tensor(total, ends, total, ALU.subtract))
            link(dve.scalar_tensor_tensor(out=base, in0=total, scalar=float(2 * P), in1=ps[:, 4, 0:BINS], op0=ALU.mult, op1=ALU.add))
            link(dve.tensor_tensor(bin_cmp, iota_pair[:, :].rearrange("p (q o) -> p q o", o=1).to_broadcast([P, G // 2, NB]),
                                   ends[:, 0:NB].rearrange("p (o b) -> p o b", o=1).to_broadcast([P, G // 2, NB]), ALU.is_ge))
            link(dve.tensor_reduce(bin_of, bin_cmp, X, ALU.add))
            dve.tensor_copy(bin_of_i, bin_of).then_inc(s_bins, 1)
            own.add(dve.memset(mv[:, :, :], 0.0))
            dve.wait_ge(s_x, 16 * LD_X)

            def moments(i):
                dve.sem_inc(s_go, 1)
                for u in range(BB):
                    own.add(dve.bn_stats(stats[:, u, :], row_of(i * BB + u)))
                dve.wait_ge(s_dve, own.value)
                dve.sem_inc(s_go, 1)
                for u in range(BB):
                    own.add(dve.bn_aggr(mv_one[:, u, :], stats[:, u, :]))
                dve.wait_ge(s_dve, own.value)
                link(dve.tensor_scalar(mv[:, ds(i * BB, BB), :], mv_one[:, :, :], 0.0, None, ALU.add))

            def row_of(b):
                return x_sb[:, ds(b, 1), :].rearrange("p o d -> p (o d)")

            start = own.value
            with dve.Fori(0, BINS // BB) as i:
                own.value = i * (2 * BB + 1) + start
                moments(i)
            own.value = start + BINS // BB * (2 * BB + 1)
            ve = tmp_a[:, :, 0]
            sq = tmp_a[:, :, 1]

            def inverse_std(n_std, s_out):
                link(dve.tensor_scalar(ve, mv[:, :, 1], EPS, None, ALU.add))
                dve.tensor_copy(rstd[:, :], ve).then_inc(s_out, 1)
                dve.wait_ge(s_std, n_std)
                link(dve.reciprocal(nmr[:, :], rstd[:, :]))
                link(dve.tensor_tensor(sq, nmr[:, :], nmr[:, :], ALU.mult))
                link(dve.tensor_tensor(sq, sq, ve, ALU.mult))
                link(dve.tensor_scalar(sq, sq, -0.5, 1.5, ALU.mult, ALU.add))
                link(dve.tensor_tensor(rstd[:, :], nmr[:, :], sq, ALU.mult))
                link(dve.scalar_tensor_tensor(out=nmr[:, :], in0=mv[:, :, 0], scalar=-1.0, in1=rstd[:, :], op0=ALU.mult, op1=ALU.mult))

            inverse_std(1, s_var)
            dve.sem_inc(s_norm, 1)
            dve.wait_ge(s_w, 16 * LD_W)
            prod = tmp_b[:, 0:2 * P // (2 * H), :].rearrange("p a b -> p (a b)").rearrange("p (h f) -> p h f", h=H)
            for k in range(KD):
                w_k = wx[:, k, 0:HW].rearrange("p (h f) -> p h f", h=H)
                for a, to in ((ar_bc, w_k[:, :, FH]), (al_bc, wx[:, k, HW:HW + H])):
                    link(dve.tensor_tensor(prod, w_k[:, :, 0:FH], a[:, :].rearrange("p (h f) -> p h f", h=H), ALU.mult))
                    link(dve.tensor_reduce(to, prod, X, ALU.add))
            dve.sem_inc(s_norm, 1)
            link(dve.memset(pos, 0.0))
            link(dve.tensor_scalar(mask[:, 0, :], bin_16, iota_b[:, 0:1], None, ALU.is_equal))
            start = own.value
            with dve.Fori(0, 5) as i:
                own.value = i * (3 * U) + start
                for k in range(U):
                    b = i * U + k
                    w = k % 2
                    link(dve.tensor_tensor_scan(rank[:, w, :], mask[:, w, :], mask[:, w, :], base[:, ds(b, 1)], ALU.add, ALU.max))
                    own.add(dve.tensor_scalar(mask[:, 1 - w, :], bin_16, iota_b[:, ds(b + 1, 1)], None, ALU.is_equal))
                    link(dve.copy_predicated(pos, mask[:, w, :], rank[:, w, :]))
            own.value = start + 3 * U * 5
            link(dve.tensor_scalar(dst_i, pos, float(P - 1), None, ALU.add))
            link(dve.tensor_scalar(work_i, dst_i, 7, None, ALU.logical_shift_right))
            link(dve.tensor_copy(tile_of, work_i))
            link(dve.tensor_scalar(work_i, dst_i, P - 1, None, ALU.bitwise_and))
            link(dve.tensor_copy(place_of, work_i))
            link(dve.scalar_tensor_tensor(out=linear, in0=place_of, scalar=float(TILES), in1=tile_of, op0=ALU.mult, op1=ALU.add))
            dve.sem_inc(s_linear, 1)
            with dve.Fori(0, (ECP - EC_POOL) // UT) as i:
                for t in range(UT):
                    q = t % ONEHOTS
                    j = i * UT + t + EC_POOL
                    dve.wait_ge(s_mm[q], i * (UT // ONEHOTS) + t // ONEHOTS)
                    dve.tensor_scalar(oh_a[:, q, :], iota_p16[:, :], place_of[:, ds(j, 1)], code_a[:, ds(j, 1)],
                                      ALU.is_equal, ALU.mult).then_inc(s_oh, 1)
                    dve.tensor_scalar(oh_b[:, q, :], iota_p16[:, :], place_of[:, ds(j, 1)], code_b[:, ds(j, 1)],
                                      ALU.is_equal, ALU.mult).then_inc(s_oh, 1)
                    dve.tensor_scalar(oh_tile[:, q, :], iota_t16[:, :], tile_of[:, ds(j, 1)], None, ALU.is_equal).then_inc(s_oh, 1)
            dve.wait_ge(s_hcopy, 3 * BINS)
            rest_a, rest_b = tmp_a[:, 0:BINS, 0:H], tmp_a[:, 0:BINS, H:2 * H]
            link(dve.tensor_copy(hr_split[:, :, :, 0], hr[:, :, :]))
            link(dve.tensor_tensor(rest_a, hr[:, :, :], hr_split[:, :, :, 0], ALU.subtract))
            link(dve.tensor_copy(hr_split[:, :, :, 1], rest_a))
            link(dve.tensor_tensor(rest_b, rest_a, hr_split[:, :, :, 1], ALU.subtract))
            dve.tensor_copy(hr_split[:, :, :, 2], rest_b).then_inc(s_hr3, 1)
            own.add(dve.memset(slot_s[:, TILES:], 0.0))
            link(dve.memset(slot_r[:, TILES:, :], 0.0))
            dve.wait_ge(s_slots, 1)

            def halves(v):
                return v.rearrange("p (k n) -> p k n", k=2)

            own.add(dve.tensor_copy(halves(slot_a), ps[:, 0:2, 0:HALF]))
            link(dve.tensor_copy(halves(slot_b), ps[:, 2:4, 0:HALF]))
            link(dve.tensor_scalar(slot_d[:, 0:TILES], slot_a, 8, SHIFT, ALU.logical_shift_right, ALU.logical_shift_left))
            link(dve.tensor_tensor(slot_d[:, 0:TILES], slot_d[:, 0:TILES], slot_b, ALU.bitwise_or))
            dve.wait_ge(s_slotld, 16)
            own.add(dve.tensor_tensor(slot_a, slot_a, slot_c, ALU.bitwise_or))
            link(dve.tensor_scalar(slot_b, slot_c, 8, None, ALU.logical_shift_right))
            link(dve.tensor_tensor(slot_d[:, 0:TILES], slot_d[:, 0:TILES], slot_b, ALU.bitwise_or))
            dve.sem_inc(s_target, 1)
            link(dve.tensor_scalar(slot_a, slot_a, 255, None, ALU.bitwise_and))
            link(dve.tensor_copy(slot_s[:, 0:TILES], slot_a))
            link(dve.tensor_tensor(slot_t, slot_s[:, 0:TILES], slot_s[:, 0:TILES], ALU.mult))
            link(dve.tensor_copy(slot_a, slot_t))
            link(dve.tensor_scalar(slot_b, slot_a, P - 1, None, ALU.bitwise_and))
            own.add(dve.memset(slot_r[:, :, 0:2], 1.0))
            own.add(dve.tensor_copy(slot_r[:, 0:TILES, 2], slot_s[:, 0:TILES]))
            own.add(dve.tensor_copy(slot_r[:, 0:TILES, 4], slot_b))
            link(dve.tensor_tensor(slot_r[:, 0:TILES, 3], slot_t, slot_b, ALU.subtract))
            link(dve.tensor_scalar(slot_a[:, 0:1], part_i[:, :], 5, None, ALU.logical_shift_right))
            link(dve.tensor_copy(part_k[:, :], slot_a[:, 0:1]))
            link(dve.tensor_scalar(quarter[:, :], iota_b[:, 0:4], part_k[:, :], None, ALU.is_equal))
            link(dve.tensor_scalar(part_i[:, :], part_i[:, :], 31, None, ALU.bitwise_and))
            link(dve.tensor_copy(part_k[:, :], part_i[:, :]))
            for k, value in enumerate((-NEG, -NEG, 2 * NEG, -NEG, -NEG)):
                link(dve.tensor_scalar(coef[:, k:k + 1], part_k[:, :], float(k), value, ALU.is_equal, ALU.mult))
            link(dve.tensor_tensor(coef[:, 3:4], coef[:, 3:4], coef[:, 4:5], ALU.add))
            sq_n, lo_n, lo_i = slot_t[:, 0:P], slot_t[:, P:2 * P], slot_a[:, 0:P]
            link(dve.tensor_tensor(sq_n, iota_1[:, :], iota_1[:, :], ALU.mult))
            link(dve.tensor_copy(lo_i, sq_n))
            link(dve.tensor_scalar(lo_i, lo_i, P - 1, None, ALU.bitwise_and))
            link(dve.tensor_copy(lo_n, lo_i))
            link(dve.tensor_tensor(sq_n, sq_n, lo_n, ALU.subtract))
            link(dve.tensor_scalar(sq_n, sq_n, coef[:, 0:1], coef[:, 3:4], ALU.mult, ALU.add))
            link(dve.scalar_tensor_tensor(out=sq_n, in0=lo_n, scalar=coef[:, 1:2], in1=sq_n, op0=ALU.mult, op1=ALU.add))
            link(dve.scalar_tensor_tensor(out=sq_n, in0=iota_1[:, :], scalar=coef[:, 2:3], in1=sq_n, op0=ALU.mult, op1=ALU.add))
            for k in range(4):
                own.add(dve.tensor_scalar(l_mask[:, k, :], sq_n, quarter[:, k:k + 1], None, ALU.mult))
            for h in range(H):
                link(dve.tensor_scalar(coef[:, 5:6], part_k[:, :], float(5 + 3 * h), None, ALU.is_ge))
                link(dve.tensor_scalar(coef[:, 6:7], part_k[:, :], float(7 + 3 * h), None, ALU.is_le))
                link(dve.tensor_tensor(coef[:, 7:8], coef[:, 5:6], coef[:, 6:7], ALU.mult))
                for k in range(4):
                    own.add(dve.tensor_scalar(l_hr[:, k, h, :], ones[:, :], coef[:, 7:8], quarter[:, k:k + 1], ALU.mult, ALU.mult))
                dve.wait_ge(s_dve, own.value)
            link(dve.tensor_copy(ident_b[:, :], ident[:, :]))
            dve.wait_ge(s_binall, 16)
            own.add(dve.memset(begins, -1e38))
            own.add(dve.memset(new_bin[:, 0:1], 0.0))
            link(dve.tensor_tensor(new_bin[:, 1:], bins_all[:, 1:], bins_all[:, 0:GF * G // 2 - 1], ALU.not_equal))
            for h in range(H):
                own.add(dve.tensor_scalar(begins[:, :, h, 1:5], new_bin.rearrange("p (g q) -> p g q", q=G // 2), -1e30, None, ALU.mult))
            dve.wait_ge(s_dve, own.value)
            own.add(dve.memset(largest[:, :, :, :], -1e30))
            link(dve.memset(pack, 0.0))
            dve.sem_inc(s_table, 1)

            dve.wait_ge(s_binld, 16)

            def largest_of(i, r, g, q):
                w = q % 2
                dve.wait_ge(s_plane[w], g * 2 + q // 2 + 1)
                dve.tensor_reduce(largest[:, r, :, q + 1], ps[:, 2 * w:2 * w + 2, :].rearrange("p t (h n) -> p h t n", h=H),
                                  XY, ALU.max).then_inc(s_plfree[w], 1)

            def maxima(i, r, g):
                for w in range(2):
                    dve.wait_ge(s_plfree[w], g * 2 + 2)
                first = begins[:, ds(g, 1), :, :].rearrange("p o h q -> p (o h q)")
                link(dve.tensor_tensor_scan(running[:, r, :, :].rearrange("p h q -> p (h q)"), first,
                                            largest[:, r, :, :].rearrange("p h q -> p (h q)"), -1e30, ALU.add, ALU.max))
                dve.wait_ge(s_hl, g * 4 + 4)
                own.add(dve.tensor_scalar(largest[:, (r + 1) % R, :, 0], running[:, r, :, 4], 0.0, None, ALU.add))
                own.add(dve.tensor_tensor(now_m[:, :, :], running[:, r, :, 1:5].rearrange("p h q -> p q h"), look[:, r, :, 0:H], ALU.add))
                link(dve.tensor_tensor(so_far[:, :, :], running[:, r, :, 0:4],
                                       begins[:, ds(g, 1), :, 1:5].rearrange("p o h q -> p (o h) q"), ALU.add))
                link(dve.tensor_tensor(so_far_m[:, :, :], so_far[:, :, :].rearrange("p h q -> p q h"), look[:, r, :, 0:H], ALU.add))
                own.add(dve.scalar_tensor_tensor(out=look[:, r, :, H:2 * H], in0=now_m[:, :, :], scalar=SLOPE, in1=now_m[:, :, :],
                                                 op0=ALU.mult, op1=ALU.max))
                link(dve.scalar_tensor_tensor(out=so_far_m[:, :, :], in0=so_far_m[:, :, :], scalar=SLOPE, in1=so_far_m[:, :, :],
                                              op0=ALU.mult, op1=ALU.max))
                dve.tensor_tensor(scale[:, r, :, :], so_far_m[:, :, :], look[:, r, :, H:2 * H], ALU.subtract).then_inc(s_node, 1)
                dve.wait_ge(s_node, g + 1)

            STEPS = 7 + 3

            def found(i, r, g):
                dve.wait_ge(s_look, g + 1)
                dve.tensor_reduce(z[:, r, :, :], ps[:, 7, 0:G * 6 * H].rearrange("p (t v s) -> p t v s", t=G, s=3), X, ALU.add).then_inc(s_found, 1)

            def score_of(i, r, g):
                dve.wait_ge(s_found, g + 1)
                v = z[:, r, :, 0:H]
                own.add(dve.tensor_tensor(v, v, rows[:, r, :, 0:HW].rearrange("p t (h f) -> p t h f", h=H)[:, :, :, FH], ALU.add))

            def exponent(i, r, g):
                v = z[:, r, :, 0:H]
                dve.wait_ge(s_dve, own.value)
                link(dve.scalar_tensor_tensor(out=v, in0=v, scalar=SLOPE, in1=v, op0=ALU.mult, op1=ALU.max))
                link(dve.tensor_tensor(v, v, z[:, r, :, H:2 * H], ALU.subtract))
                dve.tensor_scalar(v, v, 0.0, None, ALU.min).then_inc(s_arg, 1)

            def weigh(i, r, g, q):
                v = rows[:, r, 2 * q:2 * q + 2, 0:HW].rearrange("p t (h f) -> p t h f", h=H)
                dve.tensor_tensor(v[:, :, :, 0:FH], v[:, :, :, 0:FH], v[:, :, :, FH:FW].to_broadcast([P, 2, H, FH]), ALU.mult).then_inc(s_msg, 1)

            def add_up(i, r, g, q, b):
                w = q % 2
                dve.wait_ge(s_sum[w], g * 2 + q // 2 + 1)
                dve.wait_ge(s_rescale, g * 4 + q + 1)
                where = acc[:, ds(b, 1), :].rearrange("p o n -> p (o n)")
                step = dve.tensor_tensor(where, where, ps[:, 4 + w, 0:HW], ALU.add)
                step.then_inc(s_add[w], 1)
                dve.wait_ge(s_add[w], g * 2 + q // 2 + 1)

            for r in range(AHEAD):
                for q in range(4):
                    largest_of(0, r, r, q)
                maxima(0, r, r)
            found(0, 0, 0)
            score_of(0, 0, 0)
            exponent(0, 0, 0)
            dve.wait_ge(s_clear, 1)
            start = own.value
            with dve.Fori(0, GROUPS // R) as i:
                for r in range(R):
                    now, near, far = after(i, r, 0), after(i, r, 1), after(i, r, AHEAD)
                    own.value = (i * R + r) * STEPS + start
                    largest_of(*far, 0)
                    dve.wait_ge(s_wgt, now[2] + 1)
                    weigh(*now, 0)
                    largest_of(*far, 1)
                    found(*near)
                    weigh(*now, 1)
                    score_of(*near)
                    bins = bins_of(DVE, now[2])
                    weigh(*now, 2)
                    exponent(*near)
                    add_up(*now, 0, bins[0])
                    largest_of(*far, 2)
                    weigh(*now, 3)
                    add_up(*now, 1, bins[1])
                    largest_of(*far, 3)
                    add_up(*now, 2, bins[2])
                    maxima(*far)
                    add_up(*now, 3, bins[3])
            own.value = start + STEPS * GROUPS
            for r in range(AHEAD + 1):
                dve.wait_ge(s_gat[r], (GROUPS // R + 1) * 16 * G)
            dve.wait_ge(s_wgt, GROUPS + 1)
            dve.memset(x_sb[:, NB - 1:XB, :], 0.0).then_inc(s_passed, 1)
            den = tmp_b[:, 0:BINS, 0:H]
            link(dve.tensor_scalar(den, acc_h[:, :, :, FH], 1e-16, None, ALU.max))
            link(dve.reciprocal(den, den))
            dve.sem_inc(s_den, 1)
            start = own.value
            def add_and_moments(lo, hi, start):
                with dve.Fori(lo, hi) as i:
                    own.value = (i - lo) * (2 * BB + 2) + start
                    dve.wait_ge(s_divided, i + 1)
                    batch = x_sb[:, ds(i * BB, BB), :].rearrange("p b (h f) -> p b h f", h=H)
                    link(dve.tensor_tensor(batch, batch, acc_h[:, ds(i * BB, BB), :, 0:FH], ALU.add))
                    moments(i)
                own.value = start + (hi - lo) * (2 * BB + 2)

            dve.wait_ge(s_x2[0], 16)
            add_and_moments(0, 2, own.value)
            dve.wait_ge(s_x2[1], 2 * 16)
            add_and_moments(2, BINS // BB, own.value)
            inverse_std(2, s_x1)
            link(dve.memset(half_col[:, :], -0.5))
            dve.sem_inc(s_fill, 1)
            with dve.Fori(0, BINS // (2 * BB)) as i:
                for u in range(2):
                    dve.wait_ge(s_umm[u], i)
                    dve.tensor_scalar(rstd_now[:, u, :], rstd[:, ds((i * 2 + u) * BB, BB)], 0.0, None, ALU.add).then_inc(s_u, 1)
            dve.tensor_reduce(nmr_sum[:, :], nmr[:, 0:BINS], X, ALU.add).then_inc(s_u, 1)
            dve.wait_ge(s_umm[0], BINS // (2 * BB) + 1)
            link(dve.tensor_copy(small[0:1, 20:21], ps[0:1, 1, 0:1]))
            dve.tensor_scalar(mean_row[:, :], ps[0:1, 0, 0:D], small[0:1, 20:21], 1.0 / TOKENS, ALU.add, ALU.mult).then_inc(s_mean, 1)
            dve.wait_ge(s_meanp, 1)
            dve.tensor_copy(mean_col[:, :], ps[:, 2, 0:KD]).then_inc(s_meanc, 1)
            dve.wait_ge(s_logit, 1)
            dve.wait_ge(s_small, 16 * LD_SMALL)

            def row(k):
                return logit[0:1, k * NX:(k + 1) * NX]

            def one(k):
                return small[0:1, k:k + 1]

            link(dve.tensor_tensor(row(0), ps[0:1, 3, 0:NX], br_row[:, :], ALU.add))
            link(dve.tensor_reduce(one(0), row(0), X, ALU.max))
            dve.tensor_scalar(row(1), row(0), one(0), None, ALU.subtract).then_inc(s_rt, 1)
            dve.wait_ge(s_rte, 1)
            link(dve.tensor_reduce(one(1), row(1), X, ALU.add))
            link(dve.reciprocal(one(2), one(1)))
            link(dve.tensor_scalar(row(2), row(1), one(2), None, ALU.mult))
            link(dve.tensor_scalar(row(4), row(2), float(TOKENS), None, ALU.mult))
            link(dve.reciprocal(row(5), row(4)))
            link(dve.tensor_scalar(row(5), row(5), CAPACITY, 1.0, ALU.mult, ALU.min))
            link(dve.tensor_tensor(row(6), row(2), row(5), ALU.mult))
            link(dve.tensor_reduce(one(3), row(6), X, ALU.max))
            dve.tensor_scalar(row(3), row(6), one(3), None, ALU.subtract).then_inc(s_rt, 1)
            dve.wait_ge(s_rte, 2)
            link(dve.tensor_reduce(one(4), row(3), X, ALU.add))
            link(dve.reciprocal(one(5), one(4)))
            link(dve.tensor_scalar(row(7), row(3), one(5), None, ALU.mult))
            for k in range(2):
                link(dve.tensor_reduce(one(6 + k), row(7), X, ALU.max))
                link(dve.tensor_scalar(row(8), row(7), one(6 + k), float(-NX), ALU.is_equal, ALU.mult))
                link(dve.tensor_tensor(row(8), row(8), iota_b[0:1, 0:NX], ALU.add))
                link(dve.tensor_reduce(one(8 + k), row(8), X, ALU.min))
                link(dve.tensor_scalar(one(8 + k), one(8 + k), float(NX), None, ALU.add))
                link(dve.tensor_scalar(row(9), iota_b[0:1, 0:NX], one(8 + k), -4.0, ALU.is_equal, ALU.mult))
                link(dve.tensor_tensor(row(7), row(7), row(9), ALU.add))
            link(dve.tensor_copy(chosen[:, :], small[0:1, 8:10]))
            dve.tensor_tensor(one(10), one(7), one(6), ALU.subtract).then_inc(s_rt, 1)
            dve.wait_ge(s_rte, 3)
            link(dve.tensor_scalar(one(11), one(10), 1.0, None, ALU.add))
            link(dve.reciprocal(one(12), one(11)))
            link(dve.tensor_tensor(one(13), one(10), one(12), ALU.mult))
            dve.sem_inc(s_choice, 1)
            dve.wait_ge(s_wb, 1)
            link(dve.tensor_copy(top_w[:, :], ps[:, 4, 0:2]))
            dve.wait_ge(s_exp, 8 * 16)
            for k in range(2):
                v = w2_sb[:, k, :, :].rearrange("p k n -> p (k n)")
                link(dve.tensor_scalar(v, v, top_w[:, k:k + 1], None, ALU.mult))
                link(dve.tensor_scalar(b2_bc[:, k, :], b2_bc[:, k, :], top_w[:, k:k + 1], None, ALU.mult))
            link(dve.tensor_tensor(b2_bc[:, 0, :], b2_bc[:, 0, :], b2_bc[:, 1, :], ALU.add))
            dve.sem_inc(s_expw, 1)

            def rows_in(c, u, n):
                for b in range(n):
                    w = c * CB + b
                    dve.tensor_scalar(u_rows[:, u, b, :], row_of(w), rstd[:, ds(w, 1)], nmr[:, ds(w, 1)], ALU.mult, ALU.add).then_inc(s_ub, 1)

            def sums(c, u, n):
                for b in range(n):
                    v = y[:, u, b, :]
                    dve.wait_ge(s_m2, c * CB + b + 1)
                    link(dve.tensor_tensor(v, ps[:, 4 + b, 0:D], u_rows[:, u, b, :], ALU.add))
                    link(dve.tensor_tensor(v, v, b2_bc[:, 0, :], ALU.add))
                    link(dve.bn_stats(stats[:, b, :], v))
                    dve.sem_inc(s_go, 1)
                    link(dve.bn_aggr(mv2[:, u, b, :], stats[:, b, :]))
                dve.tensor_scalar(ve2[:, u, 0:n], mv2[:, u, 0:n, 1], EPS, None, ALU.add).then_inc(s_y, 1)

            def finish(c, u, n):
                dve.wait_ge(s_pow, c + 1)
                link(dve.tensor_tensor(t2[:, u, 0:n], r2[:, u, 0:n], r2[:, u, 0:n], ALU.mult))
                link(dve.tensor_tensor(t2[:, u, 0:n], t2[:, u, 0:n], ve2[:, u, 0:n], ALU.mult))
                link(dve.tensor_scalar(t2[:, u, 0:n], t2[:, u, 0:n], -0.5, 1.5, ALU.mult, ALU.add))
                link(dve.tensor_tensor(r2[:, u, 0:n], r2[:, u, 0:n], t2[:, u, 0:n], ALU.mult))
                for b in range(n):
                    v = y[:, u, b, :]
                    link(dve.tensor_scalar(v, v, mv2[:, u, b, 0:1], r2[:, u, b:b + 1], ALU.subtract, ALU.mult))
                    link(dve.tensor_tensor(v, v, gamma_bc[:, :], ALU.mult))
                    link(dve.tensor_tensor(v, v, beta_bc[:, :], ALU.add))
                    dve.tensor_tensor(v, v, row_of(c * CB + b), ALU.add).then_inc(s_out, 1)

            rows_in(0, 0, CB)
            start = own.value
            per_chunk = 4 * CB + 4 + 3 * CB
            with dve.Fori(0, FULL // 2) as i:
                own.value = i * (2 * per_chunk) + start
                for u in range(2):
                    c = i * 2 + u
                    rows_in(c + 1, 1 - u, CB)
                    dve.wait_ge(s_st[u], i * 16)
                    sums(c, u, CB)
                    finish(c, u, CB)
            own.value = start + FULL * per_chunk
            dve.wait_ge(s_st[0], FULL // 2 * 16)
            sums(FULL, 0, 1)
            finish(FULL, 0, 1)


_INS = ['x', 'src', 'dst', 'L0_gnn_W', 'L0_gnn_a_l', 'L0_gnn_a_r', 'L0_ffn_Wr', 'L0_ffn_br', 'L0_ffn_W1', 'L0_ffn_b1',
        'L0_ffn_W2', 'L0_ffn_b2', 'L0_ffn_gamma', 'L0_ffn_beta']


def kernel(**inputs):
    import numpy as _np
    import concourse.bacc as _bacc
    from concourse import mybir as _mybir
    from concourse.bass_utils import run_bass_kernel_spmd as _run

    nc = _bacc.Bacc("TRN2", target_bir_lowering=False, num_devices=1)
    arrays, args = {}, []
    for name in _INS:
        a = _np.ascontiguousarray(inputs[name])
        arrays[f"in_{name}_dram"] = a
        args.append(nc.dram_tensor(f"in_{name}_dram", a.shape, _mybir.dt.from_np(a.dtype), kind="ExternalInput").ap())
    shape = inputs["x"].shape
    args.append(nc.dram_tensor("out_0_dram", shape, _mybir.dt.float32, kind="ExternalOutput").ap())
    gat_moe_block(nc, *args)
    r = _run(nc, [arrays], core_ids=[0])
    return r.results[0]["out_0_dram"]
```
